# Optimizing a Trainium2 kernel written in Bass

```python
import numpy as np
import jax
import jax.numpy as jnp

def _softmax(x, axis=-1):
    return jax.nn.softmax(x, axis=axis)

def _gelu(x):
    return jax.nn.gelu(x, approximate=True)

def _silu(x):
    return jax.nn.silu(x)

def _sigmoid(x):
    return jax.nn.sigmoid(x)

def _layernorm(x, axis=-1, eps=1e-05):
    m = jnp.mean(x, axis=axis, keepdims=True)
    v = jnp.var(x, axis=axis, keepdims=True)
    return (x - m) / jnp.sqrt(v + eps)

def _scatter_add(tgt, idx, src, axis=0):
    return tgt.at[idx].add(src)

def _segment_sum(src, seg, n):
    return jax.ops.segment_sum(src, seg, n)
kernel_name = 'mk_prb_d1_jaxref_r8_1b6516'

def setup_inputs(seed: int=0):
    np.random.seed(seed)
    _w = jnp.asarray

    def _L0_attn_setup():
        import jax, jax.numpy as jnp
        import numpy as np
        D_MODEL = 256
        D_STATE = 128
        D_CONV = 4
        NHEADS = 64
        NGROUPS = 1
        HEAD_DIM = 64
        CHUNK = 128
        EPS = 1e-05
        D_INNER = NHEADS * HEAD_DIM
        CONV_DIM = D_INNER + 2 * NGROUPS * D_STATE
        D_IN_PROJ = 2 * D_INNER + 2 * NGROUPS * D_STATE + NHEADS

        def _silu(x):
            return x * jax.nn.sigmoid(x)

        def _causal_conv1d(x, w, b):
            K = w.shape[1]
            S = x.shape[1]
            xp = jnp.pad(x, ((0, 0), (K - 1, 0), (0, 0)))
            y = sum((xp[:, k:k + S, :] * w[None, None, :, k].swapaxes(-1, -1) for k in range(0)))
            y = jnp.zeros_like(x)
            for k in range(K):
                y = y + xp[:, k:k + S, :] * w[:, k][None, None, :]
            return _silu(y + b)

        def _ssd(x, dt, A, Bm, Cm, chunk):
            b, s, h, p = x.shape
            g, n = (Bm.shape[2], Bm.shape[3])
            hh = h // g
            c = s // chunk
            x = x.reshape(b, c, chunk, g, hh, p)
            dt = dt.reshape(b, c, chunk, g, hh)
            Bm = Bm.reshape(b, c, chunk, g, n)
            Cm = Cm.reshape(b, c, chunk, g, n)
            dA = dt * A.reshape(g, hh)
            dA_cs = jnp.cumsum(dA, axis=2)
            dtx = dt[..., None] * x
            diff = dA_cs[:, :, :, None] - dA_cs[:, :, None, :]
            mask = jnp.tril(jnp.ones((chunk, chunk), bool))
            L = jnp.exp(jnp.where(mask[None, None, :, :, None, None], diff, -jnp.inf))
            Y = jnp.einsum('bcign,bcjgn,bcijgh,bcjghp->bcighp', Cm, Bm, L, dtx)
            decay = jnp.exp(dA_cs[:, :, -1:] - dA_cs)
            states = jnp.einsum('bcjgn,bcjgh,bcjghp->bcghpn', Bm, decay, dtx)
            chunk_decay = jnp.exp(dA_cs[:, :, -1])

            def step(prev, inp):
                cd, st = inp
                return (cd[..., None, None] * prev + st, prev)
            init = jnp.zeros_like(states[:, 0])
            _, prevs = jax.lax.scan(step, init, (jnp.moveaxis(chunk_decay, 1, 0), jnp.moveaxis(states, 1, 0)))
            prevs = jnp.moveaxis(prevs, 0, 1)
            Y = Y + jnp.einsum('bcign,bcghpn,bcigh->bcighp', Cm, prevs, jnp.exp(dA_cs))
            return Y.reshape(b, s, h, p)
        key = jax.random.key(seed)
        ks = jax.random.split(key, 9)
        B, S = (2, 512)
        return dict(hidden_states=jax.random.normal(ks[0], (B, S, D_MODEL), jnp.float32), W_in=jax.random.normal(ks[1], (D_MODEL, D_IN_PROJ), jnp.float32) * 0.02, conv_w=jax.random.normal(ks[2], (CONV_DIM, D_CONV), jnp.float32) * 0.2, conv_b=jax.random.normal(ks[3], (CONV_DIM,), jnp.float32) * 0.1, A=-jnp.exp(jax.random.uniform(ks[4], (NHEADS,), jnp.float32, 0.0, 2.0)), D=jax.random.normal(ks[5], (NHEADS,), jnp.float32), dt_bias=jax.random.normal(ks[6], (NHEADS,), jnp.float32), norm_w=jnp.ones((D_INNER,), jnp.float32), W_out=jax.random.normal(ks[7], (D_INNER, D_MODEL), jnp.float32) * 0.02)
    _L0_attn_in = _L0_attn_setup()

    def _L0_ffn_setup():
        import jax, jax.numpy as jnp
        import numpy as np
        N_BLOCKS = 6
        DIM = 256
        HIDDEN = 4 * DIM
        LN_EPS = 1e-05
        W_SCALE = 0.02

        def _block(x, w1, b1, w2, b2):
            h = jax.nn.gelu(jnp.einsum('bsd,hd->bsh', x, w1) + b1, approximate=False)
            return jnp.einsum('bsh,dh->bsd', h, w2) + b2 + x

        def _layernorm(x, g, b):
            mu = jnp.mean(x, axis=-1, keepdims=True)
            var = jnp.mean(jnp.square(x - mu), axis=-1, keepdims=True)
            return (x - mu) * jax.lax.rsqrt(var + LN_EPS) * g + b
        key = jax.random.key(seed)
        ks = jax.random.split(key, 4)
        x = jax.random.normal(ks[0], (4, 256, DIM), dtype=jnp.float32)
        W1 = jax.random.normal(ks[1], (N_BLOCKS, HIDDEN, DIM), dtype=jnp.float32) * W_SCALE
        B1 = jnp.zeros((N_BLOCKS, HIDDEN), dtype=jnp.float32)
        W2 = jax.random.normal(ks[2], (N_BLOCKS, DIM, HIDDEN), dtype=jnp.float32) * W_SCALE
        B2 = jnp.zeros((N_BLOCKS, DIM), dtype=jnp.float32)
        LN_G = jnp.ones((N_BLOCKS - 1, DIM), dtype=jnp.float32)
        LN_B = jnp.zeros((N_BLOCKS - 1, DIM), dtype=jnp.float32)
        return {'x': x, 'W1': W1, 'B1': B1, 'W2': W2, 'B2': B2, 'LN_G': LN_G, 'LN_B': LN_B}
    _L0_ffn_in = _L0_ffn_setup()
    _d = {'L0_attn_hidden_states': _L0_attn_in['hidden_states'], 'L0_attn_W_in': _L0_attn_in['W_in'], 'L0_attn_conv_w': _L0_attn_in['conv_w'], 'L0_attn_conv_b': _L0_attn_in['conv_b'], 'L0_attn_A': _L0_attn_in['A'], 'L0_attn_D': _L0_attn_in['D'], 'L0_attn_dt_bias': _L0_attn_in['dt_bias'], 'L0_attn_norm_w': _L0_attn_in['norm_w'], 'L0_attn_W_out': _L0_attn_in['W_out'], 'L0_ffn_W1': _L0_ffn_in['W1'], 'L0_ffn_B1': _L0_ffn_in['B1'], 'L0_ffn_W2': _L0_ffn_in['W2'], 'L0_ffn_B2': _L0_ffn_in['B2'], 'L0_ffn_LN_G': _L0_ffn_in['LN_G'], 'L0_ffn_LN_B': _L0_ffn_in['LN_B']}
    _x0 = _d['L0_attn_hidden_states']
    _d['L0_attn_hidden_states'] = jax.random.normal(jax.random.fold_in(jax.random.key(seed), 1), (8, 256, 256), dtype=_x0.dtype)
    del _x0
    return _d

def reference(L0_attn_hidden_states, L0_attn_W_in, L0_attn_conv_w, L0_attn_conv_b, L0_attn_A, L0_attn_D, L0_attn_dt_bias, L0_attn_norm_w, L0_attn_W_out, L0_ffn_W1, L0_ffn_B1, L0_ffn_W2, L0_ffn_B2, L0_ffn_LN_G, L0_ffn_LN_B):

    def _L0_attn_ref(hidden_states, W_in, conv_w, conv_b, A, D, dt_bias, norm_w, W_out):
        import jax, jax.numpy as jnp
        import numpy as np
        D_MODEL = 256
        D_STATE = 128
        D_CONV = 4
        NHEADS = 64
        NGROUPS = 1
        HEAD_DIM = 64
        CHUNK = 128
        EPS = 1e-05
        D_INNER = NHEADS * HEAD_DIM
        CONV_DIM = D_INNER + 2 * NGROUPS * D_STATE
        D_IN_PROJ = 2 * D_INNER + 2 * NGROUPS * D_STATE + NHEADS

        def _silu(x):
            return x * jax.nn.sigmoid(x)

        def _causal_conv1d(x, w, b):
            K = w.shape[1]
            S = x.shape[1]
            xp = jnp.pad(x, ((0, 0), (K - 1, 0), (0, 0)))
            y = sum((xp[:, k:k + S, :] * w[None, None, :, k].swapaxes(-1, -1) for k in range(0)))
            y = jnp.zeros_like(x)
            for k in range(K):
                y = y + xp[:, k:k + S, :] * w[:, k][None, None, :]
            return _silu(y + b)

        def _ssd(x, dt, A, Bm, Cm, chunk):
            b, s, h, p = x.shape
            g, n = (Bm.shape[2], Bm.shape[3])
            hh = h // g
            c = s // chunk
            x = x.reshape(b, c, chunk, g, hh, p)
            dt = dt.reshape(b, c, chunk, g, hh)
            Bm = Bm.reshape(b, c, chunk, g, n)
            Cm = Cm.reshape(b, c, chunk, g, n)
            dA = dt * A.reshape(g, hh)
            dA_cs = jnp.cumsum(dA, axis=2)
            dtx = dt[..., None] * x
            diff = dA_cs[:, :, :, None] - dA_cs[:, :, None, :]
            mask = jnp.tril(jnp.ones((chunk, chunk), bool))
            L = jnp.exp(jnp.where(mask[None, None, :, :, None, None], diff, -jnp.inf))
            Y = jnp.einsum('bcign,bcjgn,bcijgh,bcjghp->bcighp', Cm, Bm, L, dtx)
            decay = jnp.exp(dA_cs[:, :, -1:] - dA_cs)
            states = jnp.einsum('bcjgn,bcjgh,bcjghp->bcghpn', Bm, decay, dtx)
            chunk_decay = jnp.exp(dA_cs[:, :, -1])

            def step(prev, inp):
                cd, st = inp
                return (cd[..., None, None] * prev + st, prev)
            init = jnp.zeros_like(states[:, 0])
            _, prevs = jax.lax.scan(step, init, (jnp.moveaxis(chunk_decay, 1, 0), jnp.moveaxis(states, 1, 0)))
            prevs = jnp.moveaxis(prevs, 0, 1)
            Y = Y + jnp.einsum('bcign,bcghpn,bcigh->bcighp', Cm, prevs, jnp.exp(dA_cs))
            return Y.reshape(b, s, h, p)
        Bsz, S, _ = hidden_states.shape
        zxbcdt = hidden_states @ W_in
        z = zxbcdt[..., :D_INNER]
        xbc = zxbcdt[..., D_INNER:D_INNER + CONV_DIM]
        dt = zxbcdt[..., D_INNER + CONV_DIM:]
        xbc = _causal_conv1d(xbc, conv_w, conv_b)
        x = xbc[..., :D_INNER].reshape(Bsz, S, NHEADS, HEAD_DIM)
        Bm = xbc[..., D_INNER:D_INNER + NGROUPS * D_STATE].reshape(Bsz, S, NGROUPS, D_STATE)
        Cm = xbc[..., D_INNER + NGROUPS * D_STATE:].reshape(Bsz, S, NGROUPS, D_STATE)
        dt = jax.nn.softplus(dt + dt_bias)
        y = _ssd(x, dt, A, Bm, Cm, CHUNK)
        y = y + D[None, None, :, None] * x
        y = y.reshape(Bsz, S, D_INNER)
        yg = y * _silu(z)
        gsz = D_INNER // NGROUPS
        ygr = yg.reshape(Bsz, S, NGROUPS, gsz)
        rms = jax.lax.rsqrt(jnp.mean(ygr * ygr, axis=-1, keepdims=True) + EPS)
        yn = (ygr * rms).reshape(Bsz, S, D_INNER) * norm_w
        return yn @ W_out

    def _L0_ffn_ref(x, W1, B1, W2, B2, LN_G, LN_B):
        import jax, jax.numpy as jnp
        import numpy as np
        N_BLOCKS = 6
        DIM = 256
        HIDDEN = 4 * DIM
        LN_EPS = 1e-05
        W_SCALE = 0.02

        def _block(x, w1, b1, w2, b2):
            h = jax.nn.gelu(jnp.einsum('bsd,hd->bsh', x, w1) + b1, approximate=False)
            return jnp.einsum('bsh,dh->bsd', h, w2) + b2 + x

        def _layernorm(x, g, b):
            mu = jnp.mean(x, axis=-1, keepdims=True)
            var = jnp.mean(jnp.square(x - mu), axis=-1, keepdims=True)
            return (x - mu) * jax.lax.rsqrt(var + LN_EPS) * g + b
        for i in range(N_BLOCKS):
            x = _block(x, W1[i], B1[i], W2[i], B2[i])
            if i < N_BLOCKS - 1:
                x = _layernorm(x, LN_G[i], LN_B[i])
        return x
    x = L0_attn_hidden_states
    xn = _layernorm(x, axis=-1)
    x = x + _L0_attn_ref(xn, L0_attn_W_in, L0_attn_conv_w, L0_attn_conv_b, L0_attn_A, L0_attn_D, L0_attn_dt_bias, L0_attn_norm_w, L0_attn_W_out) + _L0_ffn_ref(xn, L0_ffn_W1, L0_ffn_B1, L0_ffn_W2, L0_ffn_B2, L0_ffn_LN_G, L0_ffn_LN_B)
    return x

_drawn_inputs = setup_inputs


def setup_inputs(seed=0):
    import zlib

    import numpy as np

    out = dict(_drawn_inputs(seed))
    spreads = {'L0_attn_norm_w': (1.0, 0.2),
     'L0_ffn_B1': (0.0, 0.1),
     'L0_ffn_B2': (0.0, 0.1),
     'L0_ffn_LN_G': (1.0, 0.2),
     'L0_ffn_LN_B': (0.0, 0.1)}
    factors = {}
    for name, (base, spread) in spreads.items():
        noise = np.random.default_rng([zlib.crc32(name.encode()), seed]).standard_normal(out[name].shape)
        drawn = base * np.exp(spread * noise) if base else spread * noise
        out[name] = jnp.asarray(drawn.astype(out[name].dtype))
    for name, factor in factors.items():
        out[name] = (out[name] * factor).astype(out[name].dtype)
    return out
```

```python
from contextlib import ExitStack

import concourse.bass as bass
from concourse import mybir

F32 = mybir.dt.float32
F32R = mybir.dt.float32r
ALU = mybir.AluOpType
ACT = mybir.ActivationFunctionType

P = 128
SEQ = 256
NSEQ = 8
TOK = NSEQ * SEQ
TILES = TOK // P
DM = 256
KD = DM // P
DI = 4096
NCT = DI // P
HD = 64
HPT = P // HD
NH = DI // HD
TAPS = 4
BLK = 512
NB = TOK // BLK
TPB = BLK // P
SPB = BLK // SEQ
LW = SEQ + P
HID = 1024
KH = HID // P
NL = 6
EPS = 1e-5
CAP = 80.0


def build(nc, hidden, w_bcdt, conv_bc, dt_par, w_xz, chan_par, w_out,
          w1, w2, b2, ln_g, ln_b, ln_cols, ident_in, mask_in, out):
    cs_dram = nc.dram_tensor("cs_rows", [NH, TOK], F32, kind="Internal").ap()
    xn_dram = nc.dram_tensor("xn_rows", [TOK, DM], F32, kind="Internal").ap()
    tiled = lambda ap: ap.rearrange("(t p) d -> p t d", p=P)

    with ExitStack() as ctx:
        def sb(name, shape, dt=F32, stack=ctx):
            return stack.enter_context(nc.sbuf_tensor(name, shape, dt))

        ident = sb("ident", [P, P])
        xhi = sb("xhi", [P, KD, TOK], F32R)
        xlo = sb("xlo", [P, KD, TOK], F32R)
        acc = sb("acc", [P, TILES, DM])

        with ExitStack() as mixer:
            gmat = sb("gmat", [P, NSEQ, LW], stack=mixer)
            tokpar = sb("tokpar", [P, TILES, 2 * NH], stack=mixer)
            normalise(nc, hidden, xn_dram, ident_in, ident, xhi, xlo, tiled)
            prepare(nc, w_bcdt, conv_bc, dt_par, mask_in, cs_dram,
                    ident, xhi, xlo, acc, gmat, tokpar)
            mix(nc, w_xz, chan_par, w_out, cs_dram, ident, xhi, xlo, acc, gmat, tokpar)
        mlp(nc, hidden, xn_dram, w1, w2, b2, ln_g, ln_b, ln_cols, ident, xhi, xlo, acc, out,
            tiled)


def normalise(nc, hidden, xn_dram, ident_in, ident, xhi, xlo, tiled):
    with ExitStack() as ctx:
        sb = lambda name, shape, dt=F32: ctx.enter_context(nc.sbuf_tensor("norm_" + name, shape, dt))
        sem = lambda name: ctx.enter_context(nc.semaphore("norm_" + name))
        hid = sb("hid", [P, TILES, DM])
        stats = sb("stats", [P, TILES, 6])
        mv = sb("mv", [P, TILES, 2])
        vare = sb("vare", [P, TILES])
        rstd = sb("rstd", [P, TILES])
        mhalf = sb("mhalf", [P, TPB])
        tp = [[ctx.enter_context(nc.psum_tensor(f"norm_tp{i}{k}", [P, BLK], F32)) for k in range(KD)]
              for i in range(2)]
        const_in = sem("const_in")
        hid_in = [sem(f"hid_in{b}") for b in range(NB)]
        mhalf_set = sem("mhalf_set")
        stats_done = sem("stats_done")
        mv_done = sem("mv_done")
        vare_done = sem("vare_done")
        rstd_done = sem("rstd_done")
        xn_done = sem("xn_done")
        xt_done = sem("xt_done")
        hi_done = sem("hi_done")
        lo_done = sem("lo_done")
        xn_out = sem("xn_out")
        block = ctx.enter_context(nc.Block())

        @block.sync
        def _(sp):
            for b in range(NB):
                sp.dma_start(hid[:, b * TPB:(b + 1) * TPB, :],
                             tiled(hidden)[:, b * TPB:(b + 1) * TPB, :]).then_inc(hid_in[b], 16)
                if b == 0:
                    sp.dma_start(ident[:], ident_in).then_inc(const_in, 16)
            for b in range(NB):
                sp.wait_ge(xn_done, TPB * (b + 1))
                sp.dma_start(tiled(xn_dram)[:, b * TPB:(b + 1) * TPB, :],
                             hid[:, b * TPB:(b + 1) * TPB, :]).then_inc(xn_out, 16)
            sp.wait_ge(xn_out, 16 * NB)

        @block.gpsimd
        def _(pool):
            pool.memset(mhalf[:], -0.5).then_inc(mhalf_set, 1)
            pool.wait_ge(mhalf_set, 1)
            for b in range(NB):
                pool.wait_ge(vare_done, b + 1)
                pool.tensor_tensor(rstd[:, b * TPB:(b + 1) * TPB], vare[:, b * TPB:(b + 1) * TPB],
                                   mhalf[:], ALU.pow).then_inc(rstd_done, 1)

        @block.vector
        def _(dve):
            def lo_part(b):
                for k in range(KD):
                    dve.wait_ge(hi_done, KD * b + k + 1)
                    dve.tensor_tensor(xlo[:, k, b * BLK:(b + 1) * BLK], tp[b % 2][k][:],
                                      xhi[:, k, b * BLK:(b + 1) * BLK].bitcast(F32),
                                      ALU.subtract).then_inc(lo_done, 1)

            def moments(b):
                dve.wait_ge(hid_in[b], 16)
                for t in range(b * TPB, (b + 1) * TPB):
                    dve.bn_stats(stats[:, t, :], hid[:, t, :]).then_inc(stats_done, 1)
                for t in range(b * TPB, (b + 1) * TPB):
                    dve.wait_ge(stats_done, t + 1)
                    dve.bn_aggr(mv[:, t, :], stats[:, t, :]).then_inc(mv_done, 1)
                dve.wait_ge(mv_done, TPB * (b + 1))
                dve.tensor_scalar(vare[:, b * TPB:(b + 1) * TPB], mv[:, b * TPB:(b + 1) * TPB, 1],
                                  EPS, None, ALU.add).then_inc(vare_done, 1)

            moments(0)
            for b in range(NB):
                if b + 1 < NB:
                    moments(b + 1)
                dve.wait_ge(rstd_done, b + 1)
                for t in range(b * TPB, (b + 1) * TPB):
                    dve.tensor_scalar(hid[:, t, :], hid[:, t, :], mv[:, t, 0:1], rstd[:, t:t + 1],
                                      ALU.subtract, ALU.mult).then_inc(xn_done, 1)
                if b >= 1:
                    lo_part(b - 1)
            lo_part(NB - 1)

        @block.tensor
        def _(pe):
            pe.wait_ge(const_in, 16)
            for b in range(NB):
                pe.wait_ge(xn_done, TPB * (b + 1))
                if b >= 2:
                    pe.wait_ge(lo_done, KD * (b - 1))
                for k in range(KD):
                    for t in range(TPB):
                        last = pe.transpose(tp[b % 2][k][:, t * P:(t + 1) * P],
                                            hid[:, b * TPB + t, k * P:(k + 1) * P], ident[:])
                    last.then_inc(xt_done, 1)

        @block.scalar
        def _(act):
            for b in range(NB):
                for k in range(KD):
                    act.wait_ge(xt_done, KD * b + k + 1)
                    act.copy(xhi[:, k, b * BLK:(b + 1) * BLK], tp[b % 2][k][:]).then_inc(hi_done, 1)


def prepare(nc, w_bcdt, conv_bc, dt_par, mask_in, cs_dram,
            ident, xhi, xlo, acc, gmat, tokpar):
    with ExitStack() as ctx:
        sb = lambda name, shape, dt=F32: ctx.enter_context(nc.sbuf_tensor("prep_" + name, shape, dt))
        sem = lambda name: ctx.enter_context(nc.semaphore("prep_" + name))
        mask = sb("mask", [P, LW])
        cbc = sb("cbc", [P, 2, TAPS + 1])
        par = sb("par", [P, 2])
        w_raw = sb("wbc_raw", [P, KD, 3 * P])
        w_hi = sb("wbc_hi", [P, KD, 3 * P], F32R)
        w_lo = sb("wbc_lo", [P, KD, 3 * P], F32R)
        bct = sb("bct", [P, 2, TOK])
        v = sb("v", [P, TOK])
        u = sb("u", [P, TOK])
        w = sb("w", [P, TOK])
        v_ln = sb("v_ln", [P, TOK])
        dtcs = sb("dtcs", [P, TOK])
        ones = sb("ones", [P, SEQ])
        bank = [ctx.enter_context(nc.psum_tensor(f"prep_prep{i}", [P, BLK], F32)) for i in range(8)]
        consts_in = sem("consts_in")
        wbc_in = sem("wbc_in")
        w_split = sem("w_split")
        ones_set = sem("ones_set")
        proj_done = sem("proj_done")
        v_done = sem("v_done")
        abs_done = sem("abs_done")
        u_done = sem("u_done")
        w_done = sem("w_done")
        ln_done = sem("ln_done")
        sp_step = sem("sp_step")
        dt_done = sem("dt_done")
        cs_done = sem("cs_done")
        cs_out = sem("cs_out")
        conv0_done = sem("conv0_done")
        tap_done = sem("tap_done")
        conv_done = sem("conv_done")
        bct_done = sem("bct_done")
        g_done = sem("g_done")
        g_masked = sem("g_masked")
        tr_done = sem("tr_done")
        tr_copied = sem("tr_copied")
        block = ctx.enter_context(nc.Block())

        @block.sync
        def _(sp):
            sp.dma_start(w_raw[:], w_bcdt).then_inc(wbc_in, 16)
            for dst, src in ((par, dt_par), (cbc, conv_bc), (mask, mask_in)):
                sp.dma_start(dst[:], src).then_inc(consts_in, 16)
            sp.wait_ge(cs_done, NSEQ)
            sp.dma_start(cs_dram, dtcs[HD:P, :]).then_inc(cs_out, 16)
            sp.wait_ge(cs_out, 16)

        @block.gpsimd
        def _(pool):
            pool.wait_ge(wbc_in, 16)
            pool.tensor_copy(w_hi[:], w_raw[:]).then_inc(w_split, 1)
            pool.wait_ge(w_split, 1)
            pool.tensor_tensor(w_lo[:], w_raw[:], w_hi[:].bitcast(F32), ALU.subtract).then_inc(w_split, 1)
            pool.memset(ones[:], 1.0).then_inc(ones_set, 1)
            pool.memset(acc[:], 0.0).then_inc(ones_set, 1)

        @block.tensor
        def _(pe):
            pe.wait_ge(w_split, 2)
            for n in range(3 * NB):
                m, b = n // NB, n % NB
                if n >= 8:
                    pe.wait_ge(abs_done, n - 7)
                    pe.wait_ge(v_done, n - 7)
                project(pe, bank[n % 8][:], w_hi[:, :, m * P:(m + 1) * P],
                        w_lo[:, :, m * P:(m + 1) * P], xhi, xlo, b).then_inc(proj_done, 1)
            for s in range(NSEQ):
                pe.wait_ge(bct_done, NB + s // SPB + 1)
                if s >= 4:
                    pe.wait_ge(g_masked, s - 3)
                g = bank[4 + s % 4]
                o = s * SEQ
                pe.matmul(g[:, 0:SEQ], bct[:, 0, o:o + P], bct[:, 1, o:o + SEQ],
                          start=True, stop=True)
                pe.matmul(g[:, SEQ:LW], bct[:, 0, o + P:o + SEQ], bct[:, 1, o + P:o + SEQ],
                          start=True, stop=True).then_inc(g_done, 1)
            pe.wait_ge(cs_done, NSEQ)
            pe.wait_ge(dt_done, NB)
            for b in range(NB):
                for t in range(TPB):
                    last = pe.transpose(bank[b][:, t * P:(t + 1) * P],
                                        dtcs[:, (b * TPB + t) * P:(b * TPB + t + 1) * P], ident[:])
                last.then_inc(tr_done, 1)

        @block.scalar
        def _(act):
            act.wait_ge(consts_in, 48)
            for b in range(NB):
                c = slice(b * BLK, (b + 1) * BLK)
                act.wait_ge(proj_done, b + 1)
                act.activation(u[:, c], bank[b][:], ACT.Abs, bias=par[:, 0:1]).then_inc(abs_done, 1)
                act.activation(v[:, c], bank[b][:], ACT.Identity, bias=par[:, 0:1]).then_inc(v_done, 1)
            for b in range(NB):
                c = slice(b * BLK, (b + 1) * BLK)
                act.wait_ge(abs_done, b + 1)
                act.activation(u[:, c], u[:, c], ACT.Exp, scale=-1.0).then_inc(u_done, 1)
            for n in range(2 * NB):
                m, b = n // NB, n % NB
                act.wait_ge(proj_done, NB + n + 1)
                act.activation(bct[:, m, b * BLK:(b + 1) * BLK], bank[(NB + n) % 8][:], ACT.Identity,
                               bias=cbc[:, m, TAPS:TAPS + 1],
                               scale=cbc[:, m, TAPS - 1:TAPS]).then_inc(conv0_done, 1)
            for b in range(NB):
                c = slice(b * BLK, (b + 1) * BLK)
                act.wait_ge(w_done, b + 1)
                act.activation(v_ln[:, c], w[:, c], ACT.Ln).then_inc(ln_done, 1)
            for n in range(2 * NB):
                m, b = n // NB, n % NB
                act.wait_ge(conv_done, n + 1)
                c = bct[:, m, b * BLK:(b + 1) * BLK]
                act.activation(c, c, ACT.Silu).then_inc(bct_done, 1)
            for b in range(NB):
                act.wait_ge(tr_done, b + 1)
                act.copy(tokpar[:, b * TPB:(b + 1) * TPB, :],
                         bank[b][:].rearrange("p (t h) -> p t h", t=TPB)).then_inc(tr_copied, 1)

        @block.vector
        def _(dve):
            for b in range(NB):
                c = slice(b * BLK, (b + 1) * BLK)
                dve.wait_ge(u_done, b + 1)
                dve.tensor_scalar(w[:, c], u[:, c], 1.0, None, ALU.add).then_inc(w_done, 1)
            n_tap = 0
            for n in range(2 * NB):
                m, b = n // NB, n % NB
                dve.wait_ge(conv0_done, n + 1)
                for k in range(1, TAPS):
                    ins = conv_tap(dve, bct[:, m, b * BLK:(b + 1) * BLK], bank[(NB + n) % 8][:],
                                   cbc[:, m, TAPS - 1 - k:TAPS - k], k)
                    if k < TAPS - 1:
                        ins.then_inc(tap_done, 1)
                        n_tap += 1
                        dve.wait_ge(tap_done, n_tap)
                    else:
                        ins.then_inc(conv_done, 1)
            n_sp = 0
            for b in range(NB):
                c = slice(b * BLK, (b + 1) * BLK)
                dve.wait_ge(ln_done, b + 1)
                dve.wait_ge(w_done, b + 1)
                dve.scalar_tensor_tensor(w[:, c], w[:, c], -1.0, u[:, c], ALU.add,
                                         ALU.subtract).then_inc(sp_step, 1)
                n_sp += 1
                dve.wait_ge(sp_step, n_sp)
                dve.tensor_tensor(w[:, c], v_ln[:, c], w[:, c], ALU.subtract).then_inc(sp_step, 1)
                n_sp += 1
                dve.wait_ge(sp_step, n_sp)
                dve.wait_ge(v_done, b + 1)
                dve.scalar_tensor_tensor(w[:, c], v[:, c], 0.0, w[:, c], ALU.max,
                                         ALU.add).then_inc(sp_step, 1)
                n_sp += 1
                dve.wait_ge(sp_step, n_sp)
                dve.tensor_copy(dtcs[0:HD, c], w[0:HD, c]).then_inc(dt_done, 1)
                dve.tensor_scalar(v[HD:P, c], w[HD:P, c], par[HD:P, 1:2], -1.0, ALU.mult,
                                  ALU.mult).then_inc(sp_step, 1)
                n_sp += 1
                dve.wait_ge(sp_step, n_sp)
                if b == 0:
                    dve.wait_ge(ones_set, 1)
                for s in range(b * SPB, (b + 1) * SPB):
                    q = slice(s * SEQ, (s + 1) * SEQ)
                    dve.tensor_tensor_scan(dtcs[HD:P, q], ones[HD:P, :], v[HD:P, q], 0.0,
                                           ALU.mult, ALU.add).then_inc(cs_done, 1)
            for s in range(NSEQ):
                dve.wait_ge(g_done, s + 1)
                dve.tensor_tensor(gmat[:, s, :], bank[4 + s % 4][:, 0:LW], mask[:],
                                  ALU.mult).then_inc(g_masked, 1)


def project(pe, dst, w_hi, w_lo, xhi, xlo, b):
    cols = slice(b * BLK, (b + 1) * BLK)
    passes = [(w, x, k) for k in range(KD) for w, x in ((w_hi, xhi), (w_hi, xlo), (w_lo, xhi))]
    for i, (w, x, k) in enumerate(passes):
        last = pe.matmul(dst, w[:, k, :], x[:, k, cols], start=(i == 0), stop=(i == len(passes) - 1))
    return last


def conv_tap(dve, dst, src, weight, k):
    d = dst.rearrange("p (s t) -> p s t", t=SEQ)
    s = src.rearrange("p (s t) -> p s t", t=SEQ)
    return dve.scalar_tensor_tensor(d[:, :, k:SEQ], s[:, :, 0:SEQ - k], weight, d[:, :, k:SEQ],
                                    ALU.mult, ALU.add)


def mix(nc, w_xz, chan_par, w_out, cs_dram, ident, xhi, xlo, acc, gmat, tokpar):
    with ExitStack() as ctx:
        sb = lambda name, shape, dt=F32: ctx.enter_context(nc.sbuf_tensor("mix_" + name, shape, dt))
        ps = lambda name: ctx.enter_context(nc.psum_tensor("mix_" + name, [P, BLK], F32))
        sem = lambda name: ctx.enter_context(nc.semaphore("mix_" + name))
        wraw = sb("wraw", [P, 2, 2 * KD * P])
        chan = sb("chan", [P, 2, TAPS + 2])
        stok = sb("stok", [P, 2, TILES, HPT])
        whi = sb("whi", [P, 2, 2 * KD, P], F32R)
        wlo = sb("wlo", [P, 2, 2 * KD, P], F32R)
        oraw = sb("oraw", [P, 2, DM + 1])
        ohi = sb("ohi", [P, 2, DM], F32R)
        olo = sb("olo", [P, 2, DM], F32R)
        srow = sb("srow", [P, 2, HPT, TOK // 2])
        xt = sb("xt", [P, 2, TOK])
        zt = sb("zt", [P, 2, TOK])
        dtx = sb("dtx", [P, 2, TPB, P])
        dec = sb("dec", [P, 2, SPB, HPT, LW])
        yg = sb("yg", [P, 2, BLK])
        sq = sb("sq", [P, BLK])
        sqacc = sb("sqacc", [P, TOK])
        ghi = sb("ghi", [P, 2, TOK], F32R)
        glo = sb("glo", [P, 2, TOK], F32R)
        onesq = sb("onesq", [P, 2])
        mhalf = sb("mhalf", [P, TILES])
        rms = sb("rms", [P, TILES])
        pa = [ps(f"pa{i}") for i in range(2)]
        pt = [ps(f"pt{i}") for i in range(2)]
        py = [ps(f"py{i}") for i in range(2)]
        po = [ps(f"po{i}") for i in range(2)]

        w_in = [sem(f"w_in{i}") for i in range(2)]
        chan_in = [sem(f"chan_in{i}") for i in range(2)]
        stok_done = sem("stok_done")
        w_hi_done = sem("w_hi_done")
        w_split = sem("w_split")
        o_in = sem("o_in")
        o_scaled = sem("o_scaled")
        o_hi_done = sem("o_hi_done")
        o_split = sem("o_split")
        srow_in = [sem(f"srow_in{i}") for i in range(2)]
        px_done = sem("px_done")
        pz_done = sem("pz_done")
        conv0_done = sem("conv0_done")
        tap1_done = sem("tap1_done")
        tap2_done = sem("tap2_done")
        conv_done = sem("conv_done")
        x_done = sem("x_done")
        z_done = sem("z_done")
        xtok_done = sem("xtok_done")
        dtx_done = sem("dtx_done")
        arg_done = sem("arg_done")
        dec_done = sem("dec_done")
        m_done = sem("m_done")
        y_done = sem("y_done")
        yd_done = sem("yd_done")
        gated = sem("gated")
        sq_done = sem("sq_done")
        sq_added = sem("sq_added")
        ghi_done = sem("ghi_done")
        glo_done = sem("glo_done")
        o_done = sem("o_done")
        o_added = sem("o_added")
        pool_set = sem("pool_set")
        ms_done = sem("ms_done")
        ms_copied = sem("ms_copied")
        rms_done = sem("rms_done")
        scaled = sem("scaled")
        block = ctx.enter_context(nc.Block())

        def pairs(eng, body):
            body(0, True, False)
            with eng.Fori(1, NCT // 2 - 1) as q:
                body(q, False, False)
            body(NCT // 2 - 1, False, True)

        @block.sync
        def _(sp):
            def load_w(c, par):
                sp.dma_start(wraw[:, par], w_xz[bass.ds(c, 1)].rearrange("o p n -> (o p) n")
                             ).then_inc(w_in[par], 16)

            def load_chan(c, par):
                sp.dma_start(chan[:, par], chan_par[bass.ds(c, 1)].rearrange("o p n -> (o p) n")
                             ).then_inc(chan_in[par], 16)

            def load_rows(c, half):
                for h in range(HPT):
                    sp.dma_start(srow[:, half, h, :],
                                 cs_dram[bass.ds(HPT * c + h, 1), half * TOK // 2:(half + 1) * TOK // 2]
                                 .partition_broadcast(P)).then_inc(srow_in[half], 16)

            load_w(0, 0)
            load_w(1, 1)
            load_chan(0, 0)
            load_rows(0, 0)
            load_rows(0, 1)

            def body(q, first, last):
                if not first:
                    sp.wait_ge(o_split, 2 * q)
                sp.dma_start(oraw[:], w_out[bass.ds(q, 1)].rearrange("o p e n -> (o p) e n")
                             ).then_inc(o_in, 16)
                for e in range(2):
                    c = 2 * q + e
                    if not last:
                        sp.wait_ge(w_split, c + 1)
                        load_w(c + 2, e)
                    if not (last and e):
                        if not (first and e == 0):
                            sp.wait_ge(yd_done, NB * c)
                        load_chan(c + 1, 1 - e)
                        for half in range(2):
                            sp.wait_ge(arg_done, SPB * (NB * c + NB // 2 * (half + 1)))
                            load_rows(c + 1, half)

            pairs(sp, body)

        @block.gpsimd
        def _(pool):
            pool.memset(sqacc[:], 0.0).then_inc(pool_set, 1)
            pool.memset(onesq[:], 1.0).then_inc(pool_set, 1)
            pool.memset(mhalf[:], -0.5).then_inc(pool_set, 1)
            pool.wait_ge(pool_set, 3)

            def split_w(c, par, k):
                pool.wait_ge(w_in[par], 16 * k)
                pool.wait_ge(w_hi_done, c + 1)
                pool.tensor_tensor(wlo[:, par].rearrange("p k m -> p (k m)"), wraw[:, par],
                                   whi[:, par].rearrange("p k m -> p (k m)").bitcast(F32),
                                   ALU.subtract).then_inc(w_split, 1)

            def s_by_tokens(c, par):
                pool.tensor_copy(stok[:, par], tokpar[:, :, bass.ds(NH + HPT * c, HPT)]
                                 ).then_inc(stok_done, 1)

            def split_o(q):
                pool.wait_ge(o_in, 16 * (q + 1))
                pool.tensor_tensor(oraw[:, :, 0:DM], oraw[:, :, 0:DM],
                                   oraw[:, :, DM:DM + 1].broadcast_to([P, 2, DM]),
                                   ALU.mult).then_inc(o_scaled, 1)
                pool.wait_ge(o_hi_done, 1 * q + 1)
                pool.tensor_tensor(olo[:], oraw[:, :, 0:DM], ohi[:].bitcast(F32),
                                   ALU.subtract).then_inc(o_split, 2)

            split_w(0, 0, 1)
            s_by_tokens(0, 0)

            def body(q, first, last):
                for e in range(2):
                    c = 2 * q + e
                    if not (last and e):
                        split_w(c + 1, 1 - e, q + 1 if e == 0 else q + 2)
                        if not (first and e == 0):
                            pool.wait_ge(arg_done, SPB * NB * c)
                        s_by_tokens(c + 1, 1 - e)
                    if e == 1:
                        if not first:
                            pool.wait_ge(o_done, 8 * q)
                        split_o(q)
                    for b in range(NB):
                        n = NB * c + b
                        t = slice(b * BLK, (b + 1) * BLK)
                        g = yg[:, b % 2, :]
                        pool.wait_ge(yd_done, n + 1)
                        pool.wait_ge(z_done, n + 1)
                        pool.tensor_tensor(g, g, zt[:, e, t], ALU.mult).then_inc(gated, 1)
                        pool.wait_ge(gated, n + 1)
                        if not (first and n == 0):
                            pool.wait_ge(sq_added, n)
                        pool.tensor_tensor(sq[:], g, g, ALU.mult).then_inc(sq_done, 1)
                        pool.wait_ge(ghi_done, n + 1)
                        pool.tensor_tensor(glo[:, e, t], g, ghi[:, e, t].bitcast(F32),
                                           ALU.subtract).then_inc(glo_done, 1)
                        pool.wait_ge(sq_done, n + 1)
                        pool.tensor_tensor(sqacc[:, t], sqacc[:, t], sq[:], ALU.add).then_inc(sq_added, 1)

            pairs(pool, body)
            pool.wait_ge(ms_copied, 1)
            pool.tensor_tensor(rms[:], rms[:], mhalf[:], ALU.pow).then_inc(rms_done, 1)

        @block.tensor
        def _(pe):
            def project_x(c, par, b, first):
                if b >= 2:
                    pe.wait_ge(conv_done, NB * c + b - 1)
                elif not first:
                    pe.wait_ge(z_done, NB * c + b - 1)
                project(pe, pa[b % 2][:], whi[:, par, 0:KD], wlo[:, par, 0:KD], xhi, xlo,
                        b).then_inc(px_done, 1)

            def project_z(c, par, b):
                if b >= 2:
                    pe.wait_ge(z_done, NB * c + b - 1)
                else:
                    pe.wait_ge(conv_done, NB * c + b + 3)
                project(pe, pa[b % 2][:], whi[:, par, KD:], wlo[:, par, KD:], xhi, xlo,
                        b).then_inc(pz_done, 1)

            def tokens(c, e, b, first):
                n = NB * c + b
                pe.wait_ge(x_done, n + 1)
                if not (first and e == 0 and b < 2):
                    pe.wait_ge(dtx_done, n - 1)
                for t in range(TPB):
                    last = pe.transpose(pt[b % 2][:, t * P:(t + 1) * P],
                                        xt[:, e, (b * TPB + t) * P:(b * TPB + t + 1) * P], ident[:])
                last.then_inc(xtok_done, 1)

            def outputs(c, e, b, first):
                n = NB * c + b
                pe.wait_ge(dtx_done, n + 1)
                if not (first and e == 0 and b < 2):
                    pe.wait_ge(yd_done, n - 1)
                for s in range(SPB):
                    pe.wait_ge(m_done, SPB * n + s + 1)
                    o = s * SEQ
                    for j, cols, m in ((0, slice(o, o + SEQ), slice(0, SEQ)),
                                       (1, slice(o + P, o + SEQ), slice(SEQ, LW))):
                        for h in range(HPT):
                            hp = slice(h * HD, (h + 1) * HD)
                            last = pe.matmul(py[b % 2][hp, cols], dtx[:, b % 2, 2 * s + j, hp],
                                             dec[:, b % 2, s, h, m], start=(j == 0), stop=(j == 1))
                    last.then_inc(y_done, 1)

            def output_rows(q, b, first):
                pe.wait_ge(glo_done, NB * (2 * q + 1) + b + 1)
                pe.wait_ge(o_split, 2 * q + 2)
                for t in range(TPB):
                    i = t // 2
                    if t % 2 == 0 and not (first and b == 0):
                        pe.wait_ge(o_added, 2 * NB * q + 2 * b + i - 1)
                    dst = po[i][:, (t % 2) * DM:(t % 2 + 1) * DM]
                    k = slice((b * TPB + t) * P, (b * TPB + t + 1) * P)
                    for e in range(2):
                        pe.matmul(dst, ghi[:, e, k], ohi[:, e, :], start=(e == 0), stop=False)
                        pe.matmul(dst, ghi[:, e, k], olo[:, e, :], start=False, stop=False)
                        last = pe.matmul(dst, glo[:, e, k], ohi[:, e, :], start=False, stop=(e == 1))
                    if t % 2:
                        last.then_inc(o_done, 1)

            pe.wait_ge(w_split, 1)
            for b in range(NB):
                project_x(0, 0, b, True)
            for b in range(NB):
                project_z(0, 0, b)

            def body(q, first, last):
                for e in range(2):
                    c = 2 * q + e
                    ahead = not (last and e)
                    if ahead:
                        pe.wait_ge(w_split, c + 2)
                    for b in range(NB):
                        if ahead:
                            project_x(c + 1, 1 - e, b, False)
                        tokens(c, e, b, first)
                        if b >= 1:
                            outputs(c, e, b - 1, first)
                        if e == 0 and not first and b in (1, 3):
                            output_rows(q - 1, 2 + b // 2, False)
                    outputs(c, e, NB - 1, first)
                    for b in range(NB):
                        if ahead:
                            project_z(c + 1, 1 - e, b)
                        if e == 1 and b % 2:
                            output_rows(q, b // 2, first)

            pairs(pe, body)
            for b in (2, 3):
                output_rows(NCT // 2 - 1, b, False)
            pe.wait_ge(sq_added, NB * NCT)
            for t in range(TILES):
                last = pe.matmul(pt[0][:, t:t + 1], sqacc[:, t * P:(t + 1) * P], onesq[:, 0:1],
                                 start=True, stop=True)
            last.then_inc(ms_done, 1)

        @block.scalar
        def _(act):
            def conv0(c, par, k, b, first):
                n = NB * c + b
                act.wait_ge(px_done, n + 1)
                if b == 0:
                    act.wait_ge(chan_in[par], 16 * k)
                if not first:
                    act.wait_ge(yd_done, n - 2 * NB + 1)
                act.activation(xt[:, par, b * BLK:(b + 1) * BLK], pa[b % 2][:], ACT.Identity,
                               bias=chan[:, par, TAPS:TAPS + 1],
                               scale=chan[:, par, TAPS - 1:TAPS]).then_inc(conv0_done, 1)

            def w_hi(c, par, k):
                act.wait_ge(w_in[par], 16 * k)
                act.copy(whi[:, par].rearrange("p k m -> p (k m)"), wraw[:, par]).then_inc(w_hi_done, 1)

            def silus(c, par, first):
                for b in range(NB):
                    t = slice(b * BLK, (b + 1) * BLK)
                    act.wait_ge(conv_done, NB * c + b + 1)
                    act.activation(xt[:, par, t], xt[:, par, t], ACT.Silu).then_inc(x_done, 1)
                for b in range(NB):
                    t = slice(b * BLK, (b + 1) * BLK)
                    act.wait_ge(pz_done, NB * c + b + 1)
                    if not first:
                        act.wait_ge(gated, NB * (c - 2) + b + 1)
                    act.activation(zt[:, par, t], pa[b % 2][:], ACT.Silu).then_inc(z_done, 1)

            def decays(c, b):
                for s in range(SPB):
                    act.wait_ge(arg_done, SPB * (NB * c + b) + s + 1)
                    d = dec[:, b % 2, s].rearrange("p h i -> p (h i)")
                    act.activation(d, d, ACT.Exp, scale=-1.0).then_inc(dec_done, 1)

            w_hi(0, 0, 1)
            for b in range(NB):
                conv0(0, 0, 1, b, True)
            silus(0, 0, True)

            def body(q, first, last):
                for e in range(2):
                    c = 2 * q + e
                    ahead = not (last and e)
                    k = q + 1 if e == 0 else q + 2
                    if ahead:
                        if not (first and e == 0):
                            act.wait_ge(pz_done, NB * c)
                        w_hi(c + 1, 1 - e, k)
                    for b in range(NB):
                        if ahead:
                            conv0(c + 1, 1 - e, k, b, first and e == 0)
                        decays(c, b)
                        if e == 1 and b == 0:
                            if not first:
                                act.wait_ge(o_done, 8 * q)
                            act.wait_ge(o_scaled, 1 * q + 1)
                            act.copy(ohi[:], oraw[:, :, 0:DM]).then_inc(o_hi_done, 1)
                    if ahead:
                        silus(c + 1, 1 - e, first and e == 0)

            pairs(act, body)
            for t in range(TILES):
                if t == 0:
                    act.wait_ge(rms_done, 1)
                    act.wait_ge(o_added, NB * NCT)
                act.activation(acc[:, t, :], acc[:, t, :], ACT.Identity,
                               scale=rms[:, t:t + 1]).then_inc(scaled, 1)

        @block.vector
        def _(dve):
            def taps(c, par, b, k):
                n = NB * c + b
                dst, src = xt[:, par, b * BLK:(b + 1) * BLK], pa[b % 2][:]
                wgt = chan[:, par, TAPS - 1 - k:TAPS - k]
                before, done = [(conv0_done, tap1_done), (tap1_done, tap2_done),
                                (tap2_done, conv_done)][k - 1]
                dve.wait_ge(before, n + 1)
                conv_tap(dve, dst, src, wgt, k).then_inc(done, 1)

            def dt_x(c, e, b, first):
                n = NB * c + b
                dve.wait_ge(xtok_done, n + 1)
                if not (first and e == 0 and b < 2):
                    dve.wait_ge(y_done, SPB * (n - 1))
                dt = tokpar[:, b * TPB:(b + 1) * TPB, bass.ds(HPT * c, HPT)]
                dve.tensor_tensor(dtx[:, b % 2].rearrange("p t (h d) -> p t h d", h=HPT),
                                  pt[b % 2][:].rearrange("p (t h d) -> p t h d", t=TPB, h=HPT),
                                  dt.unsqueeze(3).broadcast_to([P, TPB, HPT, HD]),
                                  ALU.mult).then_inc(dtx_done, 1)

            def exponents(c, e, b, s, first):
                m = SPB * (NB * c + b) + s
                half, i0 = b // 2, b % 2 * BLK + s * SEQ
                if b == 0 and s == 0:
                    dve.wait_ge(stok_done, 1 * c + 1)
                if b % 2 == 0 and s == 0:
                    dve.wait_ge(srow_in[half], 16 * HPT * (c + 1))
                if not (first and b < 2):
                    dve.wait_ge(y_done, m - 2 * SPB + 1)
                for h in range(HPT):
                    for j, cols, k in ((0, slice(i0, i0 + SEQ), slice(0, SEQ)),
                                       (1, slice(i0 + P, i0 + SEQ), slice(SEQ, LW))):
                        tile = b * TPB + 2 * s + j
                        last = dve.tensor_scalar(dec[:, b % 2, s, h, k], srow[:, half, h, cols],
                                                 stok[:, e, tile, h:h + 1], -CAP, ALU.subtract,
                                                 ALU.max)
                last.then_inc(arg_done, 1)

            def times_g(c, b, s):
                d = dec[:, b % 2, s]
                g = gmat[:, b * SPB + s, :].unsqueeze(1).broadcast_to([P, HPT, LW])
                dve.wait_ge(dec_done, SPB * (NB * c + b) + s + 1)
                dve.tensor_tensor(d, d, g, ALU.mult).then_inc(m_done, 1)

            def add_dx(c, e, b, first):
                n = NB * c + b
                dve.wait_ge(y_done, SPB * (n + 1))
                if not (first and e == 0 and b < 2):
                    dve.wait_ge(sq_done, n - 1)
                    dve.wait_ge(glo_done, n - 1)
                dve.scalar_tensor_tensor(yg[:, b % 2, :], xt[:, e, b * BLK:(b + 1) * BLK],
                                         chan[:, e, TAPS + 1:TAPS + 2], py[b % 2][:], ALU.mult,
                                         ALU.add).then_inc(yd_done, 1)

            def gated_hi(c, e, b, first):
                n = NB * c + b
                dve.wait_ge(gated, n + 1)
                if not first:
                    dve.wait_ge(o_done, NB * (c - e) - 2 * NB + 2 * (b + 1))
                dve.tensor_copy(ghi[:, e, b * BLK:(b + 1) * BLK], yg[:, b % 2, :]).then_inc(ghi_done, 1)

            def add_rows(q, b, first):
                for i in range(2):
                    m = 2 * NB * q + 2 * b + i
                    dve.wait_ge(o_done, m + 1)
                    if not first:
                        dve.wait_ge(o_added, m - 3)
                    rows = acc[:, b * TPB + 2 * i:b * TPB + 2 * i + 2, :].rearrange("p t d -> p (t d)")
                    dve.tensor_tensor(rows, po[i][:], rows, ALU.add).then_inc(o_added, 1)

            for b in range(NB):
                for k in range(1, TAPS):
                    taps(0, 0, b, k)
            for s in range(SPB):
                exponents(0, 0, 0, s, True)

            def body(q, first, last):
                for e in range(2):
                    c = 2 * q + e
                    ahead = not (last and e)
                    for b in range(NB):
                        def next_exponents(s):
                            if b < NB - 1:
                                exponents(c, e, b + 1, s, first and e == 0)
                            elif ahead:
                                exponents(c + 1, 1 - e, 0, s, False)

                        if ahead:
                            taps(c + 1, 1 - e, b, 1)
                        next_exponents(0)
                        dt_x(c, e, b, first)
                        if ahead:
                            taps(c + 1, 1 - e, b, 2)
                        next_exponents(1)
                        times_g(c, b, 0)
                        times_g(c, b, 1)
                        if ahead:
                            taps(c + 1, 1 - e, b, 3)
                        if b >= 1:
                            add_dx(c, e, b - 1, first)
                        if b >= 2:
                            gated_hi(c, e, b - 2, first)
                        if e == 0 and not first and b == 3:
                            add_rows(q - 1, 2, first)
                    add_dx(c, e, NB - 1, first)
                    gated_hi(c, e, NB - 2, first)
                    if e == 0 and not first:
                        add_rows(q - 1, 3, first)
                    gated_hi(c, e, NB - 1, first)
                    if e == 1:
                        add_rows(q, 0, first)
                        add_rows(q, 1, first)

            pairs(dve, body)
            add_rows(NCT // 2 - 1, 2, False)
            add_rows(NCT // 2 - 1, 3, False)
            dve.wait_ge(ms_done, 1)
            dve.tensor_scalar(rms[:], pt[0][:, 0:TILES], 1.0 / DI, EPS, ALU.mult,
                              ALU.add).then_inc(ms_copied, 1)


def mlp(nc, hidden, xn_dram, w1, w2, b2, ln_g, ln_b, ln_cols, ident, xhi, xlo, acc, out, tiled):
    with ExitStack() as ctx:
        sb = lambda name, shape, dt=F32: ctx.enter_context(nc.sbuf_tensor("mlp_" + name, shape, dt))
        ps = lambda name: ctx.enter_context(nc.psum_tensor("mlp_" + name, [P, BLK], F32))
        sem = lambda name: ctx.enter_context(nc.semaphore("mlp_" + name))
        res = sb("res", [P, TILES, DM])
        w1raw = sb("w1raw", [P, KD * HID + KH])
        w1hi = sb("w1hi", [P, KD, HID], F32R)
        w1lo = sb("w1lo", [P, KD, HID], F32R)
        w2raw = sb("w2raw", [P, KH, DM])
        w2hi = sb("w2hi", [P, KH, DM], F32R)
        w2lo = sb("w2lo", [P, KH, DM], F32R)
        b1c = sb("b1c", [P, KH])
        gbc = sb("gbc", [P, (NL - 1) * 2 * KD])
        grow = sb("grow", [P, 3, DM])
        h = sb("h", [P, 4, BLK])
        hhi = sb("hhi", [P, 2, KH, BLK], F32R)
        hlo = sb("hlo", [P, 2, KH, BLK], F32R)
        u = sb("u2", [P, 2, TPB, DM])
        xf = sb("xf", [P, KD, BLK])
        stats = sb("stats2", [P, TPB, 6])
        mv = sb("mv2", [P, TPB, 2])
        vare = sb("vare2", [P, TPB])
        rstd = sb("rstd2", [P, TPB])
        mhalf = sb("mhalf2", [P, TPB])
        hidt = sb("hidt", [P, TPB, DM])
        p1 = [ps(f"p1{i}") for i in range(4)]
        p2 = [ps(f"p2{i}") for i in range(2)]
        p3 = [ps(f"p3{i}") for i in range(2)]

        const_in = sem("const_in2")
        res_in = sem("res_in")
        w1_in = sem("w1_in")
        w2_in = sem("w2_in")
        w1_hi_done = sem("w1_hi_done")
        w1_split = sem("w1_split")
        b1_done = sem("b1_done")
        w2_hi_done = sem("w2_hi_done")
        w2_split = sem("w2_split")
        grow_in = sem("grow_in")
        brow_done = sem("brow_done")
        first_done = sem("first_done")
        gelu_done = sem("gelu_done")
        hhi_done = sem("hhi_done")
        hlo_done = sem("hlo_done")
        second_done = sem("second_done")
        u_done = sem("u_done2")
        stats_done = sem("stats_done2")
        stats_seen = sem("stats_seen")
        mv_done = sem("mv_done2")
        vare_done = sem("vare_done2")
        rstd_done = sem("rstd_done2")
        norm_done = sem("norm_done2")
        tr_done = sem("tr_done2")
        xf_done = sem("xf_done")
        xhi_done = sem("xhi_done")
        xlo_done = sem("xlo_done")
        scaled_done = sem("scaled_done")
        res_done = sem("res_done")
        pool_set = sem("pool_set2")
        hid_in = sem("hid_in2")
        mixed = sem("mixed")
        final = sem("final")
        out_done = sem("out_done")
        block = ctx.enter_context(nc.Block())

        def layers(eng, body):
            body(0, True, False)
            with eng.Fori(1, NL - 1) as l:
                body(l, False, False)
            body(NL - 1, False, True)

        @block.sync
        def _(sp):
            sp.dma_start(w1raw[:], w1[0]).then_inc(w1_in, 16)
            sp.dma_start(w2raw[:], w2[0]).then_inc(w2_in, 16)
            sp.dma_start(gbc[:], ln_cols).then_inc(const_in, 16)
            sp.dma_start(res[:], tiled(xn_dram)).then_inc(res_in, 16)
            sp.dma_start(grow[:, 2, :], b2[0:1, :].partition_broadcast(P)).then_inc(grow_in, 16)

            def body(l, first, last):
                if last:
                    return
                sp.wait_ge(w1_split, 1 * l + 1)
                sp.dma_start(w1raw[:], w1[bass.ds(l + 1, 1)].rearrange("o p n -> (o p) n")
                             ).then_inc(w1_in, 16)
                if first:
                    sp.wait_ge(res_done, NB)
                else:
                    sp.wait_ge(res_done, NB * l + NB)
                for i, row in enumerate((ln_g[bass.ds(l, 1), :], ln_b[bass.ds(l, 1), :],
                                         b2[bass.ds(l + 1, 1), :])):
                    sp.dma_start(grow[:, i, :], row.partition_broadcast(P)).then_inc(grow_in, 16)
                sp.wait_ge(w2_split, 1 * l + 1)
                sp.dma_start(w2raw[:], w2[bass.ds(l + 1, 1)].rearrange("o p k m -> (o p) k m")
                             ).then_inc(w2_in, 16)

            layers(sp, body)
            for b in range(NB):
                if b:
                    sp.wait_ge(mixed, b)
                sp.dma_start(hidt[:], tiled(hidden)[:, b * TPB:(b + 1) * TPB, :]).then_inc(hid_in, 16)
            for b in range(NB):
                sp.wait_ge(final, TPB // 2 * (b + 1))
                sp.dma_start(tiled(out)[:, b * TPB:(b + 1) * TPB, :],
                             acc[:, b * TPB:(b + 1) * TPB, :]).then_inc(out_done, 16)
            sp.wait_ge(out_done, 16 * NB)

        @block.gpsimd
        def _(pool):
            flat = lambda ap: ap[:].rearrange("p k m -> p (k m)")

            def split(l, raw, hi, lo, loaded, hi_done, done):
                pool.wait_ge(loaded, 16 * (l + 1))
                pool.wait_ge(hi_done, 1 * l + 1)
                pool.tensor_tensor(flat(lo), raw, flat(hi).bitcast(F32), ALU.subtract).then_inc(done, 1)

            pool.memset(mhalf[:], -0.5).then_inc(pool_set, 1)
            split(0, w1raw[:, 0:KD * HID], w1hi, w1lo, w1_in, w1_hi_done, w1_split)
            split(0, flat(w2raw), w2hi, w2lo, w2_in, w2_hi_done, w2_split)
            pool.wait_ge(res_in, 16)
            pool.wait_ge(grow_in, 16)
            for b in range(NB):
                r = res[:, b * TPB:(b + 1) * TPB, :]
                pool.tensor_tensor(r, r, grow[:, 2, :].unsqueeze(1).broadcast_to([P, TPB, DM]),
                                   ALU.add).then_inc(res_done, 1)
            pool.wait_ge(pool_set, 1)

            def body(l, first, last):
                if last:
                    for b in range(NB):
                        a = acc[:, b * TPB:(b + 1) * TPB, :]
                        pool.wait_ge(hid_in, 16 * (b + 1))
                        pool.tensor_tensor(a, a, hidt[:], ALU.add).then_inc(mixed, 1)
                    return
                pool.wait_ge(grow_in, 48 * l + 64)
                pool.tensor_tensor(grow[:, 1, :], grow[:, 1, :], grow[:, 2, :],
                                   ALU.add).then_inc(brow_done, 1)
                pool.wait_ge(brow_done, 1 * l + 1)
                for b in range(NB):
                    n = NB * l + b
                    if b == 3:
                        split(l + 1, w1raw[:, 0:KD * HID], w1hi, w1lo, w1_in, w1_hi_done, w1_split)
                    pool.wait_ge(vare_done, n + 1)
                    pool.tensor_tensor(rstd[:], vare[:], mhalf[:], ALU.pow).then_inc(rstd_done, 1)
                    r = res[:, b * TPB:(b + 1) * TPB, :]
                    pool.wait_ge(norm_done, TPB * (n + 1))
                    pool.tensor_tensor(r, u[:, b % 2], grow[:, 0, :].unsqueeze(1).broadcast_to([P, TPB, DM]),
                                       ALU.mult).then_inc(scaled_done, 1)
                    pool.wait_ge(scaled_done, n + 1)
                    pool.tensor_tensor(r, r, grow[:, 1, :].unsqueeze(1).broadcast_to([P, TPB, DM]),
                                       ALU.add).then_inc(res_done, 1)
                split(l + 1, flat(w2raw), w2hi, w2lo, w2_in, w2_hi_done, w2_split)

            layers(pool, body)

        @block.tensor
        def _(pe):
            def first_product(l, b, first):
                n = NB * l + b
                if b == 0:
                    pe.wait_ge(w1_split, 1 * l + 1)
                if not first:
                    pe.wait_ge(xlo_done, KD * (n - NB + 1))
                cols = slice(b * BLK, (b + 1) * BLK)
                for j in range(KH):
                    m = KH * n + j
                    if not (first and b == 0 and j < 4):
                        pe.wait_ge(gelu_done, m - 3)
                    hj = slice(j * P, (j + 1) * P)
                    project(pe, p1[j % 4][:], w1hi[:, :, hj], w1lo[:, :, hj], xhi, xlo,
                            b).then_inc(first_done, 1)

            def transposes(l, b, first):
                n = NB * l + b
                pe.wait_ge(norm_done, TPB * (n + 1))
                if not (first and b == 0):
                    pe.wait_ge(xf_done, KD * n)
                for k in range(KD):
                    for t in range(TPB):
                        last = pe.transpose(p3[k][:, t * P:(t + 1) * P],
                                            u[:, b % 2, t, k * P:(k + 1) * P], ident[:])
                    last.then_inc(tr_done, 1)

            def second_product(l, b, first):
                n = NB * l + b
                if b == 0:
                    pe.wait_ge(w2_split, 1 * l + 1)
                pe.wait_ge(hlo_done, KH * (n + 1))
                for t in range(TPB):
                    i = t // 2
                    if t % 2 == 0 and not (first and b == 0):
                        pe.wait_ge(u_done, 2 * n + i - 1)
                    dst = p2[i][:, (t % 2) * DM:(t % 2 + 1) * DM]
                    k = slice(t * P, (t + 1) * P)
                    for j in range(KH):
                        pe.matmul(dst, hhi[:, b % 2, j, k], w2hi[:, j, :], start=(j == 0), stop=False)
                        pe.matmul(dst, hhi[:, b % 2, j, k], w2lo[:, j, :], start=False, stop=False)
                        last = pe.matmul(dst, hlo[:, b % 2, j, k], w2hi[:, j, :], start=False,
                                         stop=(j == KH - 1))
                    if t % 2:
                        last.then_inc(second_done, 1)

            first_product(0, 0, True)

            def body(l, first, last):
                for b in range(NB):
                    if b < NB - 1:
                        first_product(l, b + 1, first)
                    elif not last:
                        first_product(l + 1, 0, False)
                    if b == 0:
                        if not first:
                            transposes(l - 1, NB - 1, False)
                    elif not last:
                        transposes(l, b - 1, first)
                    second_product(l, b, first)

            layers(pe, body)

        @block.scalar
        def _(act):
            def hidden_block(l, b, first):
                n = NB * l + b
                for j in range(KH):
                    m = KH * n + j
                    act.wait_ge(first_done, m + 1)
                    if not (first and b == 0 and j < 4):
                        act.wait_ge(hlo_done, m - 3)
                    act.activation(h[:, j % 4, :], p1[j % 4][:], ACT.Gelu,
                                   bias=b1c[:, j:j + 1]).then_inc(gelu_done, 1)
                    act.wait_ge(gelu_done, m + 1)
                    if j == 0 and not (first and b < 2):
                        act.wait_ge(second_done, 2 * (n - 1))
                    act.copy(hhi[:, b % 2, j, :], h[:, j % 4, :]).then_inc(hhi_done, 1)

            def x_hi(l, b):
                n = NB * l + b
                for k in range(KD):
                    act.wait_ge(xf_done, KD * n + k + 1)
                    act.copy(xhi[:, k, b * BLK:(b + 1) * BLK], xf[:, k, :]).then_inc(xhi_done, 1)

            flat = lambda ap: ap[:].rearrange("p k m -> p (k m)")

            def w_hi(l, raw, hi, loaded, done):
                act.wait_ge(loaded, 16 * (l + 1))
                act.copy(flat(hi), raw).then_inc(done, 1)

            def biases(l):
                act.copy(b1c[:], w1raw[:, KD * HID:]).then_inc(b1_done, 1)
                act.wait_ge(b1_done, 1 * l + 1)

            act.wait_ge(w1_in, 16)
            biases(0)
            w_hi(0, w1raw[:, 0:KD * HID], w1hi, w1_in, w1_hi_done)
            w_hi(0, flat(w2raw), w2hi, w2_in, w2_hi_done)
            hidden_block(0, 0, True)

            def body(l, first, last):
                for b in range(NB):
                    if b == 1 and not first:
                        act.wait_ge(second_done, 2 * NB * l)
                        w_hi(l, flat(w2raw), w2hi, w2_in, w2_hi_done)
                    if b < NB - 1:
                        hidden_block(l, b + 1, first)
                    elif not last:
                        act.wait_ge(first_done, KH * NB * (l + 1))
                        act.wait_ge(gelu_done, KH * NB * (l + 1))
                        act.wait_ge(w1_in, 16 * (l + 2))
                        biases(l + 1)
                        w_hi(l + 1, w1raw[:, 0:KD * HID], w1hi, w1_in, w1_hi_done)
                        hidden_block(l + 1, 0, False)
                    if b == 0:
                        if not first:
                            x_hi(l - 1, NB - 1)
                    elif not last:
                        x_hi(l, b - 1)

            layers(act, body)

        @block.vector
        def _(dve):
            def h_lo(l, b, first):
                n = NB * l + b
                for j in range(KH):
                    m = KH * n + j
                    dve.wait_ge(hhi_done, m + 1)
                    if j == 0 and not (first and b < 2):
                        dve.wait_ge(second_done, 2 * (n - 1))
                    dve.tensor_tensor(hlo[:, b % 2, j, :], h[:, j % 4, :],
                                      hhi[:, b % 2, j, :].bitcast(F32), ALU.subtract).then_inc(hlo_done, 1)

            def sums(l, b, first):
                n = NB * l + b
                dve.wait_ge(res_done, 1 * n + 1)
                if not (first and b < 2):
                    dve.wait_ge(tr_done, KD * (n - 1))
                    if first:
                        dve.wait_ge(res_done, NB + n - 1)
                    else:
                        dve.wait_ge(res_done, NB + n - 1)
                for i in range(2):
                    dve.wait_ge(second_done, 2 * n + i + 1)
                    dve.tensor_tensor(u[:, b % 2, 2 * i:2 * i + 2, :].rearrange("p t d -> p (t d)"),
                                      p2[i][:],
                                      res[:, b * TPB + 2 * i:b * TPB + 2 * i + 2, :]
                                      .rearrange("p t d -> p (t d)"), ALU.add).then_inc(u_done, 1)
                for t in range(TPB):
                    dve.wait_ge(u_done, 2 * n + t // 2 + 1)
                    dve.bn_stats(stats[:, t, :], u[:, b % 2, t, :]).then_inc(stats_done, 1)
                dve.wait_ge(stats_done, TPB * (n + 1))
                dve.sem_inc(stats_seen, 1)
                for t in range(TPB):
                    dve.bn_aggr(mv[:, t, :], stats[:, t, :]).then_inc(mv_done, 1)
                dve.wait_ge(mv_done, TPB * (n + 1))
                dve.tensor_scalar(vare[:], mv[:, :, 1], EPS, None, ALU.add).then_inc(vare_done, 1)
                dve.wait_ge(rstd_done, n + 1)
                for t in range(TPB):
                    dve.tensor_scalar(u[:, b % 2, t, :], u[:, b % 2, t, :], mv[:, t, 0:1],
                                      rstd[:, t:t + 1], ALU.subtract, ALU.mult).then_inc(norm_done, 1)

            def x_parts(l, b, first):
                n = NB * l + b
                for k in range(KD):
                    dve.wait_ge(tr_done, KD * n + k + 1)
                    if not (first and b == 0):
                        dve.wait_ge(xlo_done, KD * n - KD + k + 1)
                        dve.wait_ge(xhi_done, KD * n - KD + k + 1)
                    dve.tensor_scalar(xf[:, k, :], p3[k][:], gbc[:, bass.ds(2 * KD * l + k, 1)],
                                      gbc[:, bass.ds(2 * KD * l + KD + k, 1)], ALU.mult,
                                      ALU.add).then_inc(xf_done, 1)
                for k in range(KD):
                    dve.wait_ge(xhi_done, KD * n + k + 1)
                    dve.tensor_tensor(xlo[:, k, b * BLK:(b + 1) * BLK], xf[:, k, :],
                                      xhi[:, k, b * BLK:(b + 1) * BLK].bitcast(F32),
                                      ALU.subtract).then_inc(xlo_done, 1)

            def last_sums(l, b):
                n = NB * l + b
                dve.wait_ge(res_done, n + 1)
                dve.wait_ge(mixed, b + 1)
                for i in range(2):
                    dve.wait_ge(second_done, 2 * n + i + 1)
                    r = res[:, b * TPB + 2 * i:b * TPB + 2 * i + 2, :].rearrange("p t d -> p (t d)")
                    a = acc[:, b * TPB + 2 * i:b * TPB + 2 * i + 2, :].rearrange("p t d -> p (t d)")
                    dve.tensor_tensor(r, p2[i][:], r, ALU.add).then_inc(u_done, 1)
                    dve.wait_ge(u_done, 2 * n + i + 1)
                    dve.tensor_tensor(a, a, r, ALU.add).then_inc(final, 1)

            dve.wait_ge(const_in, 16)
            h_lo(0, 0, True)

            def body(l, first, last):
                for b in range(NB):
                    if b < NB - 1:
                        h_lo(l, b + 1, first)
                    elif not last:
                        h_lo(l + 1, 0, False)
                    if b == 0:
                        if not first:
                            x_parts(l - 1, NB - 1, False)
                    elif not last:
                        x_parts(l, b - 1, first)
                    if last:
                        last_sums(l, b)
                    else:
                        sums(l, b, first)

            layers(dve, body)


def kernel(**inputs):
    import numpy as np
    import concourse.bacc as bacc
    from concourse.bass_utils import run_bass_kernel_spmd

    a = {k: np.asarray(v) for k, v in inputs.items()}

    def cols(x, n):
        return np.moveaxis(x.reshape(n, P, *x.shape[1:]), 0, 1)

    w_in = cols(a["L0_attn_W_in"], KD)
    z, x, bc, dt = np.split(w_in, [DI, 2 * DI, 2 * DI + 2 * P], axis=2)
    xz = np.concatenate([x.reshape(P, KD, NCT, P), z.reshape(P, KD, NCT, P)], axis=1)
    conv = np.concatenate([a["L0_attn_conv_w"], a["L0_attn_conv_b"][:, None]], axis=1)
    conv = conv.reshape(NCT + 2, P, TAPS + 1)
    w1 = a["L0_ffn_W1"].transpose(0, 2, 1).reshape(NL, KD, P, HID).transpose(0, 2, 1, 3)
    b1 = a["L0_ffn_B1"].reshape(NL, KH, P).transpose(0, 2, 1)
    rows = np.arange(P)
    upper = (rows[None, :] >= rows[:, None]).astype(np.float32)
    ln_cols = np.stack([a["L0_ffn_LN_G"].reshape(NL - 1, KD, P), a["L0_ffn_LN_B"].reshape(NL - 1, KD, P)],
                       axis=1)
    arrays = dict(
        hidden=a["L0_attn_hidden_states"].reshape(TOK, DM),
        w_bcdt=np.concatenate([dt, dt, bc], axis=2),
        w_xz=xz.transpose(2, 0, 1, 3).reshape(NCT, P, 2 * KD * P),
        chan_par=np.concatenate([conv[:NCT], np.repeat(a["L0_attn_D"], HD).reshape(NCT, P, 1)], axis=2),
        conv_bc=np.moveaxis(conv[NCT:], 0, 1),
        dt_par=np.stack([np.tile(a["L0_attn_dt_bias"], 2), np.tile(a["L0_attn_A"], 2)], axis=1),
        w_out=np.concatenate([a["L0_attn_W_out"], a["L0_attn_norm_w"][:, None]], axis=1)
        .reshape(NCT // 2, 2, P, DM + 1).transpose(0, 2, 1, 3),
        w1=np.concatenate([w1.reshape(NL, P, KD * HID), b1], axis=2),
        w2=a["L0_ffn_W2"].transpose(0, 2, 1).reshape(NL, KH, P, DM).transpose(0, 2, 1, 3),
        b2=a["L0_ffn_B2"],
        ln_g=a["L0_ffn_LN_G"],
        ln_b=a["L0_ffn_LN_B"],
        ln_cols=np.moveaxis(ln_cols, 3, 0).reshape(P, -1),
        ident_in=np.eye(P, dtype=np.float32),
        mask_in=np.concatenate([upper, np.ones((P, P), np.float32), upper], axis=1),
    )
    arrays = {k: np.ascontiguousarray(v) for k, v in arrays.items()}
    nc = bacc.Bacc("TRN2", target_bir_lowering=False, num_devices=1)
    args = {k: nc.dram_tensor(k, v.shape, mybir.dt.from_np(v.dtype), kind="ExternalInput").ap()
            for k, v in arrays.items()}
    shape = a["L0_attn_hidden_states"].shape
    result = nc.dram_tensor("result", (TOK, DM), F32, kind="ExternalOutput").ap()
    build(nc, out=result, **args)
    r = run_bass_kernel_spmd(nc, [arrays], core_ids=[0])
    return r.results[0]["result"].reshape(shape)
```

```python
from collections import namedtuple
from contextlib import ExitStack

import concourse.bass as bass
from concourse import mybir

F32 = mybir.dt.float32
F32R = mybir.dt.float32r
ALU = mybir.AluOpType
ACT = mybir.ActivationFunctionType

P = 128
SEQ = 256
NSEQ = 8
TOK = NSEQ * SEQ
TILES = TOK // P
DM = 256
KD = DM // P
DI = 4096
NCT = DI // P
PAIRS = NCT // 2
HD = 64
HPT = P // HD
NH = DI // HD
TAPS = 4
BLK = 512
NB = TOK // BLK
TPB = BLK // P
SPB = BLK // SEQ
LW = SEQ + P
HID = 1024
KH = HID // P
NL = 6
EPS = 1e-5
CAP = 80.0


def build(nc, hidden, w_bcdt, conv_bc, dt_par, w_xz, conv_par, d_par, w_out,
          w1, w2, b2, ln_g, ln_b, ln_cols, ident_in, mask_in, out):
    cs_dram = nc.dram_tensor("cs_rows", [NH, TOK], F32, kind="Internal").ap()
    xn_dram = nc.dram_tensor("xn_rows", [TOK, DM], F32, kind="Internal").ap()
    tiled = lambda ap: ap.rearrange("(t p) d -> p t d", p=P)

    with ExitStack() as ctx:
        def sb(name, shape, dt=F32, stack=ctx):
            return stack.enter_context(nc.sbuf_tensor(name, shape, dt))

        ident = sb("ident", [P, P])
        xhi = sb("xhi", [P, KD, TOK], F32R)
        xlo = sb("xlo", [P, KD, TOK], F32R)
        acc = sb("acc", [P, TILES, DM])

        with ExitStack() as mixer:
            gmat = sb("gmat", [P, NSEQ, LW], stack=mixer)
            tokpar = sb("tokpar", [P, TILES, 2 * NH], stack=mixer)
            normalise(nc, hidden, xn_dram, ident_in, ident, xhi, xlo, tiled)
            prepare(nc, w_bcdt, conv_bc, dt_par, mask_in, cs_dram,
                    ident, xhi, xlo, acc, gmat, tokpar)
            mix(nc, w_xz, conv_par, d_par, w_out, cs_dram, ident, xhi, xlo, acc, gmat, tokpar)
        mlp(nc, hidden, xn_dram, w1, w2, b2, ln_g, ln_b, ln_cols, ident, xhi, xlo, acc, out,
            tiled)


def normalise(nc, hidden, xn_dram, ident_in, ident, xhi, xlo, tiled):
    with ExitStack() as ctx:
        sb = lambda name, shape, dt=F32: ctx.enter_context(nc.sbuf_tensor("norm_" + name, shape, dt))
        sem = lambda name: ctx.enter_context(nc.semaphore("norm_" + name))
        hid = sb("hid", [P, TILES, DM])
        stats = sb("stats", [P, TILES, 6])
        mv = sb("mv", [P, TILES, 2])
        vare = sb("vare", [P, TILES])
        rstd = sb("rstd", [P, TILES])
        mhalf = sb("mhalf", [P, TPB])
        tp = [[ctx.enter_context(nc.psum_tensor(f"norm_tp{i}{k}", [P, BLK], F32)) for k in range(KD)]
              for i in range(2)]
        const_in = sem("const_in")
        hid_in = [sem(f"hid_in{b}") for b in range(NB)]
        mhalf_set = sem("mhalf_set")
        stats_done = sem("stats_done")
        mv_done = sem("mv_done")
        vare_done = sem("vare_done")
        rstd_done = sem("rstd_done")
        xn_done = sem("xn_done")
        xt_done = sem("xt_done")
        hi_done = sem("hi_done")
        lo_done = sem("lo_done")
        xn_out = sem("xn_out")
        block = ctx.enter_context(nc.Block())

        @block.sync
        def _(sp):
            for b in range(NB):
                sp.dma_start(hid[:, b * TPB:(b + 1) * TPB, :],
                             tiled(hidden)[:, b * TPB:(b + 1) * TPB, :]).then_inc(hid_in[b], 16)
                if b == 0:
                    sp.dma_start(ident[:], ident_in).then_inc(const_in, 16)
            for b in range(NB):
                sp.wait_ge(xn_done, TPB * (b + 1))
                sp.dma_start(tiled(xn_dram)[:, b * TPB:(b + 1) * TPB, :],
                             hid[:, b * TPB:(b + 1) * TPB, :]).then_inc(xn_out, 16)
            sp.wait_ge(xn_out, 16 * NB)

        @block.gpsimd
        def _(pool):
            pool.memset(mhalf[:], -0.5).then_inc(mhalf_set, 1)
            pool.wait_ge(mhalf_set, 1)
            for b in range(NB):
                pool.wait_ge(vare_done, b + 1)
                pool.tensor_tensor(rstd[:, b * TPB:(b + 1) * TPB], vare[:, b * TPB:(b + 1) * TPB],
                                   mhalf[:], ALU.pow).then_inc(rstd_done, 1)

        @block.vector
        def _(dve):
            def lo_part(b):
                for k in range(KD):
                    dve.wait_ge(hi_done, KD * b + k + 1)
                    dve.tensor_tensor(xlo[:, k, b * BLK:(b + 1) * BLK], tp[b % 2][k][:],
                                      xhi[:, k, b * BLK:(b + 1) * BLK].bitcast(F32),
                                      ALU.subtract).then_inc(lo_done, 1)

            def moments(b):
                dve.wait_ge(hid_in[b], 16)
                for t in range(b * TPB, (b + 1) * TPB):
                    dve.bn_stats(stats[:, t, :], hid[:, t, :]).then_inc(stats_done, 1)
                for t in range(b * TPB, (b + 1) * TPB):
                    dve.wait_ge(stats_done, t + 1)
                    dve.bn_aggr(mv[:, t, :], stats[:, t, :]).then_inc(mv_done, 1)
                dve.wait_ge(mv_done, TPB * (b + 1))
                dve.tensor_scalar(vare[:, b * TPB:(b + 1) * TPB], mv[:, b * TPB:(b + 1) * TPB, 1],
                                  EPS, None, ALU.add).then_inc(vare_done, 1)

            moments(0)
            for b in range(NB):
                if b + 1 < NB:
                    moments(b + 1)
                dve.wait_ge(rstd_done, b + 1)
                for t in range(b * TPB, (b + 1) * TPB):
                    dve.tensor_scalar(hid[:, t, :], hid[:, t, :], mv[:, t, 0:1], rstd[:, t:t + 1],
                                      ALU.subtract, ALU.mult).then_inc(xn_done, 1)
                if b >= 1:
                    lo_part(b - 1)
            lo_part(NB - 1)

        @block.tensor
        def _(pe):
            pe.wait_ge(const_in, 16)
            for b in range(NB):
                pe.wait_ge(xn_done, TPB * (b + 1))
                if b >= 2:
                    pe.wait_ge(lo_done, KD * (b - 1))
                for k in range(KD):
                    for t in range(TPB):
                        last = pe.transpose(tp[b % 2][k][:, t * P:(t + 1) * P],
                                            hid[:, b * TPB + t, k * P:(k + 1) * P], ident[:])
                    last.then_inc(xt_done, 1)

        @block.scalar
        def _(act):
            for b in range(NB):
                for k in range(KD):
                    act.wait_ge(xt_done, KD * b + k + 1)
                    act.copy(xhi[:, k, b * BLK:(b + 1) * BLK], tp[b % 2][k][:]).then_inc(hi_done, 1)


def prepare(nc, w_bcdt, conv_bc, dt_par, mask_in, cs_dram,
            ident, xhi, xlo, acc, gmat, tokpar):
    with ExitStack() as ctx:
        sb = lambda name, shape, dt=F32: ctx.enter_context(nc.sbuf_tensor("prep_" + name, shape, dt))
        sem = lambda name: ctx.enter_context(nc.semaphore("prep_" + name))
        mask = sb("mask", [P, LW])
        cbc = sb("cbc", [P, 2, TAPS + 1])
        par = sb("par", [P, 2])
        w_raw = sb("wbc_raw", [P, KD, 3 * P])
        w_hi = sb("wbc_hi", [P, KD, 3 * P], F32R)
        w_lo = sb("wbc_lo", [P, KD, 3 * P], F32R)
        bct = sb("bct", [P, 2, TOK])
        v = sb("v", [P, TOK])
        u = sb("u", [P, TOK])
        w = sb("w", [P, TOK])
        v_ln = sb("v_ln", [P, TOK])
        dtcs = sb("dtcs", [P, TOK])
        ones = sb("ones", [P, SEQ])
        bank = [ctx.enter_context(nc.psum_tensor(f"prep_prep{i}", [P, BLK], F32)) for i in range(8)]
        consts_in = sem("consts_in")
        wbc_in = sem("wbc_in")
        w_split = sem("w_split")
        ones_set = sem("ones_set")
        proj_done = sem("proj_done")
        v_done = sem("v_done")
        abs_done = sem("abs_done")
        u_done = sem("u_done")
        w_done = sem("w_done")
        ln_done = sem("ln_done")
        sp_step = sem("sp_step")
        dt_done = sem("dt_done")
        cs_done = sem("cs_done")
        cs_out = sem("cs_out")
        conv0_done = sem("conv0_done")
        tap_done = sem("tap_done")
        conv_done = sem("conv_done")
        bct_done = sem("bct_done")
        g_done = sem("g_done")
        g_masked = sem("g_masked")
        tr_done = sem("tr_done")
        tr_copied = sem("tr_copied")
        block = ctx.enter_context(nc.Block())

        @block.sync
        def _(sp):
            sp.dma_start(w_raw[:], w_bcdt).then_inc(wbc_in, 16)
            for dst, src in ((par, dt_par), (cbc, conv_bc), (mask, mask_in)):
                sp.dma_start(dst[:], src).then_inc(consts_in, 16)
            sp.wait_ge(cs_done, NSEQ)
            sp.dma_start(cs_dram, dtcs[HD:P, :]).then_inc(cs_out, 16)
            sp.wait_ge(cs_out, 16)

        @block.gpsimd
        def _(pool):
            pool.wait_ge(wbc_in, 16)
            pool.tensor_copy(w_hi[:], w_raw[:]).then_inc(w_split, 1)
            pool.wait_ge(w_split, 1)
            pool.tensor_tensor(w_lo[:], w_raw[:], w_hi[:].bitcast(F32), ALU.subtract).then_inc(w_split, 1)
            pool.memset(ones[:], 1.0).then_inc(ones_set, 1)
            pool.memset(acc[:], 0.0).then_inc(ones_set, 1)

        @block.tensor
        def _(pe):
            pe.wait_ge(w_split, 2)
            for n in range(3 * NB):
                m, b = n // NB, n % NB
                if n >= 8:
                    pe.wait_ge(abs_done, n - 7)
                    pe.wait_ge(v_done, n - 7)
                project(pe, bank[n % 8][:], w_hi[:, :, m * P:(m + 1) * P],
                        w_lo[:, :, m * P:(m + 1) * P], xhi, xlo, b).then_inc(proj_done, 1)
            for s in range(NSEQ):
                pe.wait_ge(bct_done, NB + s // SPB + 1)
                if s >= 4:
                    pe.wait_ge(g_masked, s - 3)
                g = bank[4 + s % 4]
                o = s * SEQ
                pe.matmul(g[:, 0:SEQ], bct[:, 0, o:o + P], bct[:, 1, o:o + SEQ],
                          start=True, stop=True)
                pe.matmul(g[:, SEQ:LW], bct[:, 0, o + P:o + SEQ], bct[:, 1, o + P:o + SEQ],
                          start=True, stop=True).then_inc(g_done, 1)
            pe.wait_ge(cs_done, NSEQ)
            pe.wait_ge(dt_done, NB)
            for b in range(NB):
                for t in range(TPB):
                    last = pe.transpose(bank[b][:, t * P:(t + 1) * P],
                                        dtcs[:, (b * TPB + t) * P:(b * TPB + t + 1) * P], ident[:])
                last.then_inc(tr_done, 1)

        @block.scalar
        def _(act):
            act.wait_ge(consts_in, 48)
            for b in range(NB):
                c = slice(b * BLK, (b + 1) * BLK)
                act.wait_ge(proj_done, b + 1)
                act.activation(u[:, c], bank[b][:], ACT.Abs, bias=par[:, 0:1]).then_inc(abs_done, 1)
                act.activation(v[:, c], bank[b][:], ACT.Identity, bias=par[:, 0:1]).then_inc(v_done, 1)
            for b in range(NB):
                c = slice(b * BLK, (b + 1) * BLK)
                act.wait_ge(abs_done, b + 1)
                act.activation(u[:, c], u[:, c], ACT.Exp, scale=-1.0).then_inc(u_done, 1)
            for n in range(2 * NB):
                m, b = n // NB, n % NB
                act.wait_ge(proj_done, NB + n + 1)
                act.activation(bct[:, m, b * BLK:(b + 1) * BLK], bank[(NB + n) % 8][:], ACT.Identity,
                               bias=cbc[:, m, TAPS:TAPS + 1],
                               scale=cbc[:, m, TAPS - 1:TAPS]).then_inc(conv0_done, 1)
            for b in range(NB):
                c = slice(b * BLK, (b + 1) * BLK)
                act.wait_ge(w_done, b + 1)
                act.activation(v_ln[:, c], w[:, c], ACT.Ln).then_inc(ln_done, 1)
            for n in range(2 * NB):
                m, b = n // NB, n % NB
                act.wait_ge(conv_done, n + 1)
                c = bct[:, m, b * BLK:(b + 1) * BLK]
                act.activation(c, c, ACT.Silu).then_inc(bct_done, 1)
            for b in range(NB):
                act.wait_ge(tr_done, b + 1)
                act.copy(tokpar[:, b * TPB:(b + 1) * TPB, :],
                         bank[b][:].rearrange("p (t h) -> p t h", t=TPB)).then_inc(tr_copied, 1)

        @block.vector
        def _(dve):
            for b in range(NB):
                c = slice(b * BLK, (b + 1) * BLK)
                dve.wait_ge(u_done, b + 1)
                dve.tensor_scalar(w[:, c], u[:, c], 1.0, None, ALU.add).then_inc(w_done, 1)
            n_tap = 0
            for n in range(2 * NB):
                m, b = n // NB, n % NB
                dve.wait_ge(conv0_done, n + 1)
                for k in range(1, TAPS):
                    ins = conv_tap(dve, bct[:, m, b * BLK:(b + 1) * BLK], bank[(NB + n) % 8][:],
                                   cbc[:, m, TAPS - 1 - k:TAPS - k], k)
                    if k < TAPS - 1:
                        ins.then_inc(tap_done, 1)
                        n_tap += 1
                        dve.wait_ge(tap_done, n_tap)
                    else:
                        ins.then_inc(conv_done, 1)
            n_sp = 0
            for b in range(NB):
                c = slice(b * BLK, (b + 1) * BLK)
                dve.wait_ge(ln_done, b + 1)
                dve.wait_ge(w_done, b + 1)
                dve.scalar_tensor_tensor(w[:, c], w[:, c], -1.0, u[:, c], ALU.add,
                                         ALU.subtract).then_inc(sp_step, 1)
                n_sp += 1
                dve.wait_ge(sp_step, n_sp)
                dve.tensor_tensor(w[:, c], v_ln[:, c], w[:, c], ALU.subtract).then_inc(sp_step, 1)
                n_sp += 1
                dve.wait_ge(sp_step, n_sp)
                dve.wait_ge(v_done, b + 1)
                dve.scalar_tensor_tensor(w[:, c], v[:, c], 0.0, w[:, c], ALU.max,
                                         ALU.add).then_inc(sp_step, 1)
                n_sp += 1
                dve.wait_ge(sp_step, n_sp)
                dve.tensor_copy(dtcs[0:HD, c], w[0:HD, c]).then_inc(dt_done, 1)
                dve.tensor_scalar(v[HD:P, c], w[HD:P, c], par[HD:P, 1:2], -1.0, ALU.mult,
                                  ALU.mult).then_inc(sp_step, 1)
                n_sp += 1
                dve.wait_ge(sp_step, n_sp)
                if b == 0:
                    dve.wait_ge(ones_set, 1)
                for s in range(b * SPB, (b + 1) * SPB):
                    q = slice(s * SEQ, (s + 1) * SEQ)
                    dve.tensor_tensor_scan(dtcs[HD:P, q], ones[HD:P, :], v[HD:P, q], 0.0,
                                           ALU.mult, ALU.add).then_inc(cs_done, 1)
            for s in range(NSEQ):
                dve.wait_ge(g_done, s + 1)
                dve.tensor_tensor(gmat[:, s, :], bank[4 + s % 4][:, 0:LW], mask[:],
                                  ALU.mult).then_inc(g_masked, 1)


def project(pe, dst, w_hi, w_lo, xhi, xlo, b):
    cols = slice(b * BLK, (b + 1) * BLK)
    passes = [(w, x, k) for k in range(KD) for w, x in ((w_hi, xhi), (w_hi, xlo), (w_lo, xhi))]
    for i, (w, x, k) in enumerate(passes):
        last = pe.matmul(dst, w[:, k, :], x[:, k, cols], start=(i == 0), stop=(i == len(passes) - 1))
    return last


def conv_tap(dve, dst, src, weight, k):
    d = dst.rearrange("p (s t) -> p s t", t=SEQ)
    s = src.rearrange("p (s t) -> p s t", t=SEQ)
    return dve.scalar_tensor_tensor(d[:, :, k:SEQ], s[:, :, 0:SEQ - k], weight, d[:, :, k:SEQ],
                                    ALU.mult, ALU.add)


def wait_past(eng, sem, count):
    if not (isinstance(count, int) and count <= 0):
        eng.wait_ge(sem, count)


Tile = namedtuple('Tile', 'c par pair')


def mix(nc, w_xz, conv_par, d_par, w_out, cs_dram, ident, xhi, xlo, acc, gmat, tokpar):
    with ExitStack() as ctx:
        sb = lambda name, shape, dt=F32: ctx.enter_context(nc.sbuf_tensor("mix_" + name, shape, dt))
        ps = lambda name: ctx.enter_context(nc.psum_tensor("mix_" + name, [P, BLK], F32))
        sem = lambda name: ctx.enter_context(nc.semaphore("mix_" + name))
        wraw = sb("wraw", [P, 2, 2 * KD * P])
        whi = sb("whi", [P, 2, 2 * KD, P], F32R)
        wlo = sb("wlo", [P, 2, 2 * KD, P], F32R)
        conv = sb("conv", [P, 2, TAPS + 1])
        dcol = sb("dcol", [P, 2, 1])
        stok = sb("stok", [P, 2, TILES, HPT])
        srow = sb("srow", [P, 2, HPT, TOK // 2])
        oraw = sb("oraw", [P, 2, DM + 1])
        ohi = sb("ohi", [P, 2, DM], F32R)
        olo = sb("olo", [P, 2, DM], F32R)
        xt = sb("xt", [P, 2, TOK])
        zt = sb("zt", [P, 2, TOK])
        dtx = sb("dtx", [P, 2, TPB, P])
        dec = sb("dec", [P, 2, SPB, HPT, LW])
        yg = sb("yg", [P, NB, BLK])
        sq = sb("sq", [P, 2, BLK])
        sqacc = sb("sqacc", [P, TOK])
        ghi = sb("ghi", [P, 2, TOK], F32R)
        glo = sb("glo", [P, 2, TOK], F32R)
        onesq = sb("onesq", [P, 2])
        mhalf = sb("mhalf", [P, TILES])
        rms = sb("rms", [P, TILES])
        pa = [ps(f"pa{i}") for i in range(2)]
        pt = [ps(f"pt{i}") for i in range(2)]
        py = [ps(f"py{i}") for i in range(2)]
        po = [ps(f"po{i}") for i in range(2)]

        w_in = [sem(f"w_in{i}") for i in range(2)]
        conv_in = [sem(f"conv_in{i}") for i in range(2)]
        d_in = [sem(f"d_in{i}") for i in range(2)]
        srow_in = [sem(f"srow_in{i}") for i in range(2)]
        o_in = sem("o_in")
        w_hi_done = sem("w_hi_done")
        w_split = sem("w_split")
        stok_done = sem("stok_done")
        o_scaled = sem("o_scaled")
        o_hi_done = sem("o_hi_done")
        o_split = sem("o_split")
        px_done = sem("px_done")
        pz_done = sem("pz_done")
        conv0_done = sem("conv0_done")
        tap1_done = sem("tap1_done")
        tap2_done = sem("tap2_done")
        conv_done = sem("conv_done")
        x_done = sem("x_done")
        z_done = sem("z_done")
        xtok_done = sem("xtok_done")
        dtx_done = sem("dtx_done")
        arg_done = sem("arg_done")
        dec_done = sem("dec_done")
        dve_g_done = sem("dve_g_done")
        pool_g_done = sem("pool_g_done")
        y_done = sem("y_done")
        yd_done = sem("yd_done")
        gated = sem("gated")
        ghi_done = sem("ghi_done")
        sq_done = sem("sq_done")
        glo_done = sem("glo_done")
        sq_added = sem("sq_added")
        o_done = sem("o_done")
        o_added = sem("o_added")
        pool_set = sem("pool_set")
        ms_done = sem("ms_done")
        ms_copied = sem("ms_copied")
        rms_done = sem("rms_done")
        scaled = sem("scaled")
        block = ctx.enter_context(nc.Block())

        def pairs(eng, body):
            body(0, True, False)
            body(1, False, False)
            with eng.Fori(2, PAIRS - 1) as q:
                body(q, False, False)
            body(PAIRS - 1, False, True)

        def steps(eng, step):
            def body(q, first, last):
                for e in range(2):
                    now, old = Tile(2 * q + e, e, q), Tile(2 * q + e - 1, 1 - e, q + e - 1)
                    new, next_new = Tile(2 * q + e + 1, 1 - e, q + e), Tile(2 * q + e + 2, e, q + 1)
                    step(q, e, now, old, new, next_new, first, last)

            pairs(eng, body)

        first_tile, second_tile, last_tile = Tile(0, 0, 0), Tile(1, 1, 0), Tile(NCT - 1, 1, PAIRS - 1)

        def cols(b):
            return slice(b * BLK, (b + 1) * BLK)

        @block.sync
        def _(sp):
            def load(c, src, dst, sem):
                sp.dma_start(dst, src[bass.ds(c, 1)].rearrange("o p n -> (o p) n")).then_inc(sem, 16)

            def load_rows(c, half):
                for h in range(HPT):
                    sp.dma_start(srow[:, half, h, :],
                                 cs_dram[bass.ds(HPT * c + h, 1), half * TOK // 2:(half + 1) * TOK // 2]
                                 .partition_broadcast(P)).then_inc(srow_in[half], 16)

            for c in range(2):
                load(c, w_xz, wraw[:, c], w_in[c])
                load(c, conv_par, conv[:, c], conv_in[c])
            load(0, d_par, dcol[:, 0], d_in[0])
            load_rows(0, 0)
            load_rows(0, 1)

            def body(q, first, last):
                wait_past(sp, o_split, 1 * q)
                sp.dma_start(oraw[:], w_out[bass.ds(q, 1)].rearrange("o p e n -> (o p) e n")
                             ).then_inc(o_in, 16)
                for e in range(2):
                    c = 2 * q + e
                    ahead = not (last and e)
                    if not last:
                        sp.wait_ge(w_split, c + 1)
                        load(c + 2, w_xz, wraw[:, e], w_in[e])
                        sp.wait_ge(conv_done, NB * (c + 1))
                        load(c + 2, conv_par, conv[:, e], conv_in[e])
                    if ahead:
                        wait_past(sp, yd_done, NB * c)
                        load(c + 1, d_par, dcol[:, 1 - e], d_in[1 - e])
                        for half in range(2):
                            sp.wait_ge(arg_done, SPB * (NB * c + NB // 2 * (half + 1)))
                            load_rows(c + 1, half)

            pairs(sp, body)

        @block.gpsimd
        def _(pool):
            pool.memset(sqacc[:], 0.0).then_inc(pool_set, 1)
            pool.memset(onesq[:], 1.0).then_inc(pool_set, 1)
            pool.memset(mhalf[:], -0.5).then_inc(pool_set, 1)
            pool.wait_ge(pool_set, 3)

            def w_lo(t):
                pool.wait_ge(w_hi_done, t.c + 1)
                pool.tensor_tensor(wlo[:, t.par].rearrange("p k m -> p (k m)"), wraw[:, t.par],
                                   whi[:, t.par].rearrange("p k m -> p (k m)").bitcast(F32),
                                   ALU.subtract).then_inc(w_split, 1)

            def s_by_tokens(t):
                wait_past(pool, arg_done, SPB * NB * (t.c - 1))
                pool.tensor_copy(stok[:, t.par], tokpar[:, :, bass.ds(NH + HPT * t.c, HPT)]
                                 ).then_inc(stok_done, 1)

            def scale_o(q):
                pool.wait_ge(o_in, 16 * (q + 1))
                pool.tensor_tensor(oraw[:, :, 0:DM], oraw[:, :, 0:DM],
                                   oraw[:, :, DM:DM + 1].broadcast_to([P, 2, DM]),
                                   ALU.mult).then_inc(o_scaled, 1)

            def o_lo(q):
                pool.wait_ge(o_hi_done, 1 * q + 1)
                pool.tensor_tensor(olo[:], oraw[:, :, 0:DM], ohi[:].bitcast(F32),
                                   ALU.subtract).then_inc(o_split, 1)

            def times_g(t, b):
                pool.wait_ge(dec_done, SPB * (NB * t.c + b) + 2)
                d = dec[:, b % 2, 1]
                g = gmat[:, b * SPB + 1, :].unsqueeze(1).broadcast_to([P, HPT, LW])
                pool.tensor_tensor(d, d, g, ALU.mult).then_inc(pool_g_done, 1)

            def gate(t, b):
                n = NB * t.c + b
                pool.wait_ge(yd_done, n + 1)
                pool.wait_ge(z_done, n + 1)
                pool.tensor_tensor(yg[:, b, :], yg[:, b, :], zt[:, t.par, cols(b)],
                                   ALU.mult).then_inc(gated, 1)

            def low(t, b):
                pool.wait_ge(ghi_done, NB * t.c + b + 1)
                pool.tensor_tensor(glo[:, t.par, cols(b)], yg[:, b, :],
                                   ghi[:, t.par, cols(b)].bitcast(F32),
                                   ALU.subtract).then_inc(glo_done, 1)

            def add_square(t, b):
                n = NB * t.c + b
                pool.wait_ge(sq_done, n + 1)
                wait_past(pool, sq_added, n - NB + 1)
                pool.tensor_tensor(sqacc[:, cols(b)], sqacc[:, cols(b)], sq[:, b % 2, :],
                                   ALU.add).then_inc(sq_added, 1)

            w_lo(first_tile)
            w_lo(second_tile)
            s_by_tokens(first_tile)

            def step(q, e, now, old, new, next_new, first, last):
                before = not (first and e == 0)
                ahead = not (last and e == 1)
                if before:
                    gate(old, 1)
                times_g(now, 0)
                if before:
                    low(old, 0)
                    gate(old, 2)
                    gate(old, 3)
                if e == 1:
                    scale_o(q)
                times_g(now, 1)
                if not last:
                    w_lo(next_new)
                if before:
                    low(old, 1)
                    add_square(old, 0)
                    add_square(old, 1)
                times_g(now, 2)
                gate(now, 0)
                if before:
                    add_square(old, 2)
                    add_square(old, 3)
                if ahead:
                    s_by_tokens(new)
                times_g(now, 3)
                if before:
                    low(old, 2)
                    low(old, 3)
                if e == 1:
                    o_lo(q)

            steps(pool, step)
            gate(last_tile, 1)
            low(last_tile, 0)
            gate(last_tile, 2)
            gate(last_tile, 3)
            low(last_tile, 1)
            add_square(last_tile, 0)
            add_square(last_tile, 1)
            add_square(last_tile, 2)
            add_square(last_tile, 3)
            low(last_tile, 2)
            low(last_tile, 3)

            pool.wait_ge(ms_copied, 1)
            pool.tensor_tensor(rms[:], rms[:], mhalf[:], ALU.pow).then_inc(rms_done, 1)

        @block.tensor
        def _(pe):
            def project_x(t, b):
                if b == 0:
                    pe.wait_ge(w_split, t.c + 1)
                if b >= 2:
                    pe.wait_ge(conv_done, NB * t.c + b - 1)
                else:
                    wait_past(pe, z_done, NB * t.c + b - 1)
                project(pe, pa[b % 2][:], whi[:, t.par, 0:KD], wlo[:, t.par, 0:KD], xhi, xlo,
                        b).then_inc(px_done, 1)

            def project_z(t, b):
                if b >= 2:
                    pe.wait_ge(z_done, NB * t.c + b - 1)
                else:
                    pe.wait_ge(conv_done, NB * t.c + b + 3)
                project(pe, pa[b % 2][:], whi[:, t.par, KD:], wlo[:, t.par, KD:], xhi, xlo,
                        b).then_inc(pz_done, 1)

            def tokens(t, b):
                n = NB * t.c + b
                pe.wait_ge(x_done, n + 1)
                wait_past(pe, dtx_done, n - 1)
                for k in range(b * TPB, (b + 1) * TPB):
                    last = pe.transpose(pt[b % 2][:, k % TPB * P:(k % TPB + 1) * P],
                                        xt[:, t.par, k * P:(k + 1) * P], ident[:])
                last.then_inc(xtok_done, 1)

            def outputs(t, b, s):
                n = NB * t.c + b
                if s == 0:
                    pe.wait_ge(dtx_done, n + 1)
                    wait_past(pe, yd_done, n - 1)
                pe.wait_ge(pool_g_done if s else dve_g_done, n + 1)
                o = s * SEQ
                for j, i, m in ((0, slice(o, o + SEQ), slice(0, SEQ)),
                                (1, slice(o + P, o + SEQ), slice(SEQ, LW))):
                    for h in range(HPT):
                        hp = slice(h * HD, (h + 1) * HD)
                        last = pe.matmul(py[b % 2][hp, i], dtx[:, b % 2, 2 * s + j, hp],
                                         dec[:, b % 2, s, h, m], start=(j == 0), stop=(j == 1))
                last.then_inc(y_done, 1)

            def output_rows(q, b, i):
                if i == 0:
                    pe.wait_ge(glo_done, NB * (2 * q + 1) + b + 1)
                    pe.wait_ge(o_split, q + 1)
                wait_past(pe, o_added, 2 * NB * q + 2 * b + i - 1)
                for t in (2 * i, 2 * i + 1):
                    dst = po[i][:, (t % 2) * DM:(t % 2 + 1) * DM]
                    k = slice((b * TPB + t) * P, (b * TPB + t + 1) * P)
                    for e in range(2):
                        pe.matmul(dst, ghi[:, e, k], ohi[:, e, :], start=(e == 0), stop=False)
                        pe.matmul(dst, ghi[:, e, k], olo[:, e, :], start=False, stop=False)
                        last = pe.matmul(dst, glo[:, e, k], ohi[:, e, :], start=False, stop=(e == 1))
                last.then_inc(o_done, 1)

            project_x(first_tile, 0)
            project_x(first_tile, 1)
            project_x(first_tile, 2)
            project_x(first_tile, 3)
            tokens(first_tile, 0)
            project_z(first_tile, 0)
            project_z(first_tile, 1)
            project_z(first_tile, 2)
            tokens(first_tile, 1)

            def step(q, e, now, old, new, next_new, first, last):
                before = not (first and e == 0)
                ahead = not (last and e == 1)
                if ahead:
                    project_x(new, 0)
                project_z(now, 3)
                if e == 1 and not first:
                    output_rows(q - 1, 1, 1)
                    output_rows(q - 1, 2, 0)
                outputs(now, 0, 0)
                if ahead:
                    project_x(new, 1)
                outputs(now, 0, 1)
                outputs(now, 1, 0)
                tokens(now, 2)
                if e == 1 and not first:
                    output_rows(q - 1, 2, 1)
                if ahead:
                    project_x(new, 2)
                if e == 0 and not first:
                    output_rows(q - 1, 0, 0)
                    output_rows(q - 1, 0, 1)
                if e == 1 and not first:
                    output_rows(q - 1, 3, 0)
                outputs(now, 1, 1)
                if ahead:
                    project_x(new, 3)
                if e == 1 and not first:
                    output_rows(q - 1, 3, 1)
                tokens(now, 3)
                if ahead:
                    tokens(new, 0)
                if e == 0 and not first:
                    output_rows(q - 1, 1, 0)
                outputs(now, 2, 0)
                if ahead:
                    project_z(new, 0)
                outputs(now, 2, 1)
                if ahead:
                    project_z(new, 1)
                    project_z(new, 2)
                outputs(now, 3, 0)
                outputs(now, 3, 1)
                if ahead:
                    tokens(new, 1)

            steps(pe, step)
            output_rows(PAIRS - 1, 0, 0)
            output_rows(PAIRS - 1, 0, 1)
            output_rows(PAIRS - 1, 1, 0)
            output_rows(PAIRS - 1, 1, 1)
            output_rows(PAIRS - 1, 2, 0)
            output_rows(PAIRS - 1, 2, 1)
            output_rows(PAIRS - 1, 3, 0)
            output_rows(PAIRS - 1, 3, 1)
            pe.wait_ge(sq_added, NB * NCT)
            for t in range(TILES):
                last = pe.matmul(pt[0][:, t:t + 1], sqacc[:, t * P:(t + 1) * P], onesq[:, 0:1],
                                 start=True, stop=True)
            last.then_inc(ms_done, 1)

        @block.scalar
        def _(act):
            def w_hi(t):
                act.wait_ge(w_in[t.par], 16 * (t.pair + 1))
                wait_past(act, pz_done, NB * (t.c - 1))
                act.copy(whi[:, t.par].rearrange("p k m -> p (k m)"), wraw[:, t.par]
                         ).then_inc(w_hi_done, 1)

            def conv0(t, b):
                n = NB * t.c + b
                if b == 0:
                    act.wait_ge(conv_in[t.par], 16 * (t.pair + 1))
                act.wait_ge(px_done, n + 1)
                wait_past(act, yd_done, n - 2 * NB + 1)
                act.activation(xt[:, t.par, cols(b)], pa[b % 2][:], ACT.Identity,
                               bias=conv[:, t.par, TAPS:TAPS + 1],
                               scale=conv[:, t.par, TAPS - 1:TAPS]).then_inc(conv0_done, 1)

            def silu_x(t, b):
                act.wait_ge(conv_done, NB * t.c + b + 1)
                act.activation(xt[:, t.par, cols(b)], xt[:, t.par, cols(b)],
                               ACT.Silu).then_inc(x_done, 1)

            def silu_z(t, b):
                act.wait_ge(pz_done, NB * t.c + b + 1)
                wait_past(act, gated, NB * (t.c - 2) + b + 1)
                act.activation(zt[:, t.par, cols(b)], pa[b % 2][:], ACT.Silu).then_inc(z_done, 1)

            def decays(t, b, s):
                act.wait_ge(arg_done, SPB * (NB * t.c + b) + s + 1)
                d = dec[:, b % 2, s].rearrange("p h i -> p (h i)")
                act.activation(d, d, ACT.Exp, scale=-1.0).then_inc(dec_done, 1)

            def high(t, b):
                act.wait_ge(gated, NB * t.c + b + 1)
                wait_past(act, o_done, 2 * NB * (t.pair - 1) + 2 * (b + 1))
                act.copy(ghi[:, t.par, cols(b)], yg[:, b, :]).then_inc(ghi_done, 1)

            def square(t, b):
                n = NB * t.c + b
                act.wait_ge(gated, n + 1)
                wait_past(act, sq_added, n - 1)
                act.activation(sq[:, b % 2, :], yg[:, b, :], ACT.Square).then_inc(sq_done, 1)

            def o_hi(q):
                wait_past(act, o_done, 2 * NB * q)
                act.wait_ge(o_scaled, q + 1)
                act.copy(ohi[:], oraw[:, :, 0:DM]).then_inc(o_hi_done, 1)

            w_hi(first_tile)
            conv0(first_tile, 0)
            conv0(first_tile, 1)
            w_hi(second_tile)
            silu_x(first_tile, 0)
            conv0(first_tile, 2)
            conv0(first_tile, 3)
            silu_x(first_tile, 1)
            silu_x(first_tile, 2)
            silu_z(first_tile, 0)
            silu_x(first_tile, 3)
            silu_z(first_tile, 1)
            silu_z(first_tile, 2)
            decays(first_tile, 0, 0)
            decays(first_tile, 0, 1)
            decays(first_tile, 1, 0)

            def step(q, e, now, old, new, next_new, first, last):
                before = not (first and e == 0)
                ahead = not (last and e == 1)
                if ahead:
                    conv0(new, 0)
                silu_z(now, 3)
                if before:
                    high(old, 1)
                decays(now, 1, 1)
                if ahead:
                    conv0(new, 1)
                if not last:
                    w_hi(next_new)
                if before:
                    square(old, 1)
                decays(now, 2, 0)
                if ahead:
                    silu_x(new, 0)
                    conv0(new, 2)
                decays(now, 2, 1)
                decays(now, 3, 0)
                if ahead:
                    conv0(new, 3)
                if before:
                    square(old, 2)
                    square(old, 3)
                decays(now, 3, 1)
                if ahead:
                    silu_x(new, 1)
                    silu_x(new, 2)
                if before:
                    high(old, 2)
                    high(old, 3)
                if ahead:
                    silu_z(new, 0)
                    silu_x(new, 3)
                high(now, 0)
                if e == 1:
                    o_hi(q)
                square(now, 0)
                if ahead:
                    silu_z(new, 1)
                    silu_z(new, 2)
                    decays(new, 0, 0)
                    decays(new, 0, 1)
                    decays(new, 1, 0)

            steps(act, step)
            high(last_tile, 1)
            square(last_tile, 1)
            square(last_tile, 2)
            square(last_tile, 3)
            high(last_tile, 2)
            high(last_tile, 3)

            act.wait_ge(rms_done, 1)
            act.wait_ge(o_added, NB * NCT)
            for t in range(TILES):
                act.activation(acc[:, t, :], acc[:, t, :], ACT.Identity,
                               scale=rms[:, t:t + 1]).then_inc(scaled, 1)

        @block.vector
        def _(dve):
            def tap(t, b, k):
                before, done = [(conv0_done, tap1_done), (tap1_done, tap2_done),
                                (tap2_done, conv_done)][k - 1]
                dve.wait_ge(before, NB * t.c + b + 1)
                conv_tap(dve, xt[:, t.par, cols(b)], pa[b % 2][:],
                         conv[:, t.par, TAPS - 1 - k:TAPS - k], k).then_inc(done, 1)

            def dt_x(t, b):
                n = NB * t.c + b
                dve.wait_ge(xtok_done, n + 1)
                wait_past(dve, y_done, SPB * (n - 1))
                dt = tokpar[:, b * TPB:(b + 1) * TPB, bass.ds(HPT * t.c, HPT)]
                dve.tensor_tensor(dtx[:, b % 2].rearrange("p t (h d) -> p t h d", h=HPT),
                                  pt[b % 2][:].rearrange("p (t h d) -> p t h d", t=TPB, h=HPT),
                                  dt.unsqueeze(3).broadcast_to([P, TPB, HPT, HD]),
                                  ALU.mult).then_inc(dtx_done, 1)

            def exponents(t, b, s):
                m = SPB * (NB * t.c + b) + s
                half, i0 = b // 2, b % 2 * BLK + s * SEQ
                if b == 0 and s == 0:
                    dve.wait_ge(stok_done, t.c + 1)
                if b % 2 == 0 and s == 0:
                    dve.wait_ge(srow_in[half], 16 * HPT * (t.c + 1))
                wait_past(dve, y_done, m - 2 * SPB + 1)
                for h in range(HPT):
                    for j, i, k in ((0, slice(i0, i0 + SEQ), slice(0, SEQ)),
                                    (1, slice(i0 + P, i0 + SEQ), slice(SEQ, LW))):
                        tile = b * TPB + 2 * s + j
                        last = dve.tensor_scalar(dec[:, b % 2, s, h, k], srow[:, half, h, i],
                                                 stok[:, t.par, tile, h:h + 1], -CAP,
                                                 ALU.subtract, ALU.max)
                last.then_inc(arg_done, 1)

            def times_g(t, b):
                dve.wait_ge(dec_done, SPB * (NB * t.c + b) + 1)
                d = dec[:, b % 2, 0]
                g = gmat[:, b * SPB, :].unsqueeze(1).broadcast_to([P, HPT, LW])
                dve.tensor_tensor(d, d, g, ALU.mult).then_inc(dve_g_done, 1)

            def add_dx(t, b):
                n = NB * t.c + b
                if b == 0:
                    dve.wait_ge(d_in[t.par], 16 * (t.pair + 1))
                dve.wait_ge(y_done, SPB * (n + 1))
                wait_past(dve, sq_done, n - NB + 1)
                wait_past(dve, glo_done, n - NB + 1)
                dve.scalar_tensor_tensor(yg[:, b, :], xt[:, t.par, cols(b)], dcol[:, t.par],
                                         py[b % 2][:], ALU.mult, ALU.add).then_inc(yd_done, 1)

            def add_rows(q, b, i):
                m = 2 * NB * q + 2 * b + i
                dve.wait_ge(o_done, m + 1)
                wait_past(dve, o_added, m - 2 * NB + 1 if isinstance(m, int) else m - 1)
                rows = acc[:, b * TPB + 2 * i:b * TPB + 2 * i + 2, :].rearrange("p t d -> p (t d)")
                dve.tensor_tensor(rows, po[i][:], rows, ALU.add).then_inc(o_added, 1)

            tap(first_tile, 0, 1)
            tap(first_tile, 0, 2)
            tap(first_tile, 0, 3)
            tap(first_tile, 1, 1)
            tap(first_tile, 1, 2)
            tap(first_tile, 1, 3)
            tap(first_tile, 2, 1)
            tap(first_tile, 2, 2)
            tap(first_tile, 3, 1)
            tap(first_tile, 2, 3)
            tap(first_tile, 3, 2)
            tap(first_tile, 3, 3)
            exponents(first_tile, 0, 0)
            dt_x(first_tile, 0)
            exponents(first_tile, 0, 1)
            exponents(first_tile, 1, 0)
            exponents(first_tile, 1, 1)
            dt_x(first_tile, 1)
            times_g(first_tile, 0)

            def step(q, e, now, old, new, next_new, first, last):
                before = not (first and e == 0)
                ahead = not (last and e == 1)
                if ahead:
                    tap(new, 0, 1)
                times_g(now, 1)
                if e == 1 and not first:
                    add_rows(q - 1, 1, 1)
                    add_rows(q - 1, 2, 0)
                if ahead:
                    tap(new, 0, 2)
                exponents(now, 2, 0)
                if ahead:
                    tap(new, 0, 3)
                add_dx(now, 0)
                if ahead:
                    tap(new, 1, 1)
                exponents(now, 2, 1)
                if ahead:
                    tap(new, 1, 2)
                exponents(now, 3, 0)
                if ahead:
                    tap(new, 1, 3)
                dt_x(now, 2)
                if ahead:
                    tap(new, 2, 1)
                if e == 1 and not first:
                    add_rows(q - 1, 2, 1)
                exponents(now, 3, 1)
                if e == 0 and not first:
                    add_rows(q - 1, 0, 0)
                if ahead:
                    tap(new, 2, 2)
                times_g(now, 2)
                if ahead:
                    tap(new, 3, 1)
                    tap(new, 2, 3)
                    tap(new, 3, 2)
                add_dx(now, 1)
                if ahead:
                    tap(new, 3, 3)
                dt_x(now, 3)
                times_g(now, 3)
                if e == 0 and not first:
                    add_rows(q - 1, 0, 1)
                if ahead:
                    exponents(new, 0, 0)
                if e == 1 and not first:
                    add_rows(q - 1, 3, 0)
                if ahead:
                    dt_x(new, 0)
                    exponents(new, 0, 1)
                if e == 1 and not first:
                    add_rows(q - 1, 3, 1)
                if e == 0 and not first:
                    add_rows(q - 1, 1, 0)
                if ahead:
                    exponents(new, 1, 0)
                    exponents(new, 1, 1)
                add_dx(now, 2)
                if ahead:
                    dt_x(new, 1)
                add_dx(now, 3)
                if ahead:
                    times_g(new, 0)

            steps(dve, step)
            add_rows(PAIRS - 1, 0, 0)
            add_rows(PAIRS - 1, 0, 1)
            add_rows(PAIRS - 1, 1, 0)
            add_rows(PAIRS - 1, 1, 1)
            add_rows(PAIRS - 1, 2, 0)
            add_rows(PAIRS - 1, 2, 1)
            add_rows(PAIRS - 1, 3, 0)
            add_rows(PAIRS - 1, 3, 1)
            dve.wait_ge(ms_done, 1)
            dve.tensor_scalar(rms[:], pt[0][:, 0:TILES], 1.0 / DI, EPS, ALU.mult,
                              ALU.add).then_inc(ms_copied, 1)


def mlp(nc, hidden, xn_dram, w1, w2, b2, ln_g, ln_b, ln_cols, ident, xhi, xlo, acc, out, tiled):
    with ExitStack() as ctx:
        sb = lambda name, shape, dt=F32: ctx.enter_context(nc.sbuf_tensor("mlp_" + name, shape, dt))
        ps = lambda name: ctx.enter_context(nc.psum_tensor("mlp_" + name, [P, BLK], F32))
        sem = lambda name: ctx.enter_context(nc.semaphore("mlp_" + name))
        res = sb("res", [P, TILES, DM])
        w1raw = sb("w1raw", [P, KD * HID + KH])
        w1hi = sb("w1hi", [P, KD, HID], F32R)
        w1lo = sb("w1lo", [P, KD, HID], F32R)
        w2raw = sb("w2raw", [P, KH, DM])
        w2hi = sb("w2hi", [P, KH, DM], F32R)
        w2lo = sb("w2lo", [P, KH, DM], F32R)
        b1c = sb("b1c", [P, KH])
        gbc = sb("gbc", [P, (NL - 1) * 2 * KD])
        grow = sb("grow", [P, 3, DM])
        h = sb("h", [P, 4, BLK])
        hhi = sb("hhi", [P, KH, BLK], F32R)
        hlo = sb("hlo", [P, KH, BLK], F32R)
        u = sb("u2", [P, 2, TPB, DM])
        xf = sb("xf", [P, KD, BLK])
        stats = sb("stats2", [P, TPB, 6])
        mv = sb("mv2", [P, TPB, 2])
        vare = sb("vare2", [P, TPB])
        rstd = sb("rstd2", [P, TPB])
        mhalf = sb("mhalf2", [P, TPB])
        hidt = sb("hidt", [P, TPB, DM])
        p1 = [ps(f"p1{i}") for i in range(2)]
        p2 = [ps(f"p2{i}") for i in range(4)]
        p3 = [ps(f"p3{i}") for i in range(2)]

        const_in = sem("const_in2")
        res_in = sem("res_in")
        w1_in = sem("w1_in")
        w2_in = sem("w2_in")
        w1_hi_done = sem("w1_hi_done")
        w1_split = sem("w1_split")
        b1_done = sem("b1_done")
        w2_hi_done = sem("w2_hi_done")
        w2_split = sem("w2_split")
        grow_in = sem("grow_in")
        brow_done = sem("brow_done")
        first_done = sem("first_done")
        gelu_done = sem("gelu_done")
        hhi_done = sem("hhi_done")
        hlo_done = sem("hlo_done")
        second_done = sem("second_done")
        u_done = sem("u_done2")
        stats_done = sem("stats_done2")
        stats_seen = sem("stats_seen")
        mv_done = sem("mv_done2")
        vare_done = sem("vare_done2")
        rstd_done = sem("rstd_done2")
        norm_done = sem("norm_done2")
        tr_done = sem("tr_done2")
        xf_done = sem("xf_done")
        xhi_done = sem("xhi_done")
        xlo_done = sem("xlo_done")
        scaled_done = sem("scaled_done")
        res_done = sem("res_done")
        pool_set = sem("pool_set2")
        hid_in = sem("hid_in2")
        mixed = sem("mixed")
        final = sem("final")
        out_done = sem("out_done")
        block = ctx.enter_context(nc.Block())

        w1tiles = w1raw[:, 0:KD * HID].rearrange("p (k m) -> p k m", k=KD)

        def layers(eng, body):
            body(0, True, False)
            with eng.Fori(1, NL - 1) as l:
                body(l, False, False)
            body(NL - 1, False, True)

        @block.sync
        def _(sp):
            sp.dma_start(w1raw[:], w1[0]).then_inc(w1_in, 16)
            sp.dma_start(w2raw[:], w2[0]).then_inc(w2_in, 16)
            sp.dma_start(gbc[:], ln_cols).then_inc(const_in, 16)
            sp.dma_start(res[:], tiled(xn_dram)).then_inc(res_in, 16)
            sp.dma_start(grow[:, 2, :], b2[0:1, :].partition_broadcast(P)).then_inc(grow_in, 16)

            def body(l, first, last):
                if last:
                    return
                sp.wait_ge(w2_split, KH * l + KH)
                sp.dma_start(w1raw[:], w1[bass.ds(l + 1, 1)].rearrange("o p n -> (o p) n")
                             ).then_inc(w1_in, 16)
                if first:
                    sp.wait_ge(res_done, NB)
                else:
                    sp.wait_ge(res_done, NB * l + NB)
                for i, row in enumerate((ln_g[bass.ds(l, 1), :], ln_b[bass.ds(l, 1), :],
                                         b2[bass.ds(l + 1, 1), :])):
                    sp.dma_start(grow[:, i, :], row.partition_broadcast(P)).then_inc(grow_in, 16)
                sp.dma_start(w2raw[:], w2[bass.ds(l + 1, 1)].rearrange("o p k m -> (o p) k m")
                             ).then_inc(w2_in, 16)

            layers(sp, body)
            for b in range(NB):
                if b:
                    sp.wait_ge(mixed, b)
                sp.dma_start(hidt[:], tiled(hidden)[:, b * TPB:(b + 1) * TPB, :]).then_inc(hid_in, 16)
            for b in range(NB):
                sp.wait_ge(final, TPB * (b + 1))
                sp.dma_start(tiled(out)[:, b * TPB:(b + 1) * TPB, :],
                             acc[:, b * TPB:(b + 1) * TPB, :]).then_inc(out_done, 16)
            sp.wait_ge(out_done, 16 * NB)

        @block.gpsimd
        def _(pool):
            def w1_lo(l, j):
                pool.wait_ge(w1_hi_done, KH * l + j + 1)
                hj = slice(j * P, (j + 1) * P)
                pool.tensor_tensor(w1lo[:, :, hj], w1tiles[:, :, hj], w1hi[:, :, hj].bitcast(F32),
                                   ALU.subtract).then_inc(w1_split, 1)

            def w2_lo(l, j):
                pool.wait_ge(w2_hi_done, KH * l + j + 1)
                pool.tensor_tensor(w2lo[:, j, :], w2raw[:, j, :], w2hi[:, j, :].bitcast(F32),
                                   ALU.subtract).then_inc(w2_split, 1)

            def inverse_deviation(l, b):
                pool.wait_ge(vare_done, NB * l + b + 1)
                pool.tensor_tensor(rstd[:], vare[:], mhalf[:], ALU.pow
                                   ).then_inc(rstd_done, 1)

            def residual(l, b):
                n = NB * l + b
                r = res[:, b * TPB:(b + 1) * TPB, :]
                rows = lambda i: grow[:, i, :].unsqueeze(1).broadcast_to([P, TPB, DM])
                pool.wait_ge(norm_done, TPB * (n + 1))
                pool.tensor_tensor(r, u[:, b % 2], rows(0), ALU.mult).then_inc(scaled_done, 1)
                pool.wait_ge(scaled_done, n + 1)
                pool.tensor_tensor(r, r, rows(1), ALU.add).then_inc(res_done, 1)

            pool.memset(mhalf[:], -0.5).then_inc(pool_set, 1)
            for j in range(KH):
                w1_lo(0, j)
            for j in range(KH):
                w2_lo(0, j)
            pool.wait_ge(res_in, 16)
            pool.wait_ge(grow_in, 16)
            for b in range(NB):
                r = res[:, b * TPB:(b + 1) * TPB, :]
                pool.tensor_tensor(r, r, grow[:, 2, :].unsqueeze(1).broadcast_to([P, TPB, DM]),
                                   ALU.add).then_inc(res_done, 1)
            pool.wait_ge(pool_set, 1)

            def body(l, first, last):
                if not first:
                    inverse_deviation(l - 1, NB - 1)
                    residual(l - 1, NB - 1)
                if last:
                    for b in range(NB):
                        a = acc[:, b * TPB:(b + 1) * TPB, :]
                        pool.wait_ge(hid_in, 16 * (b + 1))
                        pool.tensor_tensor(a, a, hidt[:], ALU.add).then_inc(mixed, 1)
                    return
                pool.wait_ge(grow_in, 48 * l + 64)
                pool.tensor_tensor(grow[:, 1, :], grow[:, 1, :], grow[:, 2, :],
                                   ALU.add).then_inc(brow_done, 1)
                pool.wait_ge(brow_done, 1 * l + 1)
                for b in range(1, NB):
                    inverse_deviation(l, b - 1)
                    residual(l, b - 1)
                    for j in range(KH):
                        if b == 2:
                            w1_lo(l + 1, j)
                        if b == 3:
                            w2_lo(l + 1, j)

            layers(pool, body)

        @block.tensor
        def _(pe):
            def first_product(l, b, j, first):
                n = NB * l + b
                if b == 0:
                    pe.wait_ge(w1_split, KH * l + j + 1)
                if j == 0 and not first:
                    pe.wait_ge(xlo_done, KD * (n - NB + 1))
                if not (first and b == 0 and j < 2):
                    pe.wait_ge(gelu_done, KH * n + j - 1)
                hj = slice(j * P, (j + 1) * P)
                project(pe, p1[j % 2][:], w1hi[:, :, hj], w1lo[:, :, hj], xhi, xlo,
                        b).then_inc(first_done, 1)

            def transposes(l, b, first):
                n = NB * l + b
                pe.wait_ge(norm_done, TPB * (n + 1))
                if not (first and b == 0):
                    pe.wait_ge(xf_done, KD * n)
                for k in range(KD):
                    for t in range(TPB):
                        last = pe.transpose(p3[k][:, t * P:(t + 1) * P],
                                            u[:, b % 2, t, k * P:(k + 1) * P], ident[:])
                    last.then_inc(tr_done, 1)

            def second_product(l, b, j, first):
                n = NB * l + b
                if b == 0:
                    pe.wait_ge(w2_split, KH * l + j + 1)
                pe.wait_ge(hlo_done, KH * n + j + 1)
                for t in range(TPB):
                    if j == 0 and not (first and b == 0):
                        pe.wait_ge(u_done, TPB * (n - 1) + t + 1)
                    dst = p2[t][:, 0:DM]
                    k = slice(t * P, (t + 1) * P)
                    pe.matmul(dst, hhi[:, j, k], w2hi[:, j, :], start=(j == 0), stop=False)
                    pe.matmul(dst, hhi[:, j, k], w2lo[:, j, :], start=False, stop=False)
                    last = pe.matmul(dst, hlo[:, j, k], w2hi[:, j, :], start=False,
                                     stop=(j == KH - 1))
                last.then_inc(second_done, 1)

            for j in range(KH):
                first_product(0, 0, j, True)

            def body(l, first, last):
                for b in range(NB):
                    for j in range(KH):
                        second_product(l, b, j, first)
                        if b < NB - 1:
                            first_product(l, b + 1, j, first)
                        elif not last:
                            first_product(l + 1, 0, j, False)
                        if j == 3:
                            if b == 0:
                                if not first:
                                    transposes(l - 1, NB - 1, False)
                            elif not last:
                                transposes(l, b - 1, first)

            layers(pe, body)

        @block.scalar
        def _(act):
            def hidden_tile(l, b, j, first):
                n = NB * l + b
                m = KH * n + j
                act.wait_ge(first_done, m + 1)
                if not (first and b == 0 and j < 4):
                    act.wait_ge(hlo_done, m - 3)
                act.activation(h[:, j % 4, :], p1[j % 2][:], ACT.Gelu,
                               bias=b1c[:, j:j + 1]).then_inc(gelu_done, 1)
                act.wait_ge(gelu_done, m + 1)
                if not (first and b == 0):
                    act.wait_ge(second_done, m - KH + 1)
                act.copy(hhi[:, j, :], h[:, j % 4, :]).then_inc(hhi_done, 1)

            def x_hi(l, b):
                n = NB * l + b
                for k in range(KD):
                    act.wait_ge(xf_done, KD * n + k + 1)
                    act.copy(xhi[:, k, b * BLK:(b + 1) * BLK], xf[:, k, :]).then_inc(xhi_done, 1)

            def w1_hi(l, j):
                hj = slice(j * P, (j + 1) * P)
                act.copy(w1hi[:, :, hj], w1tiles[:, :, hj]).then_inc(w1_hi_done, 1)

            def w2_hi(l, j):
                act.copy(w2hi[:, j, :], w2raw[:, j, :]).then_inc(w2_hi_done, 1)

            def biases(l):
                act.copy(b1c[:], w1raw[:, KD * HID:]).then_inc(b1_done, 1)
                act.wait_ge(b1_done, 1 * l + 1)

            act.wait_ge(w1_in, 16)
            biases(0)
            for j in range(KH):
                w1_hi(0, j)
            act.wait_ge(w2_in, 16)
            for j in range(KH):
                hidden_tile(0, 0, j, True)
                w2_hi(0, j)

            def body(l, first, last):
                for b in range(NB):
                    if b == 2 and not last:
                        act.wait_ge(w1_in, 16 * (l + 2))
                    if b == 3 and not last:
                        act.wait_ge(w2_in, 16 * (l + 2))
                        act.wait_ge(gelu_done, KH * NB * (l + 1))
                        biases(l + 1)
                    for j in range(KH):
                        if b < NB - 1:
                            hidden_tile(l, b + 1, j, first)
                        elif not last:
                            hidden_tile(l + 1, 0, j, False)
                        if b == 2 and not last:
                            w1_hi(l + 1, j)
                        if b == 3 and not last:
                            act.wait_ge(second_done, KH * (NB * l + b) + j + 1)
                            w2_hi(l + 1, j)
                        if j == 3:
                            if b == 0:
                                if not first:
                                    x_hi(l - 1, NB - 1)
                            elif not last:
                                x_hi(l, b - 1)

            layers(act, body)

        @block.vector
        def _(dve):
            def h_lo(l, b, j):
                dve.wait_ge(hhi_done, KH * (NB * l + b) + j + 1)
                dve.tensor_tensor(hlo[:, j, :], h[:, j % 4, :], hhi[:, j, :].bitcast(F32),
                                  ALU.subtract).then_inc(hlo_done, 1)

            def sums(l, b, first):
                n = NB * l + b
                dve.wait_ge(res_done, n + 1)
                if not (first and b < 2):
                    dve.wait_ge(tr_done, KD * (n - 1))
                    dve.wait_ge(res_done, NB + n - 1)
                dve.wait_ge(second_done, KH * (n + 1))
                for t in range(TPB):
                    dve.tensor_tensor(u[:, b % 2, t, :], p2[t][:, 0:DM], res[:, b * TPB + t, :],
                                      ALU.add).then_inc(u_done, 1)

            def variances(l, b):
                n = NB * l + b
                for t in range(TPB):
                    dve.wait_ge(u_done, TPB * n + t + 1)
                    dve.bn_stats(stats[:, t, :], u[:, b % 2, t, :]).then_inc(stats_done, 1)
                dve.wait_ge(stats_done, TPB * (n + 1))
                dve.sem_inc(stats_seen, 1)
                for t in range(TPB):
                    dve.bn_aggr(mv[:, t, :], stats[:, t, :]).then_inc(mv_done, 1)
                dve.wait_ge(mv_done, TPB * (n + 1))
                dve.tensor_scalar(vare[:], mv[:, :, 1], EPS, None, ALU.add).then_inc(vare_done, 1)

            def normalised(l, b):
                dve.wait_ge(rstd_done, NB * l + b + 1)
                for t in range(TPB):
                    dve.tensor_scalar(u[:, b % 2, t, :], u[:, b % 2, t, :], mv[:, t, 0:1],
                                      rstd[:, t:t + 1], ALU.subtract, ALU.mult).then_inc(norm_done, 1)

            def x_full(l, b, first):
                n = NB * l + b
                for k in range(KD):
                    dve.wait_ge(tr_done, KD * n + k + 1)
                    if not (first and b == 0):
                        dve.wait_ge(xlo_done, KD * n - KD + k + 1)
                        dve.wait_ge(xhi_done, KD * n - KD + k + 1)
                    dve.tensor_scalar(xf[:, k, :], p3[k][:], gbc[:, bass.ds(2 * KD * l + k, 1)],
                                      gbc[:, bass.ds(2 * KD * l + KD + k, 1)], ALU.mult,
                                      ALU.add).then_inc(xf_done, 1)

            def x_lo(l, b):
                n = NB * l + b
                for k in range(KD):
                    dve.wait_ge(xhi_done, KD * n + k + 1)
                    dve.tensor_tensor(xlo[:, k, b * BLK:(b + 1) * BLK], xf[:, k, :],
                                      xhi[:, k, b * BLK:(b + 1) * BLK].bitcast(F32),
                                      ALU.subtract).then_inc(xlo_done, 1)

            def last_sums(b):
                n = NB * (NL - 1) + b
                dve.wait_ge(res_done, n + 1)
                dve.wait_ge(mixed, b + 1)
                dve.wait_ge(second_done, KH * (n + 1))
                tiles = [(res[:, b * TPB + t, :], acc[:, b * TPB + t, :]) for t in range(TPB)]
                for t, (r, a) in enumerate(tiles):
                    dve.tensor_tensor(r, p2[t][:, 0:DM], r, ALU.add).then_inc(u_done, 1)
                for t, (r, a) in enumerate(tiles):
                    dve.wait_ge(u_done, TPB * n + t + 1)
                    dve.tensor_tensor(a, a, r, ALU.add).then_inc(final, 1)

            dve.wait_ge(const_in, 16)
            for j in range(KH - 1):
                h_lo(0, 0, j)

            def body(l, first, last):
                for b in range(NB):
                    before = None
                    if b == 0 and not first:
                        before = (l - 1, NB - 1)
                    elif b > 0 and not last:
                        before = (l, b - 1)
                    if before:
                        sums(*before, first)
                    elif last:
                        last_sums(b - 1)
                    h_lo(l, b, KH - 1)
                    if before:
                        variances(*before)
                    for j in range(KH - 1):
                        if b < NB - 1:
                            h_lo(l, b + 1, j)
                        elif not last:
                            h_lo(l + 1, 0, j)
                        if before and j == 0:
                            normalised(*before)
                        if before and j == 3:
                            x_full(*before, first)
                        if before and j == 4:
                            x_lo(*before)

            layers(dve, body)
            last_sums(NB - 1)


def kernel(**inputs):
    import numpy as np
    import concourse.bacc as bacc
    from concourse.bass_utils import run_bass_kernel_spmd

    a = {k: np.asarray(v) for k, v in inputs.items()}

    def cols(x, n):
        return np.moveaxis(x.reshape(n, P, *x.shape[1:]), 0, 1)

    w_in = cols(a["L0_attn_W_in"], KD)
    z, x, bc, dt = np.split(w_in, [DI, 2 * DI, 2 * DI + 2 * P], axis=2)
    xz = np.concatenate([x.reshape(P, KD, NCT, P), z.reshape(P, KD, NCT, P)], axis=1)
    conv = np.concatenate([a["L0_attn_conv_w"], a["L0_attn_conv_b"][:, None]], axis=1)
    conv = conv.reshape(NCT + 2, P, TAPS + 1)
    w1 = a["L0_ffn_W1"].transpose(0, 2, 1).reshape(NL, KD, P, HID).transpose(0, 2, 1, 3)
    b1 = a["L0_ffn_B1"].reshape(NL, KH, P).transpose(0, 2, 1)
    rows = np.arange(P)
    upper = (rows[None, :] >= rows[:, None]).astype(np.float32)
    ln_cols = np.stack([a["L0_ffn_LN_G"].reshape(NL - 1, KD, P), a["L0_ffn_LN_B"].reshape(NL - 1, KD, P)],
                       axis=1)
    arrays = dict(
        hidden=a["L0_attn_hidden_states"].reshape(TOK, DM),
        w_bcdt=np.concatenate([dt, dt, bc], axis=2),
        w_xz=xz.transpose(2, 0, 1, 3).reshape(NCT, P, 2 * KD * P),
        conv_par=conv[:NCT],
        d_par=np.repeat(a["L0_attn_D"], HD).reshape(NCT, P, 1),
        conv_bc=np.moveaxis(conv[NCT:], 0, 1),
        dt_par=np.stack([np.tile(a["L0_attn_dt_bias"], 2), np.tile(a["L0_attn_A"], 2)], axis=1),
        w_out=np.concatenate([a["L0_attn_W_out"], a["L0_attn_norm_w"][:, None]], axis=1)
        .reshape(NCT // 2, 2, P, DM + 1).transpose(0, 2, 1, 3),
        w1=np.concatenate([w1.reshape(NL, P, KD * HID), b1], axis=2),
        w2=a["L0_ffn_W2"].transpose(0, 2, 1).reshape(NL, KH, P, DM).transpose(0, 2, 1, 3),
        b2=a["L0_ffn_B2"],
        ln_g=a["L0_ffn_LN_G"],
        ln_b=a["L0_ffn_LN_B"],
        ln_cols=np.moveaxis(ln_cols, 3, 0).reshape(P, -1),
        ident_in=np.eye(P, dtype=np.float32),
        mask_in=np.concatenate([upper, np.ones((P, P), np.float32), upper], axis=1),
    )
    arrays = {k: np.ascontiguousarray(v) for k, v in arrays.items()}
    nc = bacc.Bacc("TRN2", target_bir_lowering=False, num_devices=1)
    args = {k: nc.dram_tensor(k, v.shape, mybir.dt.from_np(v.dtype), kind="ExternalInput").ap()
            for k, v in arrays.items()}
    shape = a["L0_attn_hidden_states"].shape
    result = nc.dram_tensor("result", (TOK, DM), F32, kind="ExternalOutput").ap()
    build(nc, out=result, **args)
    r = run_bass_kernel_spmd(nc, [arrays], core_ids=[0])
    return r.results[0]["result"].reshape(shape)
```

```python
from collections import namedtuple
from contextlib import ExitStack

import concourse.bass as bass
from concourse import mybir

F32 = mybir.dt.float32
F32R = mybir.dt.float32r
ALU = mybir.AluOpType
ACT = mybir.ActivationFunctionType

P = 128
SEQ = 256
NSEQ = 8
TOK = NSEQ * SEQ
TILES = TOK // P
DM = 256
KD = DM // P
DI = 4096
NCT = DI // P
PAIRS = NCT // 2
HD = 64
HPT = P // HD
NH = DI // HD
TAPS = 4
BLK = 512
NB = TOK // BLK
TPB = BLK // P
SPB = BLK // SEQ
LW = SEQ + P
HID = 1024
KH = HID // P
NL = 6
EPS = 1e-5
TINY = 1.2e-38
CAP = 80.0


Stages = namedtuple("Stages", "px_done pz_done conv0_done tap1_done tap2_done conv_done x_done z_done")


def build(nc, hidden, w_bcdt, conv_bc, dt_par, w_xz, conv_par, d_par, w_out,
          w1, w2, b2, ln_g, ln_b, ln_cols, ident_in, mask_in, out):
    cs_dram = nc.dram_tensor("cs_rows", [NH, TOK], F32, kind="Internal").ap()
    xn_dram = nc.dram_tensor("xn_rows", [TOK, DM], F32, kind="Internal").ap()
    tiled = lambda ap: ap.rearrange("(t p) d -> p t d", p=P)

    with ExitStack() as ctx:
        def sb(name, shape, dt=F32, stack=ctx):
            return stack.enter_context(nc.sbuf_tensor(name, shape, dt))

        ident = sb("ident", [P, P])
        xhi = sb("xhi", [P, KD, TOK], F32R)
        xlo = sb("xlo", [P, KD, TOK], F32R)
        acc = sb("acc", [P, TILES, DM])

        w1raw = sb("w1raw", [P, KD * HID + KH])
        w1_in = ctx.enter_context(nc.semaphore("w1_in"))
        meansq = sb("meansq", [P, TILES])

        with ExitStack() as mixer:
            gmat = sb("gmat", [P, NSEQ, LW], stack=mixer)
            wraw = sb("wraw", [P, 2, 2 * KD * P], stack=mixer)
            whi = sb("whi", [P, 2, 2 * KD, P], F32R, stack=mixer)
            wlo = sb("wlo", [P, 2, 2 * KD, P], F32R, stack=mixer)
            w_in = [mixer.enter_context(nc.semaphore(f"w_in{i}")) for i in range(2)]
            conv = sb("conv", [P, 2, TAPS + 1], stack=mixer)
            conv_in = [mixer.enter_context(nc.semaphore(f"conv_in{i}")) for i in range(2)]
            srow = sb("srow", [P, 2, HPT, TOK // 2], stack=mixer)
            srow_in = [mixer.enter_context(nc.semaphore(f"srow_in{i}")) for i in range(2)]
            xt = sb("xt", [P, 2, TOK], stack=mixer)
            zt = sb("zt", [P, 2, TOK], stack=mixer)
            stages = Stages(*[mixer.enter_context(nc.semaphore(name)) for name in Stages._fields])
            tokpar = sb("tokpar", [P, TILES, NH], stack=mixer)
            prepare(nc, hidden, xn_dram, w_bcdt, conv_bc, dt_par, mask_in, cs_dram, ident_in, ident,
                    xhi, xlo, acc, gmat, tokpar, w_xz, wraw, whi, wlo, w_in,
                    conv_par, conv, conv_in, srow, srow_in, xt, zt, stages, tiled)
            mix(nc, w_xz, conv_par, d_par, w_out, w1, cs_dram, ident, xhi, xlo, acc, gmat, tokpar,
                wraw, whi, wlo, w_in, conv, conv_in, srow, srow_in, xt, zt, stages,
                w1raw, w1_in, meansq)
        mlp(nc, hidden, xn_dram, w1, w2, b2, ln_g, ln_b, ln_cols, ident, xhi, xlo, acc, out,
            w1raw, w1_in, meansq, tiled)


def prepare(nc, hidden, xn_dram, w_bcdt, conv_bc, dt_par, mask_in, cs_dram, ident_in, ident,
            xhi, xlo, acc, gmat, tokpar, w_xz, wraw, whi, wlo, w_in,
            conv_par, conv, conv_in, srow, srow_in, xt, zt, stages, tiled):
    with ExitStack() as ctx:
        sb = lambda name, shape, dt=F32: ctx.enter_context(nc.sbuf_tensor("prep_" + name, shape, dt))
        sem = lambda name: ctx.enter_context(nc.semaphore("prep_" + name))
        hid = sb("hid", [P, TILES, DM])
        stats = sb("stats", [P, TILES, 6])
        mv = sb("mv", [P, TILES, 2])
        vare = sb("vare", [P, TILES])
        rstd = sb("rstd", [P, TILES])
        mhalf = sb("mhalf", [P, TPB])
        mask = sb("mask", [P, LW])
        cbc = sb("cbc", [P, 2, TAPS + 1])
        par = sb("par", [P, 2])
        bc_hi = sb("bc_hi", [P, KD, 3 * P], F32R)
        bc_lo = sb("bc_lo", [P, KD, 3 * P], F32R)
        bct = sb("bct", [P, 2, TOK])
        v = sb("v", [P, TOK])
        u = sb("u", [P, TOK])
        w = sb("w", [P, TOK])
        dtcs = sb("dtcs", [P, TOK])
        bc_raw = dtcs[:, 0:KD * 3 * P].rearrange("p (k m) -> p k m", k=KD)
        tokraw = hid[:, :, 0:2 * NH]
        ones = sb("ones", [P, SEQ])
        tiny = sb("tiny", [P, 1])
        bank = [ctx.enter_context(nc.psum_tensor(f"prep_bank{i}", [P, BLK], F32)) for i in range(8)]
        tp = [bank[4:6], bank[6:8]]

        const_in = sem("const_in")
        hid_in = [sem(f"hid_in{b}") for b in range(NB)]
        consts_in = sem("consts_in")
        bc_in = sem("bc_in")
        mhalf_set = sem("mhalf_set")
        tiny_set = sem("tiny_set")
        stats_done = sem("stats_done")
        mv_done = sem("mv_done")
        vare_done = sem("vare_done")
        rstd_done = sem("rstd_done")
        xn_done = sem("xn_done")
        xt_done = sem("xt_done")
        hi_done = sem("hi_done")
        lo_done = sem("lo_done")
        xn_out = sem("xn_out")
        bc_hi_done = sem("bc_hi_done")
        bc_split = sem("bc_split")
        w_hi_done = sem("w_hi_done")
        w_lo_done = sem("w_lo_done")
        ones_set = sem("ones_set")
        proj_done = sem("proj_done")
        v_done = sem("v_done")
        abs_done = sem("abs_done")
        u_done = sem("u_done")
        w_done = sem("w_done")
        lost_done = sem("lost_done")
        ln_done = sem("ln_done")
        log_done = sem("log_done")
        softplus_done = sem("softplus_done")
        logdt_done = sem("logdt_done")
        decay_done = sem("decay_done")
        cs_done = sem("cs_done")
        cs_out = sem("cs_out")
        conv0_done = sem("conv0_done")
        tap_done = sem("tap_done")
        conv_done = sem("conv_done")
        bct_done = sem("bct_done")
        g_done = sem("g_done")
        g_masked = sem("g_masked")
        tr_done = sem("tr_done")
        tr_copied = sem("tr_copied")
        tokpar_done = sem("tokpar_done")
        block = ctx.enter_context(nc.Block())

        @block.sync
        def _(sp):
            for b in range(NB):
                sp.dma_start(hid[:, b * TPB:(b + 1) * TPB, :],
                             tiled(hidden)[:, b * TPB:(b + 1) * TPB, :]).then_inc(hid_in[b], 16)
                if b == 0:
                    sp.dma_start(ident[:], ident_in).then_inc(const_in, 16)
                if b == 1:
                    sp.dma_start(bc_raw, w_bcdt).then_inc(bc_in, 16)
            for dst, src in ((par, dt_par), (cbc, conv_bc), (mask, mask_in)):
                sp.dma_start(dst[:], src).then_inc(consts_in, 16)
            for c in range(2):
                sp.dma_start(wraw[:, c], w_xz[c]).then_inc(w_in[c], 16)
                sp.dma_start(conv[:, c], conv_par[c]).then_inc(conv_in[c], 16)
            for b in range(NB):
                sp.wait_ge(xn_done, TPB * (b + 1))
                sp.dma_start(tiled(xn_dram)[:, b * TPB:(b + 1) * TPB, :],
                             hid[:, b * TPB:(b + 1) * TPB, :]).then_inc(xn_out, 16)
            sp.wait_ge(cs_done, NSEQ)
            sp.dma_start(cs_dram, dtcs[HD:P, :]).then_inc(cs_out, 16)
            sp.wait_ge(xn_out, 16 * NB)
            sp.wait_ge(cs_out, 16)
            for half in range(2):
                load_rows(sp, cs_dram, srow, srow_in, 0, half)

        @block.gpsimd
        def _(pool):
            pool.memset(mhalf[:], -0.5).then_inc(mhalf_set, 1)
            pool.memset(tiny[:], TINY).then_inc(tiny_set, 1)
            pool.wait_ge(mhalf_set, 1)
            for b in range(NB):
                pool.wait_ge(vare_done, b + 1)
                pool.tensor_tensor(rstd[:, b * TPB:(b + 1) * TPB], vare[:, b * TPB:(b + 1) * TPB],
                                   mhalf[:], ALU.pow).then_inc(rstd_done, 1)
                if b == 1:
                    pool.wait_ge(bc_hi_done, 1)
                    pool.tensor_tensor(bc_lo[:], bc_raw, bc_hi[:].bitcast(F32),
                                       ALU.subtract).then_inc(bc_split, 1)
            for c in range(2):
                pool.wait_ge(w_hi_done, c + 1)
                pool.tensor_tensor(wlo[:, c].rearrange("p k m -> p (k m)"), wraw[:, c],
                                   whi[:, c].rearrange("p k m -> p (k m)").bitcast(F32),
                                   ALU.subtract).then_inc(w_lo_done, 1)
            pool.memset(ones[:], 1.0).then_inc(ones_set, 1)
            pool.memset(acc[:], 0.0).then_inc(ones_set, 1)
            for b in range(NB):
                c = slice(b * BLK, (b + 1) * BLK)
                pool.wait_ge(ln_done, b + 1)
                pool.tensor_tensor(u[:, c], w[:, c], u[:, c], ALU.subtract).then_inc(log_done, 1)
                pool.wait_ge(log_done, b + 1)
                pool.wait_ge(v_done, b + 1)
                pool.tensor_tensor(u[:, c], v[:, c], u[:, c], ALU.add
                                   ).then_inc(softplus_done, 1)
            for b in range(NB):
                t = slice(b * TPB, (b + 1) * TPB)
                pool.wait_ge(tr_copied, b + 1)
                pool.tensor_tensor(tokpar[:, t, :], tokraw[:, t, 0:NH], tokraw[:, t, NH:],
                                   ALU.add).then_inc(tokpar_done, 1)

        @block.tensor
        def _(pe):
            def transposes(b):
                pe.wait_ge(xn_done, TPB * (b + 1))
                if b >= 2:
                    pe.wait_ge(lo_done, KD * (b - 1))
                for k in range(KD):
                    for t in range(TPB):
                        last = pe.transpose(tp[b % 2][k][:, t * P:(t + 1) * P],
                                            hid[:, b * TPB + t, k * P:(k + 1) * P], ident[:])
                    last.then_inc(xt_done, 1)

            def product(n):
                m, b = n // NB, n % NB
                if m == 0:
                    pe.wait_ge(lo_done, KD * (b + 1))
                if m == 2:
                    pe.wait_ge(abs_done, b + 1)
                    pe.wait_ge(v_done, b + 1)
                project(pe, bank[n % 8][:], bc_hi[:, :, m * P:(m + 1) * P],
                        bc_lo[:, :, m * P:(m + 1) * P], xhi, xlo, b).then_inc(proj_done, 1)

            pe.wait_ge(const_in, 16)
            transposes(0)
            transposes(1)
            pe.wait_ge(bc_split, 1)
            for b in range(2, NB):
                product(b - 2)
                transposes(b)
            for n in range(2, 3 * NB):
                product(n)

            def project_first(k, b):
                project(pe, bank[(6, 7, 0, 1)[b]][:], whi[:, 0, k:k + KD], wlo[:, 0, k:k + KD],
                        xhi, xlo, b).then_inc(stages.pz_done if k else stages.px_done, 1)

            def g(s):
                pe.wait_ge(bct_done, NB + s // SPB + 1)
                if s >= 2:
                    pe.wait_ge(g_masked, s - 1)
                dst = bank[4 + s % 2]
                o = s * SEQ
                pe.matmul(dst[:, 0:SEQ], bct[:, 0, o:o + P], bct[:, 1, o:o + SEQ],
                          start=True, stop=True)
                pe.matmul(dst[:, SEQ:LW], bct[:, 0, o + P:o + SEQ], bct[:, 1, o + P:o + SEQ],
                          start=True, stop=True).then_inc(g_done, 1)

            pe.wait_ge(w_lo_done, 1)
            for b in range(NB):
                pe.wait_ge(conv_done, 3 + b)
                project_first(0, b)
            for s in range(4):
                g(s)
            for b in range(NB):
                pe.wait_ge(cs_done, SPB * (b + 1))
                pe.wait_ge(logdt_done, b + 1)
                if b == 0:
                    pe.wait_ge(conv_done, 2 * NB)
                if b >= 2:
                    pe.wait_ge(tr_copied, b - 1)
                for t in range(TPB):
                    last = pe.transpose(bank[2 + b % 2][:, t * P:(t + 1) * P],
                                        dtcs[:, (b * TPB + t) * P:(b * TPB + t + 1) * P], ident[:])
                last.then_inc(tr_done, 1)
            for b in range(NB):
                if b % 2 == 0:
                    g(4 + b)
                    g(5 + b)
                pe.wait_ge(stages.conv_done, b + 1)
                project_first(KD, b)

        @block.scalar
        def _(act):
            def conv0(n):
                m, b = n // NB, n % NB
                act.wait_ge(proj_done, NB + n + 1)
                act.activation(bct[:, m, b * BLK:(b + 1) * BLK], bank[(NB + n) % 8][:], ACT.Identity,
                               bias=cbc[:, m, TAPS:TAPS + 1],
                               scale=cbc[:, m, TAPS - 1:TAPS]).then_inc(conv0_done, 1)

            for b in range(NB):
                if b == 1:
                    act.wait_ge(bc_in, 16)
                    act.copy(bc_hi[:], bc_raw).then_inc(bc_hi_done, 1)
                for k in range(KD):
                    act.wait_ge(xt_done, KD * b + k + 1)
                    act.copy(xhi[:, k, b * BLK:(b + 1) * BLK], tp[b % 2][k][:]).then_inc(hi_done, 1)
            for c in range(2):
                act.wait_ge(w_in[c], 16)
                act.copy(whi[:, c].rearrange("p k m -> p (k m)"), wraw[:, c]).then_inc(w_hi_done, 1)
            act.wait_ge(consts_in, 48)
            act.wait_ge(tiny_set, 1)
            for b in range(NB):
                c = slice(b * BLK, (b + 1) * BLK)
                act.wait_ge(proj_done, b + 1)
                act.activation(u[:, c], bank[b][:], ACT.Abs, bias=par[:, 0:1]).then_inc(abs_done, 1)
                act.activation(v[:, c], bank[b][:], ACT.Relu, bias=par[:, 0:1]).then_inc(v_done, 1)
            for b in range(NB):
                c = slice(b * BLK, (b + 1) * BLK)
                act.wait_ge(abs_done, b + 1)
                act.activation(u[:, c], u[:, c], ACT.Exp, scale=-1.0).then_inc(u_done, 1)
            for n in range(2):
                conv0(n)
            for b in range(NB):
                c = slice(b * BLK, (b + 1) * BLK)
                act.wait_ge(lost_done, b + 1)
                act.activation(w[:, c], w[:, c], ACT.Ln).then_inc(ln_done, 1)
            for n in range(2, 2 * NB):
                conv0(n)
            for n in range(2 * NB):
                m, b = n // NB, n % NB
                if n == NB:
                    act.wait_ge(conv_in[0], 16)
                    for k in range(NB):
                        act.wait_ge(stages.px_done, k + 1)
                        act.activation(xt[:, 0, k * BLK:(k + 1) * BLK], bank[(6, 7, 0, 1)[k]][:],
                                       ACT.Identity, bias=conv[:, 0, TAPS:TAPS + 1],
                                       scale=conv[:, 0, TAPS - 1:TAPS]).then_inc(stages.conv0_done, 1)
                act.wait_ge(conv_done, n + 1)
                c = bct[:, m, b * BLK:(b + 1) * BLK]
                act.activation(c, c, ACT.Silu).then_inc(bct_done, 1)
            for b in range(NB):
                c = slice(b * BLK, (b + 1) * BLK)
                act.wait_ge(softplus_done, b + 1)
                act.activation(dtcs[0:HD, c], u[0:HD, c], ACT.Ln,
                               bias=tiny[0:HD, :]).then_inc(logdt_done, 1)
            act.wait_ge(xn_out, 16 * NB)
            for b in range(NB):
                act.wait_ge(tr_done, b + 1)
                act.copy(tokraw[:, b * TPB:(b + 1) * TPB, :],
                         bank[2 + b % 2][:].rearrange("p (t h) -> p t h", t=TPB)
                         ).then_inc(tr_copied, 1)
            for b in range(NB):
                act.wait_ge(stages.conv_done, b + 1)
                x = xt[:, 0, b * BLK:(b + 1) * BLK]
                act.activation(x, x, ACT.Silu).then_inc(stages.x_done, 1)
            for b in range(NB):
                act.wait_ge(stages.pz_done, b + 1)
                act.activation(zt[:, 0, b * BLK:(b + 1) * BLK], bank[(6, 7, 0, 1)[b]][:],
                               ACT.Silu).then_inc(stages.z_done, 1)

        @block.vector
        def _(dve):
            def lo_part(b):
                for k in range(KD):
                    dve.wait_ge(hi_done, KD * b + k + 1)
                    dve.tensor_tensor(xlo[:, k, b * BLK:(b + 1) * BLK], tp[b % 2][k][:],
                                      xhi[:, k, b * BLK:(b + 1) * BLK].bitcast(F32),
                                      ALU.subtract).then_inc(lo_done, 1)

            def moments(b):
                dve.wait_ge(hid_in[b], 16)
                for t in range(b * TPB, (b + 1) * TPB):
                    dve.bn_stats(stats[:, t, :], hid[:, t, :]).then_inc(stats_done, 1)
                for t in range(b * TPB, (b + 1) * TPB):
                    dve.wait_ge(stats_done, t + 1)
                    dve.bn_aggr(mv[:, t, :], stats[:, t, :]).then_inc(mv_done, 1)
                dve.wait_ge(mv_done, TPB * (b + 1))
                dve.tensor_scalar(vare[:, b * TPB:(b + 1) * TPB], mv[:, b * TPB:(b + 1) * TPB, 1],
                                  EPS, None, ALU.add).then_inc(vare_done, 1)

            def taps(pair):
                for k in range(1, TAPS):
                    for i in range(2):
                        n = 2 * pair + i
                        m, b = n // NB, n % NB
                        if k == 1:
                            dve.wait_ge(conv0_done, n + 1)
                        else:
                            dve.wait_ge(tap_done, 4 * pair + 2 * (k - 2) + i + 1)
                        conv_tap(dve, bct[:, m, b * BLK:(b + 1) * BLK], bank[(NB + n) % 8][:],
                                 cbc[:, m, TAPS - 1 - k:TAPS - k], k
                                 ).then_inc(tap_done if k < TAPS - 1 else conv_done, 1)

            def decays(b):
                c = slice(b * BLK, (b + 1) * BLK)
                dve.wait_ge(softplus_done, b + 1)
                dve.tensor_scalar(v[HD:P, c], u[HD:P, c], par[HD:P, 1:2], -1.0, ALU.mult,
                                  ALU.mult).then_inc(decay_done, 1)
                dve.wait_ge(decay_done, b + 1)
                if b == 0:
                    dve.wait_ge(ones_set, 1)
                for s in range(b * SPB, (b + 1) * SPB):
                    q = slice(s * SEQ, (s + 1) * SEQ)
                    dve.tensor_tensor_scan(dtcs[HD:P, q], ones[HD:P, :], v[HD:P, q], 0.0,
                                           ALU.mult, ALU.add).then_inc(cs_done, 1)

            def first_taps(pair):
                done = [stages.conv0_done, stages.tap1_done, stages.tap2_done, stages.conv_done]
                for k in range(1, TAPS):
                    for b in (2 * pair, 2 * pair + 1):
                        dve.wait_ge(done[k - 1], b + 1)
                        conv_tap(dve, xt[:, 0, b * BLK:(b + 1) * BLK], bank[(6, 7, 0, 1)[b]][:],
                                 conv[:, 0, TAPS - 1 - k:TAPS - k], k).then_inc(done[k], 1)

            def masked_g(s):
                dve.wait_ge(g_done, s + 1)
                dve.tensor_tensor(gmat[:, s, :], bank[4 + s % 2][:, 0:LW], mask[:],
                                  ALU.mult).then_inc(g_masked, 1)

            moments(0)
            for b in range(NB):
                if b + 1 < NB:
                    moments(b + 1)
                dve.wait_ge(rstd_done, b + 1)
                for t in range(b * TPB, (b + 1) * TPB):
                    dve.tensor_scalar(hid[:, t, :], hid[:, t, :], mv[:, t, 0:1], rstd[:, t:t + 1],
                                      ALU.subtract, ALU.mult).then_inc(xn_done, 1)
                if b >= 1:
                    lo_part(b - 1)
            lo_part(NB - 1)
            for b in range(NB):
                c = slice(b * BLK, (b + 1) * BLK)
                dve.wait_ge(u_done, b + 1)
                dve.tensor_scalar(w[:, c], u[:, c], 1.0, None, ALU.add).then_inc(w_done, 1)
            for b in range(NB):
                c = slice(b * BLK, (b + 1) * BLK)
                dve.wait_ge(w_done, b + 1)
                dve.scalar_tensor_tensor(u[:, c], w[:, c], -1.0, u[:, c], ALU.add,
                                         ALU.subtract).then_inc(lost_done, 1)
            taps(0)
            taps(1)
            taps(2)
            decays(0)
            decays(1)
            taps(3)
            masked_g(0)
            masked_g(1)
            decays(2)
            decays(3)
            first_taps(0)
            masked_g(2)
            masked_g(3)
            first_taps(1)
            for s in range(4, NSEQ):
                masked_g(s)


def project(pe, dst, w_hi, w_lo, xhi, xlo, b):
    cols = slice(b * BLK, (b + 1) * BLK)
    passes = [(w, x, k) for k in range(KD) for w, x in ((w_hi, xhi), (w_hi, xlo), (w_lo, xhi))]
    for i, (w, x, k) in enumerate(passes):
        last = pe.matmul(dst, w[:, k, :], x[:, k, cols], start=(i == 0), stop=(i == len(passes) - 1))
    return last


def load_rows(sp, cs_dram, srow, srow_in, c, half):
    for h in range(HPT):
        sp.dma_start(srow[:, half, h, :],
                     cs_dram[bass.ds(HPT * c + h, 1), half * TOK // 2:(half + 1) * TOK // 2]
                     .partition_broadcast(P)).then_inc(srow_in[half], 16)


def conv_tap(dve, dst, src, weight, k):
    d = dst.rearrange("p (s t) -> p s t", t=SEQ)
    s = src.rearrange("p (s t) -> p s t", t=SEQ)
    return dve.scalar_tensor_tensor(d[:, :, k:SEQ], s[:, :, 0:SEQ - k], weight, d[:, :, k:SEQ],
                                    ALU.mult, ALU.add)


def wait_past(eng, sem, count):
    if not (isinstance(count, int) and count <= 0):
        eng.wait_ge(sem, count)


Tile = namedtuple('Tile', 'c par pair')


def mix(nc, w_xz, conv_par, d_par, w_out, w1, cs_dram, ident, xhi, xlo, acc, gmat, tokpar,
        wraw, whi, wlo, w_in, conv, conv_in, srow, srow_in, xt, zt, stages, w1raw, w1_in, meansq):
    DVE_G = [(0, 0)]
    POOL_G = [(b, s) for b in range(NB) for s in range(SPB) if (b, s) not in DVE_G]

    with ExitStack() as ctx:
        sb = lambda name, shape, dt=F32: ctx.enter_context(nc.sbuf_tensor("mix_" + name, shape, dt))
        ps = lambda name: ctx.enter_context(nc.psum_tensor("mix_" + name, [P, BLK], F32))
        sem = lambda name: ctx.enter_context(nc.semaphore("mix_" + name))
        dcol = sb("dcol", [P, 2, 1])
        stok = sb("stok", [P, 2, TILES, HPT])
        oraw = sb("oraw", [P, 2, DM + 1])
        ohi = sb("ohi", [P, 2, DM], F32R)
        olo = sb("olo", [P, 2, DM], F32R)
        xtok = sb("xtok", [P, 2, TPB, P])
        dec = sb("dec", [P, 2, SPB, HPT, LW])
        yg = sb("yg", [P, NB, BLK])
        sq = sb("sq", [P, 2, BLK])
        sqacc = sb("sqacc", [P, TOK])
        ghi = sb("ghi", [P, 2, TOK], F32R)
        glo = sb("glo", [P, 2, TOK], F32R)
        onesq = sb("onesq", [P, 2])
        pa = [ps(f"pa{i}") for i in range(2)]
        pt = [ps(f"pt{i}") for i in range(2)]
        py = [ps(f"py{i}") for i in range(2)]
        po = [ps(f"po{i}") for i in range(2)]

        d_in = [sem(f"d_in{i}") for i in range(2)]
        o_in = sem("o_in")
        px_done, pz_done, conv0_done, tap1_done, tap2_done, conv_done, x_done, z_done = stages
        w_hi_done = sem("w_hi_done")
        w_split = sem("w_split")
        stok_done = sem("stok_done")
        o_scaled = sem("o_scaled")
        o_hi_done = sem("o_hi_done")
        o_split = sem("o_split")
        xtok_done = sem("xtok_done")
        xtok_copied = sem("xtok_copied")
        arg_done = sem("arg_done")
        dec_done = sem("dec_done")
        dve_g_done = sem("dve_g_done")
        pool_g_done = sem("pool_g_done")
        y_done = sem("y_done")
        yd_done = sem("yd_done")
        gated = sem("gated")
        ghi_done = sem("ghi_done")
        sq_done = sem("sq_done")
        glo_done = sem("glo_done")
        sq_added = sem("sq_added")
        o_done = sem("o_done")
        o_added = sem("o_added")
        pool_set = sem("pool_set")
        ms_done = sem("ms_done")
        ms_copied = sem("ms_copied")
        block = ctx.enter_context(nc.Block())

        def pairs(eng, body):
            body(0, True, False)
            body(1, False, False)
            with eng.Fori(2, PAIRS - 1) as q:
                body(q, False, False)
            body(PAIRS - 1, False, True)

        def steps(eng, step):
            def body(q, first, last):
                for e in range(2):
                    now, old = Tile(2 * q + e, e, q), Tile(2 * q + e - 1, 1 - e, q + e - 1)
                    new, next_new = Tile(2 * q + e + 1, 1 - e, q + e), Tile(2 * q + e + 2, e, q + 1)
                    step(q, e, now, old, new, next_new, first, last)

            pairs(eng, body)

        first_tile, last_tile = Tile(0, 0, 0), Tile(NCT - 1, 1, PAIRS - 1)

        def cols(b):
            return slice(b * BLK, (b + 1) * BLK)

        @block.sync
        def _(sp):
            def load(c, src, dst, sem):
                sp.dma_start(dst, src[bass.ds(c, 1)].rearrange("o p n -> (o p) n")).then_inc(sem, 16)

            load(0, d_par, dcol[:, 0], d_in[0])
            sp.dma_start(w1raw[:], w1[0]).then_inc(w1_in, 16)

            def body(q, first, last):
                wait_past(sp, o_split, 1 * q)
                sp.dma_start(oraw[:], w_out[bass.ds(q, 1)].rearrange("o p e n -> (o p) e n")
                             ).then_inc(o_in, 16)
                for e in range(2):
                    c = 2 * q + e
                    ahead = not (last and e)
                    if not last:
                        wait_past(sp, w_split, c - 1)
                        load(c + 2, w_xz, wraw[:, e], w_in[e])
                        sp.wait_ge(conv_done, NB * (c + 1))
                        load(c + 2, conv_par, conv[:, e], conv_in[e])
                    if ahead:
                        wait_past(sp, yd_done, NB * c)
                        load(c + 1, d_par, dcol[:, 1 - e], d_in[1 - e])
                        for half in range(2):
                            sp.wait_ge(arg_done, SPB * (NB * c + NB // 2 * (half + 1)))
                            load_rows(sp, cs_dram, srow, srow_in, c + 1, half)

            pairs(sp, body)

        @block.gpsimd
        def _(pool):
            pool.memset(sqacc[:], 0.0).then_inc(pool_set, 1)
            pool.memset(onesq[:], 1.0).then_inc(pool_set, 1)
            pool.wait_ge(pool_set, 2)

            def w_lo(t):
                pool.wait_ge(w_hi_done, t.c - 1)
                pool.tensor_tensor(wlo[:, t.par].rearrange("p k m -> p (k m)"), wraw[:, t.par],
                                   whi[:, t.par].rearrange("p k m -> p (k m)").bitcast(F32),
                                   ALU.subtract).then_inc(w_split, 1)

            def o_lo(q):
                pool.wait_ge(o_hi_done, 1 * q + 1)
                pool.tensor_tensor(olo[:], oraw[:, :, 0:DM], ohi[:].bitcast(F32),
                                   ALU.subtract).then_inc(o_split, 1)

            def times_g(t, b, s):
                pool.wait_ge(dec_done, SPB * (NB * t.c + b) + s + 1)
                d = dec[:, b % 2, s]
                g = gmat[:, b * SPB + s, :].unsqueeze(1).broadcast_to([P, HPT, LW])
                pool.tensor_tensor(d, d, g, ALU.mult).then_inc(pool_g_done, 1)

            def low(t, b):
                pool.wait_ge(ghi_done, NB * t.c + b + 1)
                pool.tensor_tensor(glo[:, t.par, cols(b)], yg[:, b, :],
                                   ghi[:, t.par, cols(b)].bitcast(F32),
                                   ALU.subtract).then_inc(glo_done, 1)

            def add_square(t, b):
                n = NB * t.c + b
                pool.wait_ge(sq_done, n + 1)
                wait_past(pool, sq_added, n - NB + 1)
                pool.tensor_tensor(sqacc[:, cols(b)], sqacc[:, cols(b)], sq[:, b % 2, :],
                                   ALU.add).then_inc(sq_added, 1)

            def step(q, e, now, old, new, next_new, first, last):
                before = not (first and e == 0)
                times_g(now, 0, 1)
                if before:
                    add_square(old, 0)
                times_g(now, 1, 0)
                times_g(now, 1, 1)
                if before:
                    add_square(old, 1)
                times_g(now, 2, 0)
                times_g(now, 2, 1)
                if before:
                    low(old, 2)
                times_g(now, 3, 0)
                if not last:
                    w_lo(next_new)
                times_g(now, 3, 1)
                if before:
                    low(old, 3)
                if e == 1:
                    o_lo(q)
                low(now, 0)
                low(now, 1)
                if before:
                    add_square(old, 2)
                    add_square(old, 3)

            steps(pool, step)
            add_square(last_tile, 0)
            add_square(last_tile, 1)
            low(last_tile, 2)
            low(last_tile, 3)
            add_square(last_tile, 2)
            add_square(last_tile, 3)

        @block.tensor
        def _(pe):
            def project_x(t, b):
                if b == 0:
                    wait_past(pe, w_split, t.c - 1)
                if b >= 2:
                    pe.wait_ge(conv_done, NB * t.c + b - 1)
                else:
                    wait_past(pe, z_done, NB * t.c + b - 1)
                project(pe, pa[b % 2][:], whi[:, t.par, 0:KD], wlo[:, t.par, 0:KD], xhi, xlo,
                        b).then_inc(px_done, 1)

            def project_z(t, b):
                if b >= 2:
                    pe.wait_ge(z_done, NB * t.c + b - 1)
                else:
                    pe.wait_ge(conv_done, NB * t.c + b + 3)
                project(pe, pa[b % 2][:], whi[:, t.par, KD:], wlo[:, t.par, KD:], xhi, xlo,
                        b).then_inc(pz_done, 1)

            def tokens(t, b):
                n = NB * t.c + b
                pe.wait_ge(x_done, n + 1)
                wait_past(pe, xtok_copied, n - 1)
                for k in range(b * TPB, (b + 1) * TPB):
                    last = pe.transpose(pt[b % 2][:, k % TPB * P:(k % TPB + 1) * P],
                                        xt[:, t.par, k * P:(k + 1) * P], ident[:])
                last.then_inc(xtok_done, 1)

            def outputs(t, b, s):
                n = NB * t.c + b
                if s == 0:
                    pe.wait_ge(xtok_copied, n + 1)
                    wait_past(pe, gated, n - 1)
                if (b, s) in POOL_G:
                    pe.wait_ge(pool_g_done, len(POOL_G) * t.c + POOL_G.index((b, s)) + 1)
                else:
                    pe.wait_ge(dve_g_done, len(DVE_G) * t.c + DVE_G.index((b, s)) + 1)
                o = s * SEQ
                for j, i, m in ((0, slice(o, o + SEQ), slice(0, SEQ)),
                                (1, slice(o + P, o + SEQ), slice(SEQ, LW))):
                    for h in range(HPT):
                        hp = slice(h * HD, (h + 1) * HD)
                        last = pe.matmul(py[b % 2][hp, i], xtok[:, b % 2, 2 * s + j, hp],
                                         dec[:, b % 2, s, h, m], start=(j == 0), stop=(j == 1))
                last.then_inc(y_done, 1)

            def output_rows(q, b, i):
                if i == 0:
                    pe.wait_ge(glo_done, NB * (2 * q + 1) + b + 1)
                    pe.wait_ge(o_split, q + 1)
                wait_past(pe, o_added, 2 * NB * q + 2 * b + i - 1)
                for t in (2 * i, 2 * i + 1):
                    dst = po[i][:, (t % 2) * DM:(t % 2 + 1) * DM]
                    k = slice((b * TPB + t) * P, (b * TPB + t + 1) * P)
                    for e in range(2):
                        pe.matmul(dst, ghi[:, e, k], ohi[:, e, :], start=(e == 0), stop=False)
                        pe.matmul(dst, ghi[:, e, k], olo[:, e, :], start=False, stop=False)
                        last = pe.matmul(dst, glo[:, e, k], ohi[:, e, :], start=False, stop=(e == 1))
                last.then_inc(o_done, 1)

            def step(q, e, now, old, new, next_new, first, last):
                ahead = not (last and e == 1)
                if ahead:
                    project_x(new, 0)
                    project_x(new, 1)
                tokens(now, 0)
                tokens(now, 1)
                if e == 1 and not first:
                    output_rows(q - 1, 2, 0)
                    output_rows(q - 1, 2, 1)
                if e == 0 and not first:
                    output_rows(q - 1, 0, 0)
                    output_rows(q - 1, 0, 1)
                tokens(now, 2)
                outputs(now, 0, 0)
                outputs(now, 0, 1)
                if ahead:
                    project_x(new, 2)
                    project_x(new, 3)
                outputs(now, 1, 0)
                tokens(now, 3)
                outputs(now, 1, 1)
                if e == 1 and not first:
                    output_rows(q - 1, 3, 0)
                    output_rows(q - 1, 3, 1)
                if e == 0 and not first:
                    output_rows(q - 1, 1, 0)
                    output_rows(q - 1, 1, 1)
                outputs(now, 2, 0)
                outputs(now, 2, 1)
                if ahead:
                    project_z(new, 0)
                    project_z(new, 1)
                    project_z(new, 2)
                    project_z(new, 3)
                outputs(now, 3, 0)
                outputs(now, 3, 1)

            steps(pe, step)
            for b in range(NB):
                output_rows(PAIRS - 1, b, 0)
                output_rows(PAIRS - 1, b, 1)
            pe.wait_ge(sq_added, NB * NCT)
            for t in range(TILES):
                last = pe.matmul(pt[0][:, t:t + 1], sqacc[:, t * P:(t + 1) * P], onesq[:, 0:1],
                                 start=True, stop=True)
            last.then_inc(ms_done, 1)

        @block.scalar
        def _(act):
            def w_hi(t):
                act.wait_ge(w_in[t.par], 16 * (t.pair + 1))
                wait_past(act, pz_done, NB * (t.c - 1))
                act.copy(whi[:, t.par].rearrange("p k m -> p (k m)"), wraw[:, t.par]
                         ).then_inc(w_hi_done, 1)

            def conv0(t, b):
                n = NB * t.c + b
                if b == 0:
                    act.wait_ge(conv_in[t.par], 16 * (t.pair + 1))
                act.wait_ge(px_done, n + 1)
                wait_past(act, yd_done, n - 2 * NB + 1)
                act.activation(xt[:, t.par, cols(b)], pa[b % 2][:], ACT.Identity,
                               bias=conv[:, t.par, TAPS:TAPS + 1],
                               scale=conv[:, t.par, TAPS - 1:TAPS]).then_inc(conv0_done, 1)

            def silu_x(t, b):
                act.wait_ge(conv_done, NB * t.c + b + 1)
                act.activation(xt[:, t.par, cols(b)], xt[:, t.par, cols(b)],
                               ACT.Silu).then_inc(x_done, 1)

            def silu_z(t, b):
                act.wait_ge(pz_done, NB * t.c + b + 1)
                wait_past(act, gated, NB * (t.c - 2) + b + 1)
                act.activation(zt[:, t.par, cols(b)], pa[b % 2][:], ACT.Silu).then_inc(z_done, 1)

            def decays(t, b, s):
                act.wait_ge(arg_done, SPB * (NB * t.c + b) + s + 1)
                d = dec[:, b % 2, s].rearrange("p h i -> p (h i)")
                act.activation(d, d, ACT.Exp, scale=-1.0).then_inc(dec_done, 1)

            def high(t, b):
                act.wait_ge(gated, NB * t.c + b + 1)
                wait_past(act, o_done, 2 * NB * (t.pair - 1) + 2 * (b + 1))
                act.copy(ghi[:, t.par, cols(b)], yg[:, b, :]).then_inc(ghi_done, 1)

            def square(t, b):
                n = NB * t.c + b
                act.wait_ge(gated, n + 1)
                wait_past(act, sq_added, n - 1)
                act.activation(sq[:, b % 2, :], yg[:, b, :], ACT.Square).then_inc(sq_done, 1)

            def copy_tokens(t, b):
                n = NB * t.c + b
                act.wait_ge(xtok_done, n + 1)
                wait_past(act, y_done, SPB * (n - 1))
                act.copy(xtok[:, b % 2].rearrange("p t c -> p (t c)"), pt[b % 2][:]
                         ).then_inc(xtok_copied, 1)

            def scale_o(q):
                act.wait_ge(o_in, 16 * (q + 1))
                for e in range(2):
                    act.activation(oraw[:, e, 0:DM], oraw[:, e, 0:DM], ACT.Identity,
                                   scale=oraw[:, e, DM:DM + 1]).then_inc(o_scaled, 1)

            def o_hi(q):
                wait_past(act, o_done, 2 * NB * q)
                act.wait_ge(o_scaled, 2 * q + 2)
                act.copy(ohi[:], oraw[:, :, 0:DM]).then_inc(o_hi_done, 1)

            def step(q, e, now, old, new, next_new, first, last):
                before = not (first and e == 0)
                ahead = not (last and e == 1)
                decays(now, 0, 0)
                decays(now, 0, 1)
                if ahead:
                    conv0(new, 0)
                    conv0(new, 1)
                if before:
                    square(old, 0)
                copy_tokens(now, 0)
                decays(now, 1, 0)
                if before:
                    square(old, 1)
                decays(now, 1, 1)
                if not last:
                    w_hi(next_new)
                copy_tokens(now, 1)
                if e == 0:
                    scale_o(q)
                decays(now, 2, 0)
                if before:
                    high(old, 2)
                decays(now, 2, 1)
                if ahead:
                    conv0(new, 2)
                    conv0(new, 3)
                if before:
                    square(old, 2)
                copy_tokens(now, 2)
                copy_tokens(now, 3)
                decays(now, 3, 0)
                decays(now, 3, 1)
                if ahead:
                    silu_x(new, 0)
                    silu_x(new, 1)
                    silu_x(new, 2)
                if before:
                    high(old, 3)
                    square(old, 3)
                if ahead:
                    silu_z(new, 0)
                if e == 1:
                    o_hi(q)
                if ahead:
                    silu_z(new, 1)
                high(now, 0)
                if ahead:
                    silu_x(new, 3)
                high(now, 1)
                if ahead:
                    silu_z(new, 2)
                    silu_z(new, 3)

            steps(act, step)
            square(last_tile, 0)
            square(last_tile, 1)
            high(last_tile, 2)
            square(last_tile, 2)
            high(last_tile, 3)
            square(last_tile, 3)

        @block.vector
        def _(dve):
            def tap(t, b, k):
                before, done = [(conv0_done, tap1_done), (tap1_done, tap2_done),
                                (tap2_done, conv_done)][k - 1]
                dve.wait_ge(before, NB * t.c + b + 1)
                conv_tap(dve, xt[:, t.par, cols(b)], pa[b % 2][:],
                         conv[:, t.par, TAPS - 1 - k:TAPS - k], k).then_inc(done, 1)

            def s_by_tokens(t):
                wait_past(dve, arg_done, SPB * NB * (t.c - 1))
                dve.tensor_copy(stok[:, t.par], tokpar[:, :, bass.ds(HPT * t.c, HPT)]
                                ).then_inc(stok_done, 1)

            def exponents(t, b, s):
                m = SPB * (NB * t.c + b) + s
                half, i0 = b // 2, b % 2 * BLK + s * SEQ
                if b == 0 and s == 0:
                    dve.wait_ge(stok_done, t.c + 1)
                if b % 2 == 0 and s == 0:
                    dve.wait_ge(srow_in[half], 16 * HPT * (t.c + 1))
                wait_past(dve, y_done, m - 2 * SPB + 1)
                for h in range(HPT):
                    for j, i, k in ((0, slice(i0, i0 + SEQ), slice(0, SEQ)),
                                    (1, slice(i0 + P, i0 + SEQ), slice(SEQ, LW))):
                        tile = b * TPB + 2 * s + j
                        last = dve.tensor_scalar(dec[:, b % 2, s, h, k], srow[:, half, h, i],
                                                 stok[:, t.par, tile, h:h + 1], -CAP,
                                                 ALU.subtract, ALU.max)
                last.then_inc(arg_done, 1)

            def times_g(t, b, s):
                dve.wait_ge(dec_done, SPB * (NB * t.c + b) + s + 1)
                d = dec[:, b % 2, s]
                g = gmat[:, b * SPB + s, :].unsqueeze(1).broadcast_to([P, HPT, LW])
                dve.tensor_tensor(d, d, g, ALU.mult).then_inc(dve_g_done, 1)

            def add_dx(t, b):
                n = NB * t.c + b
                if b == 0:
                    dve.wait_ge(d_in[t.par], 16 * (t.pair + 1))
                dve.wait_ge(y_done, SPB * (n + 1))
                dve.scalar_tensor_tensor(py[b % 2][:], xt[:, t.par, cols(b)], dcol[:, t.par],
                                         py[b % 2][:], ALU.mult, ALU.add).then_inc(yd_done, 1)

            def gate(t, b):
                n = NB * t.c + b
                dve.wait_ge(yd_done, n + 1)
                dve.wait_ge(z_done, n + 1)
                wait_past(dve, sq_done, n - NB + 1)
                wait_past(dve, glo_done, n - NB + 1)
                dve.tensor_tensor(yg[:, b, :], py[b % 2][:], zt[:, t.par, cols(b)],
                                  ALU.mult).then_inc(gated, 1)

            def add_rows(q, b, i):
                m = 2 * NB * q + 2 * b + i
                dve.wait_ge(o_done, m + 1)
                wait_past(dve, o_added, m - 2 * NB + 1 if isinstance(m, int) else m - 1)
                rows = acc[:, b * TPB + 2 * i:b * TPB + 2 * i + 2, :].rearrange("p t d -> p (t d)")
                dve.tensor_tensor(rows, po[i][:], rows, ALU.add).then_inc(o_added, 1)

            s_by_tokens(first_tile)
            exponents(first_tile, 0, 0)
            exponents(first_tile, 0, 1)
            exponents(first_tile, 1, 0)

            def step(q, e, now, old, new, next_new, first, last):
                before = not (first and e == 0)
                ahead = not (last and e == 1)
                exponents(now, 1, 1)
                if before:
                    add_dx(old, 3)
                times_g(now, 0, 0)
                if before:
                    gate(old, 3)
                if ahead:
                    tap(new, 0, 1)
                    tap(new, 1, 1)
                    tap(new, 0, 2)
                    tap(new, 1, 2)
                    tap(new, 0, 3)
                    tap(new, 1, 3)
                exponents(now, 2, 0)
                add_dx(now, 0)
                exponents(now, 2, 1)
                gate(now, 0)
                if e == 1 and not first:
                    add_rows(q - 1, 2, 0)
                    add_rows(q - 1, 2, 1)
                if e == 0 and not first:
                    add_rows(q - 1, 0, 0)
                    add_rows(q - 1, 0, 1)
                exponents(now, 3, 0)
                if ahead:
                    tap(new, 2, 1)
                exponents(now, 3, 1)
                if ahead:
                    tap(new, 3, 1)
                    tap(new, 2, 2)
                    tap(new, 3, 2)
                    tap(new, 2, 3)
                    tap(new, 3, 3)
                add_dx(now, 1)
                add_dx(now, 2)
                if e == 1 and not first:
                    add_rows(q - 1, 3, 0)
                    add_rows(q - 1, 3, 1)
                if e == 0 and not first:
                    add_rows(q - 1, 1, 0)
                gate(now, 1)
                if ahead:
                    s_by_tokens(new)
                gate(now, 2)
                if ahead:
                    exponents(new, 0, 0)
                    exponents(new, 0, 1)
                if e == 0 and not first:
                    add_rows(q - 1, 1, 1)
                if ahead:
                    exponents(new, 1, 0)

            steps(dve, step)
            add_dx(last_tile, 3)
            gate(last_tile, 3)
            for b in range(NB):
                add_rows(PAIRS - 1, b, 0)
                add_rows(PAIRS - 1, b, 1)
            dve.wait_ge(ms_done, 1)
            dve.tensor_scalar(meansq[:], pt[0][:, 0:TILES], 1.0 / DI, EPS, ALU.mult,
                              ALU.add).then_inc(ms_copied, 1)


def mlp(nc, hidden, xn_dram, w1, w2, b2, ln_g, ln_b, ln_cols, ident, xhi, xlo, acc, out,
        w1raw, w1_in, meansq, tiled):
    with ExitStack() as ctx:
        sb = lambda name, shape, dt=F32: ctx.enter_context(nc.sbuf_tensor("mlp_" + name, shape, dt))
        ps = lambda name: ctx.enter_context(nc.psum_tensor("mlp_" + name, [P, BLK], F32))
        sem = lambda name: ctx.enter_context(nc.semaphore("mlp_" + name))
        res = sb("res", [P, TILES, DM])
        w1hi = sb("w1hi", [P, KD, HID], F32R)
        w1lo = sb("w1lo", [P, KD, HID], F32R)
        w2raw = sb("w2raw", [P, KH, DM])
        w2hi = sb("w2hi", [P, KH, DM], F32R)
        w2lo = sb("w2lo", [P, KH, DM], F32R)
        b1c = sb("b1c", [P, KH])
        gbc = sb("gbc", [P, (NL - 1) * 2 * KD])
        grow = sb("grow", [P, 3, DM])
        h = sb("h", [P, 4, BLK])
        hhi = sb("hhi", [P, KH, BLK], F32R)
        hlo = sb("hlo", [P, KH, BLK], F32R)
        u = sb("u2", [P, 2, TPB, DM])
        xf = sb("xf", [P, KD, BLK])
        stats = sb("stats2", [P, TPB, 6])
        mv = sb("mv2", [P, TPB, 2])
        vare = sb("vare2", [P, TPB])
        rstd = sb("rstd2", [P, TPB])
        mhalf = sb("mhalf2", [P, TPB])
        hidt = sb("hidt", [P, TPB, DM])
        mhalf16 = sb("mhalf16", [P, TILES])
        rms = sb("rms", [P, TILES])
        p1 = [ps(f"p1{i}") for i in range(2)]
        p2 = [ps(f"p2{i}") for i in range(4)]
        p3 = [ps(f"p3{i}") for i in range(2)]

        const_in = sem("const_in2")
        res_in = sem("res_in")
        w2_in = sem("w2_in")
        w1_hi_done = sem("w1_hi_done")
        w1_split = sem("w1_split")
        b1_done = sem("b1_done")
        w2_hi_done = sem("w2_hi_done")
        w2_split = sem("w2_split")
        grow_in = sem("grow_in")
        brow_done = sem("brow_done")
        first_done = sem("first_done")
        gelu_done = sem("gelu_done")
        hhi_done = sem("hhi_done")
        hlo_done = sem("hlo_done")
        second_done = sem("second_done")
        u_done = sem("u_done2")
        stats_done = sem("stats_done2")
        stats_seen = sem("stats_seen")
        mv_done = sem("mv_done2")
        vare_done = sem("vare_done2")
        rstd_done = sem("rstd_done2")
        norm_done = sem("norm_done2")
        tr_done = sem("tr_done2")
        xf_done = sem("xf_done")
        xhi_done = sem("xhi_done")
        xlo_done = sem("xlo_done")
        scaled_done = sem("scaled_done")
        res_done = sem("res_done")
        pool_set = sem("pool_set2")
        hid_in = sem("hid_in2")
        rms_done = sem("rms_done")
        rms_scaled = sem("rms_scaled")
        mixed = sem("mixed")
        all_added = sem("all_added")
        out_done = sem("out_done")
        block = ctx.enter_context(nc.Block())

        w1tiles = w1raw[:, 0:KD * HID].rearrange("p (k m) -> p k m", k=KD)

        def layers(eng, body):
            body(0, True, False)
            with eng.Fori(1, NL - 1) as l:
                body(l, False, False)
            body(NL - 1, False, True)

        @block.sync
        def _(sp):
            sp.dma_start(w2raw[:], w2[0]).then_inc(w2_in, 16)
            sp.dma_start(gbc[:], ln_cols).then_inc(const_in, 16)
            sp.dma_start(res[:], tiled(xn_dram)).then_inc(res_in, 16)
            sp.dma_start(grow[:, 2, :], b2[0:1, :].partition_broadcast(P)).then_inc(grow_in, 16)

            def body(l, first, last):
                if last:
                    return
                sp.wait_ge(w2_split, KH * l + KH)
                sp.dma_start(w1raw[:], w1[bass.ds(l + 1, 1)].rearrange("o p n -> (o p) n")
                             ).then_inc(w1_in, 16)
                if first:
                    sp.wait_ge(res_done, NB)
                else:
                    sp.wait_ge(res_done, NB * l + NB)
                for i, row in enumerate((ln_g[bass.ds(l, 1), :], ln_b[bass.ds(l, 1), :],
                                         b2[bass.ds(l + 1, 1), :])):
                    sp.dma_start(grow[:, i, :], row.partition_broadcast(P)).then_inc(grow_in, 16)
                sp.dma_start(w2raw[:], w2[bass.ds(l + 1, 1)].rearrange("o p k m -> (o p) k m")
                             ).then_inc(w2_in, 16)

            layers(sp, body)
            for b in range(NB):
                if b:
                    sp.wait_ge(mixed, b)
                sp.dma_start(hidt[:], tiled(hidden)[:, b * TPB:(b + 1) * TPB, :]).then_inc(hid_in, 16)
            for b in range(NB):
                sp.wait_ge(u_done, TPB * (NB * (NL - 1) + b + 1))
                sp.dma_start(tiled(out)[:, b * TPB:(b + 1) * TPB, :],
                             acc[:, b * TPB:(b + 1) * TPB, :]).then_inc(out_done, 16)
            sp.wait_ge(out_done, 16 * NB)

        @block.gpsimd
        def _(pool):
            def w1_lo(l, j):
                pool.wait_ge(w1_hi_done, KH * l + j + 1)
                hj = slice(j * P, (j + 1) * P)
                pool.tensor_tensor(w1lo[:, :, hj], w1tiles[:, :, hj], w1hi[:, :, hj].bitcast(F32),
                                   ALU.subtract).then_inc(w1_split, 1)

            def w2_lo(l, j):
                pool.wait_ge(w2_hi_done, KH * l + j + 1)
                pool.tensor_tensor(w2lo[:, j, :], w2raw[:, j, :], w2hi[:, j, :].bitcast(F32),
                                   ALU.subtract).then_inc(w2_split, 1)

            def inverse_deviation(l, b):
                pool.wait_ge(vare_done, NB * l + b + 1)
                pool.tensor_tensor(rstd[:], vare[:], mhalf[:], ALU.pow
                                   ).then_inc(rstd_done, 1)

            def residual(l, b):
                n = NB * l + b
                r = res[:, b * TPB:(b + 1) * TPB, :]
                rows = lambda i: grow[:, i, :].unsqueeze(1).broadcast_to([P, TPB, DM])
                pool.wait_ge(norm_done, TPB * (n + 1))
                pool.tensor_tensor(r, u[:, b % 2], rows(0), ALU.mult).then_inc(scaled_done, 1)
                pool.wait_ge(scaled_done, n + 1)
                pool.tensor_tensor(r, r, rows(1), ALU.add).then_inc(res_done, 1)

            for j in range(KH):
                w1_lo(0, j)
            pool.memset(mhalf[:], -0.5).then_inc(pool_set, 1)
            pool.memset(mhalf16[:], -0.5).then_inc(pool_set, 1)
            for j in range(KH):
                w2_lo(0, j)
            pool.wait_ge(pool_set, 2)
            pool.tensor_tensor(rms[:], meansq[:], mhalf16[:], ALU.pow).then_inc(rms_done, 1)
            pool.wait_ge(res_in, 16)
            pool.wait_ge(grow_in, 16)
            for b in range(NB):
                r = res[:, b * TPB:(b + 1) * TPB, :]
                pool.tensor_tensor(r, r, grow[:, 2, :].unsqueeze(1).broadcast_to([P, TPB, DM]),
                                   ALU.add).then_inc(res_done, 1)

            def body(l, first, last):
                if not first:
                    inverse_deviation(l - 1, NB - 1)
                    residual(l - 1, NB - 1)
                if last:
                    pool.wait_ge(rms_scaled, TILES)
                    for b in range(NB):
                        a = acc[:, b * TPB:(b + 1) * TPB, :]
                        pool.wait_ge(hid_in, 16 * (b + 1))
                        pool.tensor_tensor(a, a, hidt[:], ALU.add).then_inc(mixed, 1)
                        pool.wait_ge(mixed, b + 1)
                        pool.tensor_tensor(a, a, res[:, b * TPB:(b + 1) * TPB, :],
                                           ALU.add).then_inc(all_added, 1)
                    return
                pool.wait_ge(grow_in, 48 * l + 64)
                pool.tensor_tensor(grow[:, 1, :], grow[:, 1, :], grow[:, 2, :],
                                   ALU.add).then_inc(brow_done, 1)
                pool.wait_ge(brow_done, 1 * l + 1)
                for b in range(1, NB):
                    inverse_deviation(l, b - 1)
                    residual(l, b - 1)
                    for j in range(KH):
                        if b == 2:
                            w1_lo(l + 1, j)
                        if b == 3:
                            w2_lo(l + 1, j)

            layers(pool, body)

        @block.tensor
        def _(pe):
            def first_product(l, b, j, first):
                n = NB * l + b
                if b == 0:
                    pe.wait_ge(w1_split, KH * l + j + 1)
                if j == 0 and not first:
                    pe.wait_ge(xlo_done, KD * (n - NB + 1))
                if not (first and b == 0 and j < 2):
                    pe.wait_ge(gelu_done, KH * n + j - 1)
                hj = slice(j * P, (j + 1) * P)
                project(pe, p1[j % 2][:], w1hi[:, :, hj], w1lo[:, :, hj], xhi, xlo,
                        b).then_inc(first_done, 1)

            def transposes(l, b, first):
                n = NB * l + b
                pe.wait_ge(norm_done, TPB * (n + 1))
                if not (first and b == 0):
                    pe.wait_ge(xf_done, KD * n)
                for k in range(KD):
                    for t in range(TPB):
                        last = pe.transpose(p3[k][:, t * P:(t + 1) * P],
                                            u[:, b % 2, t, k * P:(k + 1) * P], ident[:])
                    last.then_inc(tr_done, 1)

            def second_product(l, b, j, first):
                n = NB * l + b
                if b == 0:
                    pe.wait_ge(w2_split, KH * l + j + 1)
                pe.wait_ge(hlo_done, KH * n + j + 1)
                for t in range(TPB):
                    if j == 0 and not (first and b == 0):
                        pe.wait_ge(u_done, TPB * (n - 1) + t + 1)
                    dst = p2[t][:, 0:DM]
                    k = slice(t * P, (t + 1) * P)
                    pe.matmul(dst, hhi[:, j, k], w2hi[:, j, :], start=(j == 0), stop=False)
                    pe.matmul(dst, hhi[:, j, k], w2lo[:, j, :], start=False, stop=False)
                    last = pe.matmul(dst, hlo[:, j, k], w2hi[:, j, :], start=False,
                                     stop=(j == KH - 1))
                last.then_inc(second_done, 1)

            for j in range(KH):
                first_product(0, 0, j, True)

            def body(l, first, last):
                for b in range(NB):
                    for j in range(KH):
                        second_product(l, b, j, first)
                        if b < NB - 1:
                            first_product(l, b + 1, j, first)
                        elif not last:
                            first_product(l + 1, 0, j, False)
                        if j == 3:
                            if b == 0:
                                if not first:
                                    transposes(l - 1, NB - 1, False)
                            elif not last:
                                transposes(l, b - 1, first)

            layers(pe, body)

        @block.scalar
        def _(act):
            def hidden_tile(l, b, j, first):
                n = NB * l + b
                m = KH * n + j
                act.wait_ge(first_done, m + 1)
                if not (first and b == 0 and j < 4):
                    act.wait_ge(hlo_done, m - 3)
                act.activation(h[:, j % 4, :], p1[j % 2][:], ACT.Gelu,
                               bias=b1c[:, j:j + 1]).then_inc(gelu_done, 1)
                act.wait_ge(gelu_done, m + 1)
                if not (first and b == 0):
                    act.wait_ge(second_done, m - KH + 1)
                act.copy(hhi[:, j, :], h[:, j % 4, :]).then_inc(hhi_done, 1)

            def x_hi(l, b):
                n = NB * l + b
                for k in range(KD):
                    act.wait_ge(xf_done, KD * n + k + 1)
                    act.copy(xhi[:, k, b * BLK:(b + 1) * BLK], xf[:, k, :]).then_inc(xhi_done, 1)

            def w1_hi(l, j):
                hj = slice(j * P, (j + 1) * P)
                act.copy(w1hi[:, :, hj], w1tiles[:, :, hj]).then_inc(w1_hi_done, 1)

            def w2_hi(l, j):
                act.copy(w2hi[:, j, :], w2raw[:, j, :]).then_inc(w2_hi_done, 1)

            def biases(l):
                act.copy(b1c[:], w1raw[:, KD * HID:]).then_inc(b1_done, 1)
                act.wait_ge(b1_done, 1 * l + 1)

            act.wait_ge(w1_in, 16)
            biases(0)
            for j in range(KH):
                w1_hi(0, j)
            act.wait_ge(w2_in, 16)
            for j in range(KH):
                hidden_tile(0, 0, j, True)
                w2_hi(0, j)

            def body(l, first, last):
                if first:
                    act.wait_ge(rms_done, 1)
                for b in range(NB):
                    if b == 2 and not last:
                        act.wait_ge(w1_in, 16 * (l + 2))
                    if b == 3 and not last:
                        act.wait_ge(w2_in, 16 * (l + 2))
                        act.wait_ge(gelu_done, KH * NB * (l + 1))
                        biases(l + 1)
                    for j in range(KH):
                        if b < NB - 1:
                            hidden_tile(l, b + 1, j, first)
                        elif not last:
                            hidden_tile(l + 1, 0, j, False)
                        if b == 2 and not last:
                            w1_hi(l + 1, j)
                        if b == 3 and not last:
                            act.wait_ge(second_done, KH * (NB * l + b) + j + 1)
                            w2_hi(l + 1, j)
                        if first and j >= KH - TPB:
                            t = b * TPB + j - (KH - TPB)
                            act.activation(acc[:, t, :], acc[:, t, :], ACT.Identity,
                                           scale=rms[:, t:t + 1]).then_inc(rms_scaled, 1)
                        if j == 3:
                            if b == 0:
                                if not first:
                                    x_hi(l - 1, NB - 1)
                            elif not last:
                                x_hi(l, b - 1)

            layers(act, body)

        @block.vector
        def _(dve):
            def h_lo(l, b, j):
                dve.wait_ge(hhi_done, KH * (NB * l + b) + j + 1)
                dve.tensor_tensor(hlo[:, j, :], h[:, j % 4, :], hhi[:, j, :].bitcast(F32),
                                  ALU.subtract).then_inc(hlo_done, 1)

            def sums(l, b, first):
                n = NB * l + b
                dve.wait_ge(res_done, n + 1)
                if not (first and b < 2):
                    dve.wait_ge(tr_done, KD * (n - 1))
                    dve.wait_ge(res_done, NB + n - 1)
                dve.wait_ge(second_done, KH * (n + 1))
                for t in range(TPB):
                    dve.tensor_tensor(u[:, b % 2, t, :], p2[t][:, 0:DM], res[:, b * TPB + t, :],
                                      ALU.add).then_inc(u_done, 1)

            def variances(l, b):
                n = NB * l + b
                for t in range(TPB):
                    dve.wait_ge(u_done, TPB * n + t + 1)
                    dve.bn_stats(stats[:, t, :], u[:, b % 2, t, :]).then_inc(stats_done, 1)
                dve.wait_ge(stats_done, TPB * (n + 1))
                dve.sem_inc(stats_seen, 1)
                for t in range(TPB):
                    dve.bn_aggr(mv[:, t, :], stats[:, t, :]).then_inc(mv_done, 1)
                dve.wait_ge(mv_done, TPB * (n + 1))
                dve.tensor_scalar(vare[:], mv[:, :, 1], EPS, None, ALU.add).then_inc(vare_done, 1)

            def normalised(l, b):
                dve.wait_ge(rstd_done, NB * l + b + 1)
                for t in range(TPB):
                    dve.tensor_scalar(u[:, b % 2, t, :], u[:, b % 2, t, :], mv[:, t, 0:1],
                                      rstd[:, t:t + 1], ALU.subtract, ALU.mult).then_inc(norm_done, 1)

            def x_full(l, b, first):
                n = NB * l + b
                for k in range(KD):
                    dve.wait_ge(tr_done, KD * n + k + 1)
                    if not (first and b == 0):
                        dve.wait_ge(xlo_done, KD * n - KD + k + 1)
                        dve.wait_ge(xhi_done, KD * n - KD + k + 1)
                    dve.tensor_scalar(xf[:, k, :], p3[k][:], gbc[:, bass.ds(2 * KD * l + k, 1)],
                                      gbc[:, bass.ds(2 * KD * l + KD + k, 1)], ALU.mult,
                                      ALU.add).then_inc(xf_done, 1)

            def x_lo(l, b):
                n = NB * l + b
                for k in range(KD):
                    dve.wait_ge(xhi_done, KD * n + k + 1)
                    dve.tensor_tensor(xlo[:, k, b * BLK:(b + 1) * BLK], xf[:, k, :],
                                      xhi[:, k, b * BLK:(b + 1) * BLK].bitcast(F32),
                                      ALU.subtract).then_inc(xlo_done, 1)

            def last_sums(b):
                n = NB * (NL - 1) + b
                dve.wait_ge(all_added, b + 1)
                dve.wait_ge(second_done, KH * (n + 1))
                for t in range(TPB):
                    a = acc[:, b * TPB + t, :]
                    dve.tensor_tensor(a, p2[t][:, 0:DM], a, ALU.add).then_inc(u_done, 1)

            dve.wait_ge(const_in, 16)
            for j in range(KH - 1):
                h_lo(0, 0, j)

            def body(l, first, last):
                for b in range(NB):
                    before = None
                    if b == 0 and not first:
                        before = (l - 1, NB - 1)
                    elif b > 0 and not last:
                        before = (l, b - 1)
                    if before:
                        sums(*before, first)
                    elif last:
                        last_sums(b - 1)
                    h_lo(l, b, KH - 1)
                    if before:
                        variances(*before)
                    for j in range(KH - 1):
                        if b < NB - 1:
                            h_lo(l, b + 1, j)
                        elif not last:
                            h_lo(l + 1, 0, j)
                        if before and j == 0:
                            normalised(*before)
                        if before and j == 3:
                            x_full(*before, first)
                        if before and j == 4:
                            x_lo(*before)

            layers(dve, body)
            last_sums(NB - 1)


def kernel(**inputs):
    import numpy as np
    import concourse.bacc as bacc
    from concourse.bass_utils import run_bass_kernel_spmd

    a = {k: np.asarray(v) for k, v in inputs.items()}

    def cols(x, n):
        return np.moveaxis(x.reshape(n, P, *x.shape[1:]), 0, 1)

    w_in = cols(a["L0_attn_W_in"], KD)
    z, x, bc, dt = np.split(w_in, [DI, 2 * DI, 2 * DI + 2 * P], axis=2)
    xz = np.concatenate([x.reshape(P, KD, NCT, P), z.reshape(P, KD, NCT, P)], axis=1)
    conv = np.concatenate([a["L0_attn_conv_w"], a["L0_attn_conv_b"][:, None]], axis=1)
    conv = conv.reshape(NCT + 2, P, TAPS + 1)
    w1 = a["L0_ffn_W1"].transpose(0, 2, 1).reshape(NL, KD, P, HID).transpose(0, 2, 1, 3)
    b1 = a["L0_ffn_B1"].reshape(NL, KH, P).transpose(0, 2, 1)
    rows = np.arange(P)
    upper = (rows[None, :] >= rows[:, None]).astype(np.float32)
    ln_cols = np.stack([a["L0_ffn_LN_G"].reshape(NL - 1, KD, P), a["L0_ffn_LN_B"].reshape(NL - 1, KD, P)],
                       axis=1)
    arrays = dict(
        hidden=a["L0_attn_hidden_states"].reshape(TOK, DM),
        w_bcdt=np.concatenate([dt, dt, bc], axis=2),
        w_xz=xz.transpose(2, 0, 1, 3).reshape(NCT, P, 2 * KD * P),
        conv_par=conv[:NCT],
        d_par=np.repeat(a["L0_attn_D"], HD).reshape(NCT, P, 1),
        conv_bc=np.moveaxis(conv[NCT:], 0, 1),
        dt_par=np.stack([np.tile(a["L0_attn_dt_bias"], 2), np.tile(a["L0_attn_A"], 2)], axis=1),
        w_out=np.concatenate([a["L0_attn_W_out"], a["L0_attn_norm_w"][:, None]], axis=1)
        .reshape(NCT // 2, 2, P, DM + 1).transpose(0, 2, 1, 3),
        w1=np.concatenate([w1.reshape(NL, P, KD * HID), b1], axis=2),
        w2=a["L0_ffn_W2"].transpose(0, 2, 1).reshape(NL, KH, P, DM).transpose(0, 2, 1, 3),
        b2=a["L0_ffn_B2"],
        ln_g=a["L0_ffn_LN_G"],
        ln_b=a["L0_ffn_LN_B"],
        ln_cols=np.moveaxis(ln_cols, 3, 0).reshape(P, -1),
        ident_in=np.eye(P, dtype=np.float32),
        mask_in=np.concatenate([upper, np.ones((P, P), np.float32), upper], axis=1),
    )
    arrays = {k: np.ascontiguousarray(v) for k, v in arrays.items()}
    nc = bacc.Bacc("TRN2", target_bir_lowering=False, num_devices=1)
    args = {k: nc.dram_tensor(k, v.shape, mybir.dt.from_np(v.dtype), kind="ExternalInput").ap()
            for k, v in arrays.items()}
    shape = a["L0_attn_hidden_states"].shape
    result = nc.dram_tensor("result", (TOK, DM), F32, kind="ExternalOutput").ap()
    build(nc, out=result, **args)
    r = run_bass_kernel_spmd(nc, [arrays], core_ids=[0])
    return r.results[0]["result"].reshape(shape)
```
